# Optimizing a Trainium2 kernel written in Bass

```python
import numpy as np
import jax
import jax.numpy as jnp

def _softmax(x, axis=-1):
    return jax.nn.softmax(x, axis=axis)

def _gelu(x):
    return jax.nn.gelu(x, approximate=True)

def _silu(x):
    return jax.nn.silu(x)

def _sigmoid(x):
    return jax.nn.sigmoid(x)

def _layernorm(x, axis=-1, eps=1e-05):
    m = jnp.mean(x, axis=axis, keepdims=True)
    v = jnp.var(x, axis=axis, keepdims=True)
    return (x - m) / jnp.sqrt(v + eps)

def _scatter_add(tgt, idx, src, axis=0):
    return tgt.at[idx].add(src)

def _segment_sum(src, seg, n):
    return jax.ops.segment_sum(src, seg, n)
kernel_name = 'mk_hybrid_d1_jaxref_r4_9d0803'

def setup_inputs(seed: int=0):
    np.random.seed(seed)
    _w = jnp.asarray

    def _L0_attn_a_setup():
        import jax, jax.numpy as jnp
        import numpy as np
        HIDDEN = 256
        NUM_HEADS = 16
        NUM_KV = 4
        HEAD_DIM = HIDDEN // NUM_HEADS
        GROUPS = NUM_HEADS // NUM_KV
        SCALE = HEAD_DIM ** 0.5
        key = jax.random.key(seed)
        ks = jax.random.split(key, 9)
        s = 0.02
        B, N = (4, 512)
        return {'x': jax.random.normal(ks[0], (B, N, HIDDEN), dtype=jnp.float32), 'Wq': jax.random.normal(ks[1], (HIDDEN, NUM_HEADS * HEAD_DIM), dtype=jnp.float32) * s, 'bq': jnp.zeros((NUM_HEADS * HEAD_DIM,), dtype=jnp.float32), 'Wk': jax.random.normal(ks[2], (HIDDEN, NUM_KV * HEAD_DIM), dtype=jnp.float32) * s, 'bk': jnp.zeros((NUM_KV * HEAD_DIM,), dtype=jnp.float32), 'Wv': jax.random.normal(ks[3], (HIDDEN, NUM_KV * HEAD_DIM), dtype=jnp.float32) * s, 'bv': jnp.zeros((NUM_KV * HEAD_DIM,), dtype=jnp.float32), 'Wo': jax.random.normal(ks[4], (NUM_HEADS * HEAD_DIM, HIDDEN), dtype=jnp.float32) * s, 'bo': jnp.zeros((HIDDEN,), dtype=jnp.float32)}
    _L0_attn_a_in = _L0_attn_a_setup()

    def _L0_attn_b_setup():
        import jax, jax.numpy as jnp
        import numpy as np
        B, N, EMBED, HEADS = (1, 512, 256, 16)
        HD = EMBED // HEADS
        BASE = 10000.0
        EPS = 1e-05

        def _rope(t):
            d = t.shape[-1]
            n = t.shape[-2]
            inv_freq = 1.0 / BASE ** (jnp.arange(0, d, 2, dtype=jnp.float32) / d)
            pos = jnp.arange(n, dtype=jnp.float32)
            ang = pos[:, None] * inv_freq[None, :]
            cos = jnp.concatenate([jnp.cos(ang), jnp.cos(ang)], axis=-1)
            sin = jnp.concatenate([jnp.sin(ang), jnp.sin(ang)], axis=-1)
            t1, t2 = (t[..., :d // 2], t[..., d // 2:])
            rot = jnp.concatenate([-t2, t1], axis=-1)
            return t * cos + rot * sin
        key = jax.random.key(seed)
        ks = jax.random.split(key, 7)
        s = EMBED ** (-0.5)
        return {'x': jax.random.normal(ks[0], (B, N, EMBED), dtype=jnp.float32), 'Wq': jax.random.normal(ks[1], (EMBED, EMBED), dtype=jnp.float32) * s, 'Wk': jax.random.normal(ks[2], (EMBED, EMBED), dtype=jnp.float32) * s, 'Wv': jax.random.normal(ks[3], (EMBED, EMBED), dtype=jnp.float32) * s, 'Wo': jax.random.normal(ks[4], (EMBED, EMBED), dtype=jnp.float32) * s, 'Wg1': jax.random.normal(ks[5], (EMBED, HD), dtype=jnp.float32) * s, 'Wg2': jax.random.normal(ks[6], (HD, EMBED), dtype=jnp.float32) * HD ** (-0.5), 'ln_w': jnp.ones((EMBED,), dtype=jnp.float32), 'ln_b': jnp.zeros((EMBED,), dtype=jnp.float32)}
    _L0_attn_b_in = _L0_attn_b_setup()

    def _L0_ffn_setup():
        import jax, jax.numpy as jnp
        import numpy as np
        B, S, DIM = (4, 1024, 256)
        BASE_COUPLING = 0.1
        NUM_CYCLES = 3

        def _gelu(x):
            return jax.nn.gelu(x, approximate=False)

        def _coupling_net(h, w1, b1, w2, b2, w3, b3, w4, b4):
            h = _gelu(h @ w1 + b1)
            h = _gelu(h @ w2 + b2)
            h = _gelu(h @ w3 + b3)
            return jax.nn.sigmoid(h @ w4 + b4)

        def _global_net(h, w1, b1, w2, b2, w3, b3):
            h = _gelu(h @ w1 + b1)
            h = _gelu(h @ w2 + b2)
            return jax.nn.sigmoid(h @ w3 + b3)

        def _twist(x):
            o_r, o_i, p_r, p_i = jnp.split(x, 4, axis=-1)
            return jnp.concatenate([p_r, -p_i, -o_r, o_i], axis=-1)
        key = jax.random.key(seed)
        ks = jax.random.split(key, 9)
        d = DIM

        def w(k, fan_in, fan_out):
            return jax.random.normal(k, (fan_in, fan_out), dtype=jnp.float32) / np.sqrt(fan_in).astype(np.float32)
        inp = {'x': jax.random.normal(ks[0], (B, S, d), dtype=jnp.float32)}
        cn_dims = [(d, d), (d, d // 2), (d // 2, d // 4), (d // 4, 1)]
        for i, (a, b) in enumerate(cn_dims):
            inp[f'cn_w{i + 1}'] = w(ks[1 + i], a, b)
            inp[f'cn_b{i + 1}'] = jnp.zeros((b,), dtype=jnp.float32)
        gc_dims = [(d, d // 2), (d // 2, d // 4), (d // 4, 1)]
        for i, (a, b) in enumerate(gc_dims):
            inp[f'gc_w{i + 1}'] = w(ks[5 + i], a, b)
            inp[f'gc_b{i + 1}'] = jnp.zeros((b,), dtype=jnp.float32)
        inp['adaptive_range'] = jnp.full((1,), 0.2, dtype=jnp.float32)
        return inp
    _L0_ffn_in = _L0_ffn_setup()
    _d = {'L0_attn_a_x': _L0_attn_a_in['x'], 'L0_attn_a_Wq': _L0_attn_a_in['Wq'], 'L0_attn_a_bq': _L0_attn_a_in['bq'], 'L0_attn_a_Wk': _L0_attn_a_in['Wk'], 'L0_attn_a_bk': _L0_attn_a_in['bk'], 'L0_attn_a_Wv': _L0_attn_a_in['Wv'], 'L0_attn_a_bv': _L0_attn_a_in['bv'], 'L0_attn_a_Wo': _L0_attn_a_in['Wo'], 'L0_attn_a_bo': _L0_attn_a_in['bo'], 'L0_attn_b_Wq': _L0_attn_b_in['Wq'], 'L0_attn_b_Wk': _L0_attn_b_in['Wk'], 'L0_attn_b_Wv': _L0_attn_b_in['Wv'], 'L0_attn_b_Wo': _L0_attn_b_in['Wo'], 'L0_attn_b_Wg1': _L0_attn_b_in['Wg1'], 'L0_attn_b_Wg2': _L0_attn_b_in['Wg2'], 'L0_attn_b_ln_w': _L0_attn_b_in['ln_w'], 'L0_attn_b_ln_b': _L0_attn_b_in['ln_b'], 'L0_ffn_cn_w1': _L0_ffn_in['cn_w1'], 'L0_ffn_cn_b1': _L0_ffn_in['cn_b1'], 'L0_ffn_cn_w2': _L0_ffn_in['cn_w2'], 'L0_ffn_cn_b2': _L0_ffn_in['cn_b2'], 'L0_ffn_cn_w3': _L0_ffn_in['cn_w3'], 'L0_ffn_cn_b3': _L0_ffn_in['cn_b3'], 'L0_ffn_cn_w4': _L0_ffn_in['cn_w4'], 'L0_ffn_cn_b4': _L0_ffn_in['cn_b4'], 'L0_ffn_gc_w1': _L0_ffn_in['gc_w1'], 'L0_ffn_gc_b1': _L0_ffn_in['gc_b1'], 'L0_ffn_gc_w2': _L0_ffn_in['gc_w2'], 'L0_ffn_gc_b2': _L0_ffn_in['gc_b2'], 'L0_ffn_gc_w3': _L0_ffn_in['gc_w3'], 'L0_ffn_gc_b3': _L0_ffn_in['gc_b3'], 'L0_ffn_adaptive_range': _L0_ffn_in['adaptive_range']}
    _x0 = _d['L0_attn_a_x']
    _d['L0_attn_a_x'] = jax.random.normal(jax.random.fold_in(jax.random.key(seed), 1), (2, 2048, 256), dtype=_x0.dtype)
    del _x0
    return _d

def reference(L0_attn_a_x, L0_attn_a_Wq, L0_attn_a_bq, L0_attn_a_Wk, L0_attn_a_bk, L0_attn_a_Wv, L0_attn_a_bv, L0_attn_a_Wo, L0_attn_a_bo, L0_attn_b_Wq, L0_attn_b_Wk, L0_attn_b_Wv, L0_attn_b_Wo, L0_attn_b_Wg1, L0_attn_b_Wg2, L0_attn_b_ln_w, L0_attn_b_ln_b, L0_ffn_cn_w1, L0_ffn_cn_b1, L0_ffn_cn_w2, L0_ffn_cn_b2, L0_ffn_cn_w3, L0_ffn_cn_b3, L0_ffn_cn_w4, L0_ffn_cn_b4, L0_ffn_gc_w1, L0_ffn_gc_b1, L0_ffn_gc_w2, L0_ffn_gc_b2, L0_ffn_gc_w3, L0_ffn_gc_b3, L0_ffn_adaptive_range):

    def _L0_attn_a_ref(x, Wq, bq, Wk, bk, Wv, bv, Wo, bo):
        import jax, jax.numpy as jnp
        import numpy as np
        HIDDEN = 256
        NUM_HEADS = 16
        NUM_KV = 4
        HEAD_DIM = HIDDEN // NUM_HEADS
        GROUPS = NUM_HEADS // NUM_KV
        SCALE = HEAD_DIM ** 0.5
        B, N, _ = x.shape
        q = x @ Wq + bq
        k = x @ Wk + bk
        v = x @ Wv + bv
        q = q.reshape(B, N, NUM_HEADS, HEAD_DIM).transpose(0, 2, 1, 3)
        q = q.reshape(B, NUM_KV, GROUPS, N, HEAD_DIM).transpose(0, 2, 1, 3, 4)
        k = k.reshape(B, N, NUM_KV, HEAD_DIM).transpose(0, 2, 1, 3)
        v = v.reshape(B, N, NUM_KV, HEAD_DIM).transpose(0, 2, 1, 3)
        scores = jnp.einsum('bghnd,bhsd->bghns', q, k)
        attn = jax.nn.softmax(scores / SCALE, axis=-1)
        out = jnp.einsum('bghns,bhsd->bghnd', attn, v)
        out = out.transpose(0, 3, 1, 2, 4).reshape(B, N, NUM_HEADS * HEAD_DIM)
        return out @ Wo + bo

    def _L0_attn_b_ref(x, Wq, Wk, Wv, Wo, Wg1, Wg2, ln_w, ln_b):
        import jax, jax.numpy as jnp
        import numpy as np
        B, N, EMBED, HEADS = (1, 512, 256, 16)
        HD = EMBED // HEADS
        BASE = 10000.0
        EPS = 1e-05

        def _rope(t):
            d = t.shape[-1]
            n = t.shape[-2]
            inv_freq = 1.0 / BASE ** (jnp.arange(0, d, 2, dtype=jnp.float32) / d)
            pos = jnp.arange(n, dtype=jnp.float32)
            ang = pos[:, None] * inv_freq[None, :]
            cos = jnp.concatenate([jnp.cos(ang), jnp.cos(ang)], axis=-1)
            sin = jnp.concatenate([jnp.sin(ang), jnp.sin(ang)], axis=-1)
            t1, t2 = (t[..., :d // 2], t[..., d // 2:])
            rot = jnp.concatenate([-t2, t1], axis=-1)
            return t * cos + rot * sin
        b, n, _ = x.shape
        q = jax.nn.silu(x @ Wq)
        k = jax.nn.silu(x @ Wk)
        v = x @ Wv
        split = lambda t: t.reshape(b, n, HEADS, HD).transpose(0, 2, 1, 3)
        q, k, v = (split(q), split(k), split(v))
        q = _rope(q)
        k = _rope(k)
        energy = jnp.einsum('bhnd,bhmd->bhnm', q, k)
        mask = jnp.tril(jnp.ones((n, n), dtype=energy.dtype))
        energy = energy * mask
        out = jnp.einsum('bhnm,bhmd->bhnd', energy, v)
        out = out.transpose(0, 2, 1, 3).reshape(b, n, EMBED)
        gate = jax.nn.sigmoid(x @ Wg1 @ Wg2)
        out = out * gate
        mu = out.mean(axis=-1, keepdims=True)
        var = ((out - mu) ** 2).mean(axis=-1, keepdims=True)
        out = (out - mu) / jnp.sqrt(var + EPS) * ln_w + ln_b
        return out @ Wo

    def _L0_ffn_ref(x, cn_w1, cn_b1, cn_w2, cn_b2, cn_w3, cn_b3, cn_w4, cn_b4, gc_w1, gc_b1, gc_w2, gc_b2, gc_w3, gc_b3, adaptive_range):
        import jax, jax.numpy as jnp
        import numpy as np
        B, S, DIM = (4, 1024, 256)
        BASE_COUPLING = 0.1
        NUM_CYCLES = 3

        def _gelu(x):
            return jax.nn.gelu(x, approximate=False)

        def _coupling_net(h, w1, b1, w2, b2, w3, b3, w4, b4):
            h = _gelu(h @ w1 + b1)
            h = _gelu(h @ w2 + b2)
            h = _gelu(h @ w3 + b3)
            return jax.nn.sigmoid(h @ w4 + b4)

        def _global_net(h, w1, b1, w2, b2, w3, b3):
            h = _gelu(h @ w1 + b1)
            h = _gelu(h @ w2 + b2)
            return jax.nn.sigmoid(h @ w3 + b3)

        def _twist(x):
            o_r, o_i, p_r, p_i = jnp.split(x, 4, axis=-1)
            return jnp.concatenate([p_r, -p_i, -o_r, o_i], axis=-1)
        global_context = x.mean(axis=1, keepdims=True)
        gf = _global_net(global_context, gc_w1, gc_b1, gc_w2, gc_b2, gc_w3, gc_b3)
        out = x
        for _ in range(NUM_CYCLES):
            tf = _coupling_net(out, cn_w1, cn_b1, cn_w2, cn_b2, cn_w3, cn_b3, cn_w4, cn_b4)
            combined = 0.7 * gf + 0.3 * tf
            coupling = BASE_COUPLING + adaptive_range * (combined - 0.5) * 2.0
            out = out + coupling * _twist(out)
        return out
    x = L0_attn_a_x
    x = x + _L0_attn_a_ref(_layernorm(x, axis=-1), L0_attn_a_Wq, L0_attn_a_bq, L0_attn_a_Wk, L0_attn_a_bk, L0_attn_a_Wv, L0_attn_a_bv, L0_attn_a_Wo, L0_attn_a_bo)
    x = x + _L0_ffn_ref(_layernorm(x, axis=-1), L0_ffn_cn_w1, L0_ffn_cn_b1, L0_ffn_cn_w2, L0_ffn_cn_b2, L0_ffn_cn_w3, L0_ffn_cn_b3, L0_ffn_cn_w4, L0_ffn_cn_b4, L0_ffn_gc_w1, L0_ffn_gc_b1, L0_ffn_gc_w2, L0_ffn_gc_b2, L0_ffn_gc_w3, L0_ffn_gc_b3, L0_ffn_adaptive_range)
    x = x + _L0_attn_b_ref(_layernorm(x, axis=-1), L0_attn_b_Wq, L0_attn_b_Wk, L0_attn_b_Wv, L0_attn_b_Wo, L0_attn_b_Wg1, L0_attn_b_Wg2, L0_attn_b_ln_w, L0_attn_b_ln_b)
    x = x + _L0_ffn_ref(_layernorm(x, axis=-1), L0_ffn_cn_w1, L0_ffn_cn_b1, L0_ffn_cn_w2, L0_ffn_cn_b2, L0_ffn_cn_w3, L0_ffn_cn_b3, L0_ffn_cn_w4, L0_ffn_cn_b4, L0_ffn_gc_w1, L0_ffn_gc_b1, L0_ffn_gc_w2, L0_ffn_gc_b2, L0_ffn_gc_w3, L0_ffn_gc_b3, L0_ffn_adaptive_range)
    return x

_drawn_inputs = setup_inputs


def setup_inputs(seed=0):
    import zlib

    import numpy as np

    out = dict(_drawn_inputs(seed))
    spreads = {'L0_attn_a_bq': (0.0, 0.8),
     'L0_attn_a_bk': (0.0, 0.8),
     'L0_attn_a_bv': (0.0, 0.1),
     'L0_attn_a_bo': (0.0, 0.1),
     'L0_attn_b_ln_w': (1.0, 0.2),
     'L0_attn_b_ln_b': (0.0, 0.1),
     'L0_ffn_cn_b1': (0.0, 0.8),
     'L0_ffn_cn_b2': (0.0, 0.8),
     'L0_ffn_cn_b3': (0.0, 0.8),
     'L0_ffn_gc_b1': (0.0, 0.8),
     'L0_ffn_gc_b2': (0.0, 0.8)}
    factors = {'L0_attn_a_Wq': 8.0,
     'L0_attn_a_Wk': 8.0,
     'L0_attn_a_Wv': 8.0,
     'L0_ffn_cn_w1': 4.834,
     'L0_ffn_cn_w2': 5.05,
     'L0_ffn_cn_w3': 3.992,
     'L0_ffn_cn_w4': 4.475,
     'L0_ffn_gc_w1': 8.0,
     'L0_ffn_gc_w2': 8.0,
     'L0_ffn_gc_w3': 3.377}
    for name, (base, spread) in spreads.items():
        noise = np.random.default_rng([zlib.crc32(name.encode()), seed]).standard_normal(out[name].shape)
        drawn = base * np.exp(spread * noise) if base else spread * noise
        out[name] = jnp.asarray(drawn.astype(out[name].dtype))
    for name, factor in factors.items():
        out[name] = (out[name] * factor).astype(out[name].dtype)
    return out
```

```python
from contextlib import ExitStack

import numpy as np

import concourse.bass as bass
from concourse import mybir

F32 = mybir.dt.float32
BF16 = mybir.dt.bfloat16
ACT = mybir.ActivationFunctionType
ALU = mybir.AluOpType
AX_X = mybir.AxisListType.X

P = 128
BATCH, SEQ, DIM = 2, 2048, 256
TOKENS = BATCH * SEQ
KT = DIM // P
CH = 512
NCH = TOKENS // CH
HEADS, KV_HEADS, HD = 16, 4, 16
GROUP = HEADS // KV_HEADS
KVD = KV_HEADS * HD
EPS = 1e-5

CPG = SEQ // CH
NKV = BATCH * KV_HEADS
STEPS = NKV * CPG
KTILES = SEQ // P
UNITS = KTILES * GROUP
MAXU = GROUP * (CH // P) * 2
Q_STACK = ((0, 3), (0, 2), (0, 1))
K_STACK = ((0, 3), (1, 2), (2, 1))
ROWS = 6 * HD
ROWS_M = ROWS + 2
LOADED = 16 * (len(Q_STACK) + len(K_STACK))

CYCLES = 3
FN = CYCLES * NCH
AHEAD = 16
MAXMM = 2 * MAXU
TURN = 2
LAG = 3

TILES = TOKENS // P
TPB = SEQ // P
HPK = P // HD


def hybrid_block(nc, x, wq, bq, wk, bk, wv, bv, wo, bo, lq, lk, lv, lo, g1, g2, ln_w, ln_b,
                 c1, d1, c2, d2, c3, d3, c4, d4, e1, f1, e2, f2, e3, f3, ar,
                 ident_in, cos_in, sin_in, causal_in, head_in, diag_in, sign_in, out):
    with ExitStack() as ctx:
        def sb(name, shape, dt=F32):
            return ctx.enter_context(nc.sbuf_tensor(name, shape, dt))

        def sem(name):
            return ctx.enter_context(nc.semaphore(name))

        q_scr = nc.dram_tensor("q_scr", [STEPS, 3, HD, GROUP, CH], BF16, kind="Internal").ap()
        k_scr = nc.dram_tensor("k_scr", [NKV, 3, HD, SEQ], BF16, kind="Internal").ap()
        o_scr = nc.dram_tensor("o_scr", [STEPS, GROUP, 32, CH], F32, kind="Internal").ap()
        inv_scr = nc.dram_tensor("inv_scr", [STEPS * GROUP, CH], F32, kind="Internal").ap()

        ps = ctx.enter_context(nc.psum_tensor("ps", [P, 8, CH], F32))

        XT = sb("XT", [P, KT, TOKENS])
        YT = sb("YT", [P, KT, TOKENS])
        ident = sb("ident", [P, P])
        ones = sb("ones", [P, P])
        eps = sb("eps", [P, 1])

        wq_s = sb("wq_s", [P, KT, DIM])
        wkk_s = sb("wkk_s", [P, KT, 2 * KVD])
        wv_s = sb("wv_s", [P, KT, KVD])
        wo_s = sb("wo_s", [P, KT, DIM])
        bv_s = sb("bv_s", [P, KVD])
        c1_s = sb("c1_s", [P, KT, DIM])
        c2_s = sb("c2_s", [P, KT, P])
        c3_s = sb("c3_s", [P, 64])
        c4_s = sb("c4_s", [64, P])
        e1_s = sb("e1_s", [P, KT, P])
        e2_s = sb("e2_s", [P, 64])
        e3_s = sb("e3_s", [64, P])
        last_c = sb("last_c", [64, 2])
        lqk_s = sb("lqk_s", [P, KT, 2 * DIM])
        lv_s = sb("lv_s", [P, KT, DIM])
        lo_s = sb("lo_s", [P, KT, DIM])
        g1_s = sb("g1_s", [P, KT, HD])
        g2_s = sb("g2_s", [HD, DIM])
        cos_s = sb("cos_s", [P, TPB, HD // 2])
        sin_s = sb("sin_s", [P, TPB, HD // 2])
        causal = sb("causal", [P, P])
        head = sb("head", [P, HPK])
        diag = sb("diag", [P, HEADS, HD])
        bias = sb("bias", [P, 20])
        BQ, BK, BO, D1, D2, D3, D4, F1, F2, F3, AR, LW, LB, SG = 0, 2, 3, 5, 7, 8, 9, 10, 11, 12, 13, 14, 16, 18
        half_b = sb("half_b", [P, 2])
        coup = sb("coup", [P, 4])

        def col(v):
            return v.rearrange("(p a) -> p a", a=1)

        def tiled(w):
            return w.rearrange("(k p) n -> p k n", p=P)

        weights = [
            (ident[:], ident_in), (wq_s[:], tiled(wq)),
            (wkk_s[:, :, 0:KVD], tiled(wk)), (wkk_s[:, :, KVD:2 * KVD], tiled(wk)), (wv_s[:], tiled(wv)),
            (bias[0:KVD, BK:BK + 1], col(bk)), (bias[KVD:P, BK:BK + 1], col(bk)),
            (bias[:, D2:D2 + 1], col(d2)), (bias[0:64, D3:D3 + 1], col(d3)),
            (bias[:, D4:D4 + 1], col(d4).broadcast_to((P, 1))),
            (bias[:, F1:F1 + 1], col(f1)), (bias[0:64, F2:F2 + 1], col(f2)),
            (bias[:, F3:F3 + 1], col(f3).broadcast_to((P, 1))),
            (bias[:, AR:AR + 1], col(ar).broadcast_to((P, 1))),
            (bias[:, SG:SG + 1], sign_in),
            (bv_s[:], bv.rearrange("(a n) -> a n", a=1).broadcast_to((P, KVD))),
            (wo_s[:], tiled(wo)), (c1_s[:], tiled(c1)), (c2_s[:], tiled(c2)), (c3_s[:], c3),
            (last_c[:, 0:1], c4), (e1_s[:], tiled(e1)), (e2_s[:], e2),
            (last_c[:, 1:2], e3),
            (lqk_s[:, :, 0:DIM], tiled(lq)), (lqk_s[:, :, DIM:2 * DIM], tiled(lk)), (lv_s[:], tiled(lv)),
            (lo_s[:], tiled(lo)), (g1_s[:], tiled(g1)), (g2_s[:], g2),
            (cos_s[:], cos_in.rearrange("(t p) e -> p t e", p=P)),
            (sin_s[:], sin_in.rearrange("(t p) e -> p t e", p=P)),
            (causal[:], causal_in), (head[:], head_in),
            (diag[:], diag_in.rearrange("p (h e) -> p h e", h=HEADS)),
        ]
        for at_, v in ((BQ, bq), (BO, bo), (D1, d1), (LW, ln_w), (LB, ln_b)):
            for kt in range(KT):
                weights.append((bias[:, at_ + kt:at_ + kt + 1], col(v[kt * P:(kt + 1) * P])))

        x_row = sb("x_row", [P, 2, 4, DIM])
        sq = sb("sq", [P, 2, KT, CH])
        std = sb("std", [P, 2, CH])
        rec = sb("rec", [P, 2, CH])
        vals = sb("vals", [P, NKV, KTILES, 32])
        o_sb = sb("o_sb", [P, 2, CH])
        mx = sb("mx", [P, MAXU])
        mxq = sb("mxq", [P, MAXU // 2])
        negm = sb("negm", [HD, 2, P], BF16)
        gm = sb("gm", [P, KT, BATCH])
        gh1 = sb("gh1", [P, BATCH])
        gh2 = sb("gh2", [64, BATCH])
        gth = sb("gth", [P, BATCH])
        cb = sb("cb", [P, BATCH])
        WORK = 13 * 1024
        work = sb("work", [P, WORK])
        at = [0]

        def take(*shape, dt=F32):
            n = int(np.prod(shape))
            words = n if dt == F32 else n // 2
            ap = work[:, at[0]:at[0] + words]
            at[0] += words
            assert at[0] <= WORK, at[0]
            if dt != F32:
                ap = ap.bitcast(dt)
            names = "abcd"[:len(shape)]
            return ap.rearrange(f"p ({' '.join(names)}) -> p {' '.join(names)}", **dict(zip(names, shape)))

        qkf = take(2, 3, CH)
        res = take(2, 3, CH)
        part = take(2, 3, 3, CH, dt=BF16)
        at[0] = 0
        ka, kb = take(2, SEQ, dt=BF16), take(2, SEQ, dt=BF16)
        qa, qb = take(2, GROUP, CH, dt=BF16), take(2, GROUP, CH, dt=BF16)
        vst = take(2, KTILES, 32)
        prob = take(8, CH)
        at[0] = 0
        a_in, a_inv, den = take(2, KT, CH), take(2, KT, CH), take(CH)
        at[0] = 0
        h1, h2, h3 = take(2, KT, CH), take(2, CH), take(2, CH)
        th, cs, tw = take(2, CH), take(2, CH), take(2, KT, CH)
        at[0] = 0
        y_st8 = take(2, KT, P)
        qk_a, qk_r = take(2, 2 * DIM), take(2, 2 * DIM)
        rt = take(4, 2 * HEADS, HD // 2)
        v_r, gate = take(2, DIM), take(2, DIM)
        k_t, q_t = take(2, KT, P), take(2, KT, P)
        q_x = take(KT, HPK, P)
        e_m = take(HEADS, P)
        s_x = take(HEADS, 32)
        o_t = take(CH)
        o_r, o_n = take(2, DIM), take(2, DIM)
        on_t = take(2, KT, P)
        hg_tile = sb("hg_tile", [HD, 2, P])
        h_g = vals[0:HD].rearrange("p a b c -> p (a b c)")
        stats = sb("stats", [P, 6])
        mv = sb("mv", [P, 2, 2])
        var_e = sb("var_e", [P, 2])
        rstd = sb("rstd", [P, 2])
        mhalf = sb("mhalf", [P, 1])

        names = """w_ld consts c_dve x_tr x_eva x_evd ln_mean ln_cent ln_sq ln_var ln_std ln_rec ln_out
            p_mm p_act p_res p_mid p_low p_val v_ones kb_ones a_mm a_max a_fin a_tr
            nm_hi nm_lo m_ld qk_mm exp_ok pv_mm o_ev v_st den_ld den_inv inv_st o_norm o_mm
            o_res f_sum f_g f_ga f_cb f_h1 f_a1 f_h2 f_a2 f_h3 f_a3 f_z f_th f_cs f_tw f_up f_out
            l_hm l_hg l_ys l_qk l_vg l_silu l_v l_gate l_rt l_rope l_t l_kt l_qt l_qx l_e l_em
            l_o l_s l_sx l_oe l_ot l_r l_gt l_bn l_mv l_ve l_rs l_n l_y l_ye l_w l_x
            y_tr y_eva y_evd """.split()
        S = {n: sem(n) for n in names}
        (w_ld, consts, c_dve, x_tr, x_eva, x_evd, ln_mean, ln_cent, ln_sq, ln_var, ln_std, ln_rec, ln_out,
         p_mm, p_act, p_res, p_mid, p_low, p_val, v_ones, kb_ones, a_mm, a_max, a_fin, a_tr,
         nm_hi, nm_lo, m_ld, qk_mm, exp_ok, pv_mm, o_ev, v_st, den_ld, den_inv, inv_st, o_norm, o_mm,
         o_res, f_sum, f_g, f_ga, f_cb, f_h1, f_a1, f_h2, f_a2, f_h3, f_a3, f_z, f_th, f_cs, f_tw, f_up, f_out,
         l_hm, l_hg, l_ys, l_qk, l_vg, l_silu, l_v, l_gate, l_rt, l_rope, l_t, l_kt, l_qt, l_qx, l_e, l_em,
         l_o, l_s, l_sx, l_oe, l_ot, l_r, l_gt, l_bn, l_mv, l_ve, l_rs, l_n, l_y, l_ye, l_w, l_x,
         y_tr, y_eva, y_evd, ) = [S[n] for n in names]

        x_ld, p_st, qa_ld, qb_ld, o_st, o_ld, y_st = (
            [sem(f"{n}{p}") for p in range(2)] for n in ("x_ld", "p_st", "qa_ld", "qb_ld", "o_st", "o_ld", "y_st"))

        def ch(c):
            return slice(c * CH, (c + 1) * CH)

        def wait(eng, s, value):
            if not isinstance(value, int) or value > 0:
                eng.wait_ge(s, value)

        block = ctx.enter_context(nc.Block())

        @block.sync
        def _(sp):
            xr = x.rearrange("b (c t p) f -> (b c) p t f", t=4, p=P)
            yr = out.rearrange("b (c t p) f -> (b c) p t f", t=4, p=P)
            for c in range(NCH):
                wait(sp, x_tr, c - 1)
                sp.dma_start(x_row[:, c % 2], xr[c]).then_inc(x_ld[c % 2], 16)
                if c == 1:
                    for dst, src in weights:
                        sp.dma_start(dst, src).then_inc(w_ld, 16)

            for c in range(NCH):
                b, c4 = c // CPG, c % CPG
                for pt, done in ((0, p_act), (1, p_mid), (2, p_low)):
                    sp.wait_ge(done, c + 1)
                    for g in range(KV_HEADS):
                        s = (b * KV_HEADS + g) * CPG + c4
                        row = g % 2 * 64
                        sp.dma_start(q_scr[s, pt].rearrange("d j n -> j d n"),
                                     part[row:row + 64, c % 2, pt, g // 2, :]).then_inc(p_st[c % 2], 16)
                    sp.dma_start(k_scr[b * KV_HEADS:(b + 1) * KV_HEADS, pt, :, ch(c4)],
                                 part[0:64, c % 2, pt, 2, :]).then_inc(p_st[c % 2], 16)
            for p in range(2):
                sp.wait_ge(p_st[p], 16 * 15 * NCH // 2)

            def load(q_dst, k_dst, p, s, done):
                done = done[p]
                row = 0
                for first, n in Q_STACK:
                    sp.dma_start(q_dst[row:row + n * HD, p],
                                 q_scr[s, 0:n].rearrange("r d j n -> (r d) j n")).then_inc(done, 16)
                    row += n * HD
                row = 0
                for first, n in K_STACK:
                    sp.dma_start(k_dst[row:row + n * HD, p],
                                 k_scr[s // CPG, first:first + 1].broadcast_to((n, HD, SEQ))).then_inc(done, 16)
                    row += n * HD

            def leave(s, p, more):
                if more:
                    sp.wait_ge(nm_lo, s + 2)
                    for r in range(2):
                        sp.dma_start(qb[ROWS + r:ROWS + r + 1, 1 - p].rearrange("p j n -> p (j n)"),
                                     negm[:, r, :]).then_inc(m_ld, 16)
                sp.wait_ge(o_ev, s + 1)
                sp.dma_start(o_scr[s].rearrange("j r n -> (j r) n"), o_sb[:, p, :]).then_inc(o_st[p], 16)

            def refill(s, p):
                load(qb, kb, p, s + 2, qb_ld)

            def refill_max(s, p):
                sp.wait_ge(a_tr, s + 1)
                load(qa, ka, p, s + 2, qa_ld)

            for s in (0, 1):
                load(qa, ka, s, s, qa_ld)
            sp.wait_ge(kb_ones, 2)
            for s in (0, 1):
                load(qb, kb, s, s, qb_ld)
            sp.wait_ge(nm_lo, 1)
            for r in range(2):
                sp.dma_start(qb[ROWS + r:ROWS + r + 1, 0].rearrange("p j n -> p (j n)"), negm[:, r, :]).then_inc(m_ld, 16)
            refill_max(0, 0)
            with sp.Fori(0, STEPS // 2 - 2) as i:
                for p in range(2):
                    leave(2 * i + p, p, True)
                    refill(2 * i + p, p)
                    refill_max(2 * i + p + 1, 1 - p)
            leave(STEPS - 4, 0, True)
            refill(STEPS - 4, 0)
            refill_max(STEPS - 3, 1)
            leave(STEPS - 3, 1, True)
            refill(STEPS - 3, 1)
            leave(STEPS - 2, 0, True)
            leave(STEPS - 1, 1, False)
            for p in range(2):
                sp.wait_ge(o_st[p], 16 * STEPS // 2)

            sp.dma_start(den, o_scr[:, :, HD, :].rearrange("s j n -> (s j) n")).then_inc(den_ld, 16)
            sp.wait_ge(den_inv, 1)
            sp.dma_start(inv_scr, den).then_inc(inv_st, 16)
            sp.wait_ge(inv_st, 16)
            for c in range(NCH):
                b, c4 = c // CPG, c % CPG
                wait(sp, o_mm, c - 1)
                for g in range(KV_HEADS):
                    s = (b * KV_HEADS + g) * CPG + c4
                    row = g % 2 * 64
                    sp.dma_start(a_in[row:row + 64, c % 2, g // 2, :], o_scr[s, :, 0:HD, :]).then_inc(o_ld[c % 2], 16)
                    sp.dma_start(a_inv[row:row + 64, c % 2, g // 2, :],
                                 inv_scr[s * GROUP:(s + 1) * GROUP, :].rearrange("j (a n) -> j a n", a=1)
                                 .broadcast_to((GROUP, HD, CH))).then_inc(o_ld[c % 2], 16)

            for c in range(NCH):
                sp.wait_ge(y_eva, c + 1)
                sp.wait_ge(y_evd, c + 1)
                sp.dma_start(yr[c], x_row[:, c % 2]).then_inc(y_st[c % 2], 16)
            for p in range(2):
                sp.wait_ge(y_st[p], 16 * NCH // 2)

        @block.tensor
        def _(pe):
            mm = pe.matmul

            def layer_norm(k, ready):
                for c in range(NCH + 1):
                    if c < NCH:
                        ready(c)
                        wait(pe, ln_cent, k * NCH + c - 1)
                        for kt in range(KT):
                            m = mm(ps[:, 4 + c % 2, :], ones[:], XT[:, kt, ch(c)], start=kt == 0, stop=kt == KT - 1)
                        m.then_inc(ln_mean, 1)
                    if c >= 1:
                        v = c - 1
                        pe.wait_ge(ln_sq, k * NCH + v + 1)
                        wait(pe, ln_std, k * NCH + v - 1)
                        for kt in range(KT):
                            m = mm(ps[:, 6 + v % 2, :], ones[:], sq[:, v % 2, kt, :], start=kt == 0, stop=kt == KT - 1)
                        m.then_inc(ln_var, 1)

            pe.wait_ge(w_ld, 16 * len(weights))
            for c in range(NCH):
                pe.wait_ge(x_ld[c % 2], 16 * (c // 2 + 1))
                wait(pe, x_eva, c - 1)
                wait(pe, x_evd, c - 1)
                for kt in range(KT):
                    for t in range(4):
                        m = pe.transpose(ps[:, 2 * (c % 2) + kt, t * P:(t + 1) * P],
                                         x_row[:, c % 2, t, kt * P:(kt + 1) * P], ident[:])
                m.then_inc(x_tr, 1)
            pe.wait_ge(consts, 5)

            def x_ready(c):
                pe.wait_ge(x_eva, c + 1)
                pe.wait_ge(x_evd, c + 1)
            layer_norm(0, x_ready)

            pe.wait_ge(ln_std, NCH)
            pe.wait_ge(ln_cent, NCH)
            for c in range(NCH):
                o = 4 * (c % 2)
                pe.wait_ge(ln_out, c + 1)
                wait(pe, p_act, c - 1)
                wait(pe, p_val, c - 1)
                for n in range(3):
                    for kt in range(KT):
                        w = wq_s[:, kt, n * P:(n + 1) * P] if n < KT else wkk_s[:, kt, :]
                        mm(ps[:, o + n, :], w, YT[:, kt, ch(c)], start=kt == 0, stop=kt == KT - 1)
                for t in range(4):
                    for kt in range(KT):
                        tok = c * CH + t * P
                        m = mm(ps[:, o + 3, t * KVD:(t + 1) * KVD], YT[:, kt, tok:tok + P], wv_s[:, kt, :],
                               start=kt == 0, stop=kt == KT - 1)
                m.then_inc(p_mm, 1)

            pe.wait_ge(p_act, NCH)
            pe.wait_ge(p_val, NCH)

            def max_mm(i, p, n):
                s, u, half = 2 * i + p, n // 2, n % 2
                j, qt, hk = u // 8, u // 2 % 4, u % 2
                if n == 0:
                    pe.wait_ge(qa_ld[p], LOADED * (i + 1))
                if n == 2:
                    wait(pe, nm_lo, s)
                if half == 0:
                    wait(pe, a_max, MAXU * s + u - 1)
                m = mm(ps[:, 2 * (u % 2) + half, :], qa[0:ROWS, p, j, qt * P:(qt + 1) * P],
                       ka[0:ROWS, p, (2 * hk + half) * CH:(2 * hk + half + 1) * CH], start=True, stop=True)
                if half == 1:
                    m.then_inc(a_mm, 1)

            def max_transpose(s):
                pe.wait_ge(a_fin, s + 1)
                pe.transpose(ps[0:MAXU // 2, 2, 0:P], mxq[:], ident[:]).then_inc(a_tr, 1)

            def step(i, p, ahead):
                s = 2 * i + p

                def sums(t):
                    pe.wait_ge(exp_ok, UNITS * s + GROUP * (t + 1))
                    if t == 0:
                        pe.wait_ge(v_st, s + 1)
                        wait(pe, o_ev, s)
                    for j in range(GROUP):
                        m = mm(ps[32 * j:32 * j + 32, 7, :], vst[:, p, t, :], prob[:, (GROUP * t + j) % 8, :],
                               start=t == 0, stop=t == KTILES - 1)
                    m.then_inc(pv_mm, 1)

                def maxima(k):
                    n = k + AHEAD
                    if n < MAXMM and ahead >= 1:
                        max_mm(i + p, 1 - p, n)
                    if n >= MAXMM and ahead >= 2:
                        max_mm(i + 1, p, n - MAXMM)

                pe.wait_ge(qb_ld[p], LOADED * (i + 1))
                pe.wait_ge(m_ld, 32 * (s + 1))
                for t in range(KTILES):
                    for j in range(GROUP):
                        u = GROUP * t + j
                        wait(pe, exp_ok, UNITS * s + u - 2)
                        mm(ps[:, 4 + u % 3, :], kb[0:ROWS_M, p, t * P:(t + 1) * P], qb[0:ROWS_M, p, j, :],
                           start=True, stop=True).then_inc(qk_mm, 1)
                        if u == MAXMM - AHEAD + TURN and ahead >= 1:
                            max_transpose(s + 1)
                        maxima(u)
                    if t >= 1:
                        sums(t - 1)
                sums(KTILES - 1)

            for n in range(MAXMM):
                max_mm(0, 0, n)
            max_transpose(0)
            for n in range(AHEAD):
                max_mm(0, 1, n)
            pe.wait_ge(kb_ones, 2)
            step(0, 0, 2)
            step(0, 1, 2)
            with pe.Fori(1, STEPS // 2 - 1) as i:
                step(i, 0, 2)
                step(i, 1, 2)
            step(STEPS // 2 - 1, 0, 1)
            step(STEPS // 2 - 1, 1, 0)

            pe.wait_ge(nm_lo, STEPS)
            for c in range(NCH):
                pe.wait_ge(o_norm, c + 1)
                wait(pe, o_res, c - 1)
                for mt in range(KT):
                    for kt in range(KT):
                        m = mm(ps[:, 2 * (c % 2) + mt, :], wo_s[:, kt, mt * P:(mt + 1) * P], a_in[:, c % 2, kt, :],
                               start=kt == 0, stop=kt == KT - 1)
                m.then_inc(o_mm, 1)
            pe.wait_ge(exp_ok, UNITS * STEPS)
            pe.wait_ge(o_ev, STEPS)
            layer_norm(1, lambda c: pe.wait_ge(o_res, c + 1))

            def feed_forward(k):
                base = k * FN
                pe.wait_ge(f_sum, k + 1)
                for kt in range(KT):
                    m = mm(ps[:, 0, 0:BATCH], e1_s[:, kt, :], gm[:, kt, :], start=kt == 0, stop=kt == KT - 1)
                m.then_inc(f_g, 1)
                pe.wait_ge(f_ga, 3 * k + 1)
                mm(ps[0:64, 1, 0:BATCH], e2_s[:], gh1[:], start=True, stop=True).then_inc(f_g, 1)
                pe.wait_ge(f_ga, 3 * k + 2)
                mm(ps[:, 2, 0:BATCH], e3_s[:], gh2[0:64, :], start=True, stop=True).then_inc(f_g, 1)
                pe.wait_ge(f_ga, 3 * k + 3)

                def layers(n, c, has):
                    if has(0):
                        if has(-NCH):
                            pe.wait_ge(f_up, base + n - NCH + 1)
                        if has(-1):
                            pe.wait_ge(f_a1, base + n)
                        for mt in range(KT):
                            for kt in range(KT):
                                m = mm(ps[:, mt, :], c1_s[:, kt, mt * P:(mt + 1) * P], YT[:, kt, ch(c)],
                                       start=kt == 0, stop=kt == KT - 1)
                        m.then_inc(f_h1, 1)
                    if has(-1):
                        pe.wait_ge(f_a1, base + n)
                        if has(-2):
                            pe.wait_ge(f_a2, base + n - 1)
                        for kt in range(KT):
                            m = mm(ps[:, 2, :], c2_s[:, kt, :], h1[:, (c - 1) % 2, kt, :], start=kt == 0, stop=kt == KT - 1)
                        m.then_inc(f_h2, 1)
                    if has(-2):
                        pe.wait_ge(f_a2, base + n - 1)
                        if has(-3):
                            pe.wait_ge(f_a3, base + n - 2)
                        mm(ps[0:64, 3, :], c3_s[:], h2[:, (c - 2) % 2, :], start=True, stop=True).then_inc(f_h3, 1)
                    if has(-3):
                        pe.wait_ge(f_a3, base + n - 2)
                        if has(-4):
                            pe.wait_ge(f_th, base + n - 3)
                        mm(ps[:, 4, :], c4_s[0:64, :], h3[0:64, (c - 3) % 2, :], start=True, stop=True).then_inc(f_z, 1)

                for n in range(NCH):
                    layers(n, n, lambda d: n + d >= 0)
                with pe.Fori(1, CYCLES) as cy:
                    for c in range(NCH):
                        layers(cy * NCH + c, c, lambda d: True)
                for n in range(FN, FN + LAG):
                    layers(n, n % NCH, lambda d: n + d < FN)

            pe.wait_ge(ln_std, 2 * NCH)
            pe.wait_ge(ln_cent, 2 * NCH)
            feed_forward(0)
            pe.wait_ge(f_th, FN)
            layer_norm(2, lambda c: pe.wait_ge(f_out, c + 1))

            pe.wait_ge(ln_std, 3 * NCH)
            pe.wait_ge(ln_cent, 3 * NCH)
            for c in range(NCH):
                pe.wait_ge(ln_out, 2 * NCH + c + 1)
                wait(pe, l_hg, c - 1)
                for kt in range(KT):
                    m = mm(ps[0:HD, c % 2, :], g1_s[:, kt, :], YT[:, kt, ch(c)], start=kt == 0, stop=kt == KT - 1)
                m.then_inc(l_hm, 1)
            pe.wait_ge(l_hg, NCH)

            def project(n, p):
                pe.wait_ge(l_ys, n + 1)
                wait(pe, l_silu, n)
                for kt in range(KT):
                    m = mm(ps[:, 0, :], y_st8[:, p, kt, :], lqk_s[:, kt, :], start=kt == 0, stop=kt == KT - 1)
                m.then_inc(l_qk, 1)
                wait(pe, l_v, n)
                wait(pe, l_gate, n)
                for kt in range(KT):
                    mm(ps[:, 1, 0:DIM], y_st8[:, p, kt, :], lv_s[:, kt, :], start=kt == 0, stop=kt == KT - 1)
                mm(ps[:, 1, DIM:2 * DIM], hg_tile[:, p, :], g2_s[:], start=True, stop=True).then_inc(l_vg, 1)

            def turn(n, p):
                pe.wait_ge(l_rope, n + 1)
                wait(pe, l_kt, n)
                wait(pe, l_qt, n)
                wait(pe, l_qx, n)
                wait(pe, l_ye, n - 1)
                for i in range(2 * KT):
                    m = pe.transpose(ps[:, 2, i * P:(i + 1) * P], qk_r[:, p, i * P:(i + 1) * P], ident[:])
                m.then_inc(l_t, 1)

            def energy(n, p, kt):
                if kt == 0:
                    pe.wait_ge(l_kt, n + 1)
                    pe.wait_ge(l_qx, n + 1)
                wait(pe, l_em, KT * n + kt)
                for half in range(2):
                    m = mm(ps[:, 3 + half, :], k_t[:, p, kt, :], q_x[:, kt, 4 * half:4 * half + 4, :], start=True, stop=True)
                m.then_inc(l_e, 1)

            def attend(n, p, first):
                pe.wait_ge(l_qt, n + 1)
                pe.wait_ge(l_sx, n + 1)
                wait(pe, l_oe, n)
                for g in range(4):
                    mm(ps[:, 6, g * P:(g + 1) * P], s_x[:, 4 * g:4 * g + 4, :], q_t[:, p, g // 2, :],
                       start=g == 0, stop=False, skip_group_check=True)
                pe.wait_ge(l_em, KT * (n + 1))
                for g in range(4):
                    for j in range(4):
                        h = 4 * g + j
                        m = mm(ps[32 * j:32 * j + HD, 6, g * P:(g + 1) * P], v_r[:, p, h * HD:(h + 1) * HD], e_m[:, h, :],
                               start=False, stop=g == 3, skip_group_check=True)
                m.then_inc(l_o, 1)
                for kt in range(KT):
                    m = mm(ps[:, 5, kt * P:(kt + 1) * P], qk_r[:, p, DIM + kt * P:DIM + (kt + 1) * P],
                           v_r[:, p, kt * P:(kt + 1) * P], start=first and kt == 0, stop=kt == KT - 1, skip_group_check=True)
                m.then_inc(l_s, 1)

            def rows(n):
                pe.wait_ge(l_oe, n + 1)
                wait(pe, l_x, n)
                for g in range(4):
                    m = pe.transpose(ps[:, 7, g * P:(g + 1) * P], o_t[:, g * P:(g + 1) * P], ident[:])
                m.then_inc(l_ot, 1)

            def norm_turn(n, p):
                pe.wait_ge(l_n, n + 1)
                pe.wait_ge(l_kt, n + 2 if n_more(n) else n + 1)
                pe.wait_ge(l_qt, n + 2 if n_more(n) else n + 1)
                pe.wait_ge(l_qx, n + 2 if n_more(n) else n + 1)
                for kt in range(KT):
                    m = pe.transpose(ps[:, 2, kt * P:(kt + 1) * P], o_n[:, p, kt * P:(kt + 1) * P], ident[:])
                m.then_inc(l_y, 1)

            def n_more(n):
                return not isinstance(n, int) or n < TILES - 1

            def out_proj(n, p):
                pe.wait_ge(l_ye, n + 1)
                pe.wait_ge(l_r, n + 1)
                for mt in range(KT):
                    for kt in range(KT):
                        m = mm(ps[:, 7, mt * P:(mt + 1) * P], lo_s[:, kt, mt * P:(mt + 1) * P], on_t[:, p, kt, :],
                               start=kt == 0, stop=kt == KT - 1)
                m.then_inc(l_w, 1)

            def tile(n, p, first, last, begin=False):
                if not last:
                    project(n + 1, 1 - p)
                energy(n, p, 0)
                if not begin:
                    norm_turn(n - 1, 1 - p)
                energy(n, p, 1)
                if not begin:
                    out_proj(n - 1, 1 - p)
                if not last:
                    turn(n + 1, 1 - p)
                attend(n, p, first)
                rows(n)

            project(0, 0)
            turn(0, 0)
            for b in range(BATCH):
                t0 = b * TPB
                tile(t0, 0, True, False, begin=b == 0)
                with pe.Fori(0, TPB // 2 - 1) as i:
                    tile(t0 + 2 * i + 1, 1, False, False)
                    tile(t0 + 2 * i + 2, 0, False, False)
                tile(t0 + TPB - 1, 1, False, b == BATCH - 1)
            norm_turn(TILES - 1, 1)
            out_proj(TILES - 1, 1)

            pe.wait_ge(l_em, KT * TILES)
            pe.wait_ge(l_oe, TILES)
            pe.wait_ge(l_x, TILES)
            layer_norm(3, lambda c: pe.wait_ge(l_x, 4 * (c + 1)))
            pe.wait_ge(ln_std, 4 * NCH)
            pe.wait_ge(ln_cent, 4 * NCH)
            feed_forward(1)

            pe.wait_ge(f_th, 2 * FN)
            for c in range(NCH):
                pe.wait_ge(f_out, NCH + c + 1)
                wait(pe, y_eva, c - 1)
                wait(pe, y_evd, c - 1)
                for t in range(4):
                    for kt in range(KT):
                        tok = c * CH + t * P
                        m = pe.transpose(ps[:, 2 * (c % 2) + t // 2, (t % 2) * DIM + kt * P:(t % 2) * DIM + (kt + 1) * P],
                                         XT[:, kt, tok:tok + P], ident[:])
                m.then_inc(y_tr, 1)

        @block.scalar
        def _(act):
            fn = act.activation
            act.wait_ge(w_ld, 16 * len(weights))
            for c in range(NCH):
                act.wait_ge(x_tr, c + 1)
                act.copy(XT[:, 0, ch(c)], ps[:, 2 * (c % 2), :]).then_inc(x_eva, 1)

            def layer_norm(k):
                for c in range(NCH + 1):
                    if c < NCH:
                        act.wait_ge(ln_cent, k * NCH + c + 1)
                        wait(act, ln_var, k * NCH + c - 1)
                        fn(sq[:, c % 2], YT[:, :, ch(c)], ACT.Square).then_inc(ln_sq, 1)
                    if c >= 1:
                        v = c - 1
                        act.wait_ge(ln_var, k * NCH + v + 1)
                        wait(act, ln_rec, k * NCH + v - 1)
                        fn(std[:, v % 2, :], ps[:, 6 + v % 2, :], ACT.Sqrt, bias=eps[:]).then_inc(ln_std, 1)

            act.wait_ge(consts, 5)
            layer_norm(0)

            for c in range(NCH):
                o, p = 4 * (c % 2), c % 2
                act.wait_ge(p_mm, c + 1)
                wait(act, p_low, c - 1)
                wait(act, p_st[p], 16 * 15 * (c // 2))
                for n in range(3):
                    b = bias[:, BQ + n:BQ + n + 1]
                    fn(qkf[:, p, n, :], ps[:, o + n, :], ACT.Identity, bias=b)
                    m = fn(part[:, p, 0, n, :], ps[:, o + n, :], ACT.Identity, bias=b)
                m.then_inc(p_act, 1)

            def step(i, p):
                s = 2 * i + p
                for t in range(KTILES):
                    for j in range(GROUP):
                        u = GROUP * t + j
                        act.wait_ge(qk_mm, UNITS * s + u + 1)
                        if j == 0:
                            wait(act, pv_mm, KTILES * s + t - 1)
                        fn(prob[:, u % 8, :], ps[:, 4 + u % 3, :], ACT.Exp, scale=HD ** -0.5).then_inc(exp_ok, 1)
                act.wait_ge(pv_mm, KTILES * (s + 1))
                wait(act, o_st[p], 16 * i)
                act.copy(o_sb[:, p, :], ps[:, 7, :]).then_inc(o_ev, 1)

            step(0, 0)
            step(0, 1)
            with act.Fori(1, STEPS // 2) as i:
                step(i, 0)
                step(i, 1)

            layer_norm(1)

            def feed_forward(k):
                base = k * FN
                act.wait_ge(f_g, 3 * k + 1)
                fn(gh1[:], ps[:, 0, 0:BATCH], ACT.Gelu, bias=bias[:, F1:F1 + 1], scale=1.0 / SEQ).then_inc(f_ga, 1)
                act.wait_ge(f_g, 3 * k + 2)
                fn(gh2[0:64, :], ps[0:64, 1, 0:BATCH], ACT.Gelu, bias=bias[0:64, F2:F2 + 1]).then_inc(f_ga, 1)
                act.wait_ge(f_g, 3 * k + 3)
                fn(gth[:], ps[:, 2, 0:BATCH], ACT.Tanh, bias=half_b[:, 1:2], scale=0.5).then_inc(f_ga, 1)

                def layers(n, c, has):
                    if has(0):
                        act.wait_ge(f_h1, base + n + 1)
                        if has(-2):
                            act.wait_ge(f_h2, base + n - 1)
                        for mt in range(KT):
                            m = fn(h1[:, c % 2, mt, :], ps[:, mt, :], ACT.Gelu, bias=bias[:, D1 + mt:D1 + mt + 1])
                        m.then_inc(f_a1, 1)
                    if has(-1):
                        act.wait_ge(f_h2, base + n)
                        if has(-3):
                            act.wait_ge(f_h3, base + n - 2)
                        fn(h2[:, (c - 1) % 2, :], ps[:, 2, :], ACT.Gelu, bias=bias[:, D2:D2 + 1]).then_inc(f_a2, 1)
                    if has(-2):
                        act.wait_ge(f_h3, base + n - 1)
                        if has(-4):
                            act.wait_ge(f_z, base + n - 3)
                        fn(h3[0:64, (c - 2) % 2, :], ps[0:64, 3, :], ACT.Gelu, bias=bias[0:64, D3:D3 + 1]).then_inc(f_a3, 1)
                    if has(-3):
                        act.wait_ge(f_z, base + n - 2)
                        if has(-5):
                            act.wait_ge(f_cs, base + n - 4)
                        fn(th[:, (c - 3) % 2, :], ps[:, 4, :], ACT.Tanh, bias=half_b[:, 0:1], scale=0.5).then_inc(f_th, 1)

                for n in range(NCH):
                    layers(n, n, lambda d: n + d >= 0)
                with act.Fori(1, CYCLES) as cy:
                    for c in range(NCH):
                        layers(cy * NCH + c, c, lambda d: True)
                for n in range(FN, FN + LAG):
                    layers(n, n % NCH, lambda d: n + d < FN)

            feed_forward(0)
            layer_norm(2)

            for c in range(NCH):
                act.wait_ge(l_hm, c + 1)
                act.copy(h_g[:, ch(c)], ps[0:HD, c % 2, :]).then_inc(l_hg, 1)

            def front(n, p):
                act.wait_ge(l_qk, n + 1)
                wait(act, l_rope, n - 1)
                fn(qk_a[:, p, :], ps[:, 0, :], ACT.Silu).then_inc(l_silu, 1)
                act.wait_ge(l_vg, n + 1)
                wait(act, l_s, n - 1)
                act.copy(v_r[:, p, :], ps[:, 1, 0:DIM]).then_inc(l_v, 1)
                wait(act, l_r, n - 1)
                fn(gate[:, p, :], ps[:, 1, DIM:2 * DIM], ACT.Tanh, scale=0.5).then_inc(l_gate, 1)

            def turned(n, p):
                act.wait_ge(l_t, n + 1)
                act.wait_ge(l_qx, n + 1)
                wait(act, l_e, KT * (n - 1))
                act.copy(k_t[:, p].rearrange("p a b -> p (a b)"), ps[:, 2, KT * P:2 * KT * P]).then_inc(l_kt, 1)
                wait(act, l_o, n - 1)
                act.copy(q_t[:, p].rearrange("p a b -> p (a b)"), ps[:, 2, 0:KT * P]).then_inc(l_qt, 1)

            def affine(n, p):
                act.wait_ge(l_y, n + 1)
                wait(act, l_w, n - 1)
                for kt in range(KT):
                    m = fn(on_t[:, p, kt, :], ps[:, 2, kt * P:(kt + 1) * P], ACT.Identity,
                           bias=bias[:, LB + kt:LB + kt + 1], scale=bias[:, LW + kt:LW + kt + 1])
                m.then_inc(l_ye, 1)

            def tile(n, p, last, begin=False):
                if not last:
                    front(n + 1, 1 - p)
                if not begin:
                    affine(n - 1, 1 - p)
                if not last:
                    turned(n + 1, 1 - p)
                act.wait_ge(l_o, n + 1)
                wait(act, l_ot, n)
                act.copy(o_t, ps[:, 6, :]).then_inc(l_oe, 1)

            front(0, 0)
            turned(0, 0)
            tile(0, 0, False, begin=True)
            tile(1, 1, False)
            tile(2, 0, False)
            with act.Fori(1, TILES // 2 - 1) as i:
                tile(2 * i + 1, 1, False)
                tile(2 * i + 2, 0, False)
            tile(TILES - 1, 1, True)
            affine(TILES - 1, 1)

            layer_norm(3)
            feed_forward(1)
            for c in range(NCH):
                act.wait_ge(y_tr, c + 1)
                wait(act, y_st[c % 2], 16 * (c // 2))
                act.copy(x_row[:, c % 2, 0:2].rearrange("p a b -> p (a b)"), ps[:, 2 * (c % 2), :]).then_inc(y_eva, 1)

        @block.vector
        def _(dve):
            dve.memset(ones[:], 1.0 / DIM).then_inc(consts, 1)
            dve.memset(eps[:], EPS).then_inc(consts, 1)
            dve.memset(mhalf[:], -0.5).then_inc(consts, 1)
            dve.memset(vals[:, :, :, HD:32], 1.0).then_inc(v_ones, 1)
            dve.wait_ge(w_ld, 16 * len(weights))
            dve.tensor_copy(c4_s[:], last_c[:, 0:1].broadcast_to((64, P))).then_inc(consts, 1)
            dve.tensor_copy(e3_s[:], last_c[:, 1:2].broadcast_to((64, P))).then_inc(consts, 1)
            dve.tensor_scalar(half_b[:, 0:1], bias[:, D4:D4 + 1], 0.5, None, ALU.mult)
            dve.tensor_scalar(half_b[:, 1:2], bias[:, F3:F3 + 1], 0.5, None, ALU.mult)
            dve.tensor_tensor(coup[:, 0:1], bias[:, AR:AR + 1], bias[:, SG:SG + 1], ALU.mult).then_inc(c_dve, 1)
            dve.wait_ge(c_dve, 1)
            dve.tensor_scalar(coup[:, 1:2], coup[:, 0:1], 0.3, None, ALU.mult)
            dve.tensor_scalar(coup[:, 2:3], bias[:, SG:SG + 1], 0.1, None, ALU.mult)
            dve.tensor_scalar(coup[:, 3:4], coup[:, 0:1], 0.7, None, ALU.mult).then_inc(c_dve, 1)
            for c in range(NCH):
                dve.wait_ge(x_tr, c + 1)
                dve.tensor_copy(XT[:, 1, ch(c)], ps[:, 2 * (c % 2) + 1, :]).then_inc(x_evd, 1)

            def layer_norm(k):
                for c in range(NCH + 1):
                    if c < NCH:
                        dve.wait_ge(ln_mean, k * NCH + c + 1)
                        dve.tensor_tensor(YT[:, :, ch(c)], XT[:, :, ch(c)],
                                          ps[:, 4 + c % 2:5 + c % 2, :].broadcast_to((P, KT, CH)),
                                          ALU.subtract).then_inc(ln_cent, 1)
                    if c >= 1:
                        v = c - 1
                        dve.wait_ge(ln_std, k * NCH + v + 1)
                        dve.reciprocal(rec[:, v % 2, :], std[:, v % 2, :]).then_inc(ln_rec, 1)
                        dve.wait_ge(ln_rec, k * NCH + v + 1)
                        dve.tensor_tensor(YT[:, :, ch(v)], YT[:, :, ch(v)],
                                          rec[:, v % 2:v % 2 + 1, :].broadcast_to((P, KT, CH)),
                                          ALU.mult).then_inc(ln_out, 1)

            dve.wait_ge(x_eva, NCH)
            dve.wait_ge(x_evd, NCH)
            layer_norm(0)

            dve.wait_ge(v_ones, 1)
            for c in range(NCH):
                p, b = c % 2, c // CPG
                dve.wait_ge(p_act, c + 1)
                wait(dve, p_st[p], 16 * 15 * (c // 2))
                dve.tensor_tensor(res[:, p], qkf[:, p], part[:, p, 0], ALU.subtract).then_inc(p_res, 1)
                dve.tensor_tensor(vals[:, b * KV_HEADS:(b + 1) * KV_HEADS, 4 * (c % CPG):4 * (c % CPG) + 4, 0:HD]
                                  .rearrange("p g t d -> p t g d"),
                                  ps[:, 4 * (c % 2) + 3, 0:4 * KVD].rearrange("p (t g d) -> p t g d", t=4, g=KV_HEADS),
                                  bv_s[:].rearrange("p (a g d) -> p a g d", a=1, g=KV_HEADS).broadcast_to((P, 4, KV_HEADS, HD)),
                                  ALU.add).then_inc(p_val, 1)
                dve.wait_ge(p_res, c + 1)
                dve.tensor_copy(part[:, p, 1], res[:, p]).then_inc(p_mid, 1)
                dve.wait_ge(p_mid, c + 1)
                dve.tensor_tensor(part[:, p, 2], res[:, p], part[:, p, 1], ALU.subtract).then_inc(p_low, 1)

            for p in range(2):
                dve.wait_ge(p_st[p], 16 * 15 * NCH // 2)
            for p in range(2):
                dve.memset(kb[ROWS:ROWS_M, p, :], 1.0).then_inc(kb_ones, 1)

            def maxima(s):
                for u in range(MAXU):
                    dve.wait_ge(a_mm, MAXU * s + u + 1)
                    b = 2 * (u % 2)
                    dve.tensor_reduce(mx[:, u:u + 1], ps[:, b:b + 2, :], mybir.AxisListType.XY, ALU.max).then_inc(a_max, 1)
                dve.wait_ge(a_max, MAXU * (s + 1))
                halves = mx[:].rearrange("p (a b) -> p a b", b=2)
                dve.tensor_tensor(mxq[:], halves[:, :, 0], halves[:, :, 1], ALU.max).then_inc(a_fin, 1)
                dve.wait_ge(a_tr, s + 1)
                wait(dve, m_ld, 32 * s)
                turned = ps[0:MAXU // 2, 2, 0:P]
                dve.tensor_scalar(negm[:, 0, :], turned, -1.0, None, ALU.mult).then_inc(nm_hi, 1)
                dve.wait_ge(nm_hi, s + 1)
                dve.scalar_tensor_tensor(out=negm[:, 1, :], in0=turned, scalar=-1.0, in1=negm[:, 0, :],
                                         op0=ALU.mult, op1=ALU.subtract).then_inc(nm_lo, 1)

            maxima(0)
            with dve.Fori(1, STEPS) as s:
                maxima(s)

            dve.wait_ge(den_ld, 16)
            dve.reciprocal(den, den).then_inc(den_inv, 1)
            for c in range(NCH):
                dve.wait_ge(o_ld[c % 2], 128 * (c // 2 + 1))
                dve.tensor_tensor(a_in[:, c % 2], a_in[:, c % 2], a_inv[:, c % 2], ALU.mult).then_inc(o_norm, 1)
                if c >= 1:
                    v = c - 1
                    dve.wait_ge(o_mm, v + 1)
                    for kt in range(KT):
                        m = dve.scalar_tensor_tensor(out=XT[:, kt, ch(v)], in0=ps[:, 2 * (v % 2) + kt, :],
                                                     scalar=bias[:, BO + kt:BO + kt + 1], in1=XT[:, kt, ch(v)],
                                                     op0=ALU.add, op1=ALU.add)
                    m.then_inc(o_res, 1)
            dve.wait_ge(o_mm, NCH)
            for kt in range(KT):
                m = dve.scalar_tensor_tensor(out=XT[:, kt, ch(NCH - 1)], in0=ps[:, 2 * ((NCH - 1) % 2) + kt, :],
                                             scalar=bias[:, BO + kt:BO + kt + 1], in1=XT[:, kt, ch(NCH - 1)],
                                             op0=ALU.add, op1=ALU.add)
            m.then_inc(o_res, 1)
            dve.wait_ge(o_res, NCH)
            layer_norm(1)

            def feed_forward(k):
                base = k * FN
                dve.wait_ge(ln_out, (2 * k + 2) * NCH)
                dve.tensor_reduce(gm[:], YT[:].rearrange("p k (b n) -> p k b n", b=BATCH), AX_X, ALU.add).then_inc(f_sum, 1)
                dve.wait_ge(f_ga, 3 * k + 3)
                dve.tensor_scalar(cb[:], gth[:], coup[:, 3:4], coup[:, 2:3], ALU.mult, ALU.add).then_inc(f_cb, 1)
                dve.wait_ge(f_cb, k + 1)

                def update(n, c):
                    p, b = c % 2, c // CPG
                    dve.wait_ge(f_th, base + n + 1)
                    dve.tensor_scalar(cs[:, p, :], th[:, p, :], coup[:, 1:2], cb[:, b:b + 1], ALU.mult, ALU.add).then_inc(f_cs, 1)
                    dve.wait_ge(f_cs, base + n + 1)
                    dve.tensor_tensor(tw[:, p, 0, :], cs[:, p, :], YT[:, 1, ch(c)], ALU.mult)
                    dve.tensor_tensor(tw[:, p, 1, :], cs[:, p, :], YT[:, 0, ch(c)], ALU.mult).then_inc(f_tw, 1)
                    dve.wait_ge(f_tw, base + n + 1)
                    dve.tensor_tensor(YT[:, 0, ch(c)], YT[:, 0, ch(c)], tw[:, p, 0, :], ALU.add)
                    dve.tensor_tensor(YT[:, 1, ch(c)], YT[:, 1, ch(c)], tw[:, p, 1, :], ALU.subtract).then_inc(f_up, 1)

                with dve.Fori(0, CYCLES) as cy:
                    for c in range(NCH):
                        update(cy * NCH + c, c)
                for c in range(NCH):
                    dve.wait_ge(f_up, base + FN - NCH + c + 1)
                    dve.tensor_tensor(XT[:, :, ch(c)], XT[:, :, ch(c)], YT[:, :, ch(c)], ALU.add).then_inc(f_out, 1)

            feed_forward(0)
            dve.wait_ge(f_out, NCH)
            layer_norm(2)

            def halves(ap):
                v = ap.rearrange("p (h a e) -> p h a e", a=2, e=HD // 2)
                return v[:, :, 0, :], v[:, :, 1, :]

            def rope(n, p, t):
                dve.wait_ge(l_silu, n + 1)
                wait(dve, l_s, n - 1)
                wait(dve, l_t, n - 1)
                a, b = halves(qk_a[:, p, :])
                ra, rb = halves(qk_r[:, p, :])
                co = cos_s[:, bass.ds(t, 1), :].broadcast_to((P, 2 * HEADS, HD // 2))
                si = sin_s[:, bass.ds(t, 1), :].broadcast_to((P, 2 * HEADS, HD // 2))
                for i, (u, v) in enumerate(((a, co), (b, si), (b, co), (a, si))):
                    m = dve.tensor_tensor(rt[:, i], u, v, ALU.mult)
                m.then_inc(l_rt, 1)
                dve.wait_ge(l_rt, n + 1)
                dve.tensor_tensor(ra, rt[:, 0], rt[:, 1], ALU.subtract)
                dve.tensor_tensor(rb, rt[:, 2], rt[:, 3], ALU.add).then_inc(l_rope, 1)

            def spread(n, p):
                dve.wait_ge(l_t, n + 1)
                wait(dve, l_e, KT * n)
                for kt in range(KT):
                    m = dve.tensor_tensor(q_x[:, kt], ps[:, 2, kt * P:(kt + 1) * P].rearrange("p (a n) -> p a n", a=1)
                                          .broadcast_to((P, HPK, P)),
                                          head[:].rearrange("p (h a) -> p h a", a=1).broadcast_to((P, HPK, P)), ALU.mult)
                m.then_inc(l_qx, 1)

            def mask(n, kt):
                dve.wait_ge(l_e, KT * n + kt + 1)
                if kt == 0:
                    wait(dve, l_o, n)
                dve.tensor_tensor(e_m[:, HPK * kt:HPK * (kt + 1), :],
                                  ps[:, 3:5, :].rearrange("p a (h n) -> p (a h) n", h=4),
                                  causal[:].rearrange("p (a n) -> p a n", a=1).broadcast_to((P, HPK, P)),
                                  ALU.mult).then_inc(l_em, 1)

            def state(n, reset):
                dve.wait_ge(l_s, n + 1)
                dve.wait_ge(l_o, n + 1)
                dve.wait_ge(l_bn, n + 1)
                if reset:
                    dve.memset(s_x[:, :, 0:HD], 0.0).then_inc(l_sx, 1)
                else:
                    dve.tensor_tensor(s_x[:, :, 0:HD], ps[:, 5, 0:DIM].rearrange("p (h d) -> p h d", h=HEADS),
                                      diag[:], ALU.mult).then_inc(l_sx, 1)

            def normalise(n, p, reset):
                dve.wait_ge(l_gate, n + 1)
                dve.tensor_scalar(gate[:, p, :], gate[:, p, :], 0.5, 0.5, ALU.mult, ALU.add).then_inc(l_gt, 1)
                dve.wait_ge(l_gt, n + 1)
                dve.wait_ge(l_ot, n + 1)
                dve.tensor_tensor(o_r[:, p, :].rearrange("p (h d) -> p h d", h=HEADS),
                                  ps[:, 7, :].rearrange("p (h r) -> p h r", r=32)[:, :, 0:HD],
                                  gate[:, p, :].rearrange("p (h d) -> p h d", h=HEADS), ALU.mult).then_inc(l_r, 1)
                dve.wait_ge(l_r, n + 1)
                dve.bn_stats(stats[:], o_r[:, p, :]).then_inc(l_bn, 1)
                state(n, reset)
                dve.bn_aggr(mv[:, p, :], stats[:]).then_inc(l_mv, 1)
                dve.wait_ge(l_mv, n + 1)
                dve.tensor_scalar(var_e[:, p:p + 1], mv[:, p, 1:2], EPS, None, ALU.add).then_inc(l_ve, 1)
                wait(dve, l_y, n - 1)
                dve.wait_ge(l_rs, n + 1)
                dve.tensor_scalar(o_n[:, p, :], o_r[:, p, :], mv[:, p, 0:1], rstd[:, p:p + 1],
                                  ALU.subtract, ALU.mult).then_inc(l_n, 1)

            def residual(n):
                dve.wait_ge(l_w, n + 1)
                dve.tensor_tensor(XT[:, :, bass.ds(n * P, P)], XT[:, :, bass.ds(n * P, P)],
                                  ps[:, 7, 0:DIM].rearrange("p (k n) -> p k n", k=KT), ALU.add).then_inc(l_x, 1)

            def tile(n, p, t, reset=False, last=False, begin=False):
                if not last:
                    rope(n + 1, 1 - p, t)
                mask(n, 0)
                mask(n, 1)
                if not begin:
                    residual(n - 1)
                if not last:
                    spread(n + 1, 1 - p)
                normalise(n, p, reset)

            rope(0, 0, 0)
            spread(0, 0)
            dve.memset(s_x, 0.0).then_inc(l_sx, 1)
            for b in range(BATCH):
                t0 = b * TPB
                tile(t0, 0, 1, begin=b == 0)
                with dve.Fori(0, TPB // 2 - 1) as i:
                    tile(t0 + 2 * i + 1, 1, 2 * i + 2)
                    tile(t0 + 2 * i + 2, 0, 2 * i + 3)
                tile(t0 + TPB - 1, 1, 0, reset=True, last=b == BATCH - 1)
            residual(TILES - 1)

            dve.wait_ge(l_x, TILES)
            layer_norm(3)
            feed_forward(1)
            for c in range(NCH):
                dve.wait_ge(y_tr, c + 1)
                wait(dve, y_st[c % 2], 16 * (c // 2))
                dve.tensor_copy(x_row[:, c % 2, 2:4].rearrange("p a b -> p (a b)"), ps[:, 2 * (c % 2) + 1, :]).then_inc(y_evd, 1)

        @block.gpsimd
        def _(pool):
            pool.wait_ge(p_val, NCH)
            for p in range(2):
                pool.wait_ge(p_st[p], 16 * 15 * NCH // 2)

            def values(s, p):
                wait(pool, pv_mm, KTILES * (s - 1))
                pool.tensor_copy(vst[:, p].rearrange("p t d -> p (t d)"),
                                 vals[:, s // CPG].rearrange("p t d -> p (t d)")).then_inc(v_st, 1)

            values(0, 0)
            values(1, 1)
            with pool.Fori(1, STEPS // 2) as i:
                values(2 * i, 0)
                values(2 * i + 1, 1)

            pool.wait_ge(ln_out, 3 * NCH)
            pool.wait_ge(l_hg, NCH)

            def columns(n, p):
                wait(pool, l_vg, n - 1)
                pool.tensor_copy(hg_tile[:, p, :], h_g[:, bass.ds(n * P, P)])
                pool.tensor_copy(y_st8[:, p], YT[:, :, bass.ds(n * P, P)]).then_inc(l_ys, 1)

            def root(n, p):
                pool.wait_ge(l_ve, n + 1)
                wait(pool, l_n, n - 1)
                pool.tensor_tensor(rstd[:, p:p + 1], var_e[:, p:p + 1], mhalf[:], ALU.pow).then_inc(l_rs, 1)

            columns(0, 0)
            columns(1, 1)
            root(0, 0)
            columns(2, 0)
            root(1, 1)
            columns(3, 1)
            with pool.Fori(1, TILES // 2 - 1) as i:
                root(2 * i, 0)
                columns(2 * i + 2, 0)
                root(2 * i + 1, 1)
                columns(2 * i + 3, 1)
            root(TILES - 2, 0)
            root(TILES - 1, 1)


_INS = ['L0_attn_a_x', 'L0_attn_a_Wq', 'L0_attn_a_bq', 'L0_attn_a_Wk', 'L0_attn_a_bk', 'L0_attn_a_Wv',
        'L0_attn_a_bv', 'L0_attn_a_Wo', 'L0_attn_a_bo', 'L0_attn_b_Wq', 'L0_attn_b_Wk', 'L0_attn_b_Wv',
        'L0_attn_b_Wo', 'L0_attn_b_Wg1', 'L0_attn_b_Wg2', 'L0_attn_b_ln_w', 'L0_attn_b_ln_b',
        'L0_ffn_cn_w1', 'L0_ffn_cn_b1', 'L0_ffn_cn_w2', 'L0_ffn_cn_b2', 'L0_ffn_cn_w3', 'L0_ffn_cn_b3',
        'L0_ffn_cn_w4', 'L0_ffn_cn_b4', 'L0_ffn_gc_w1', 'L0_ffn_gc_b1', 'L0_ffn_gc_w2', 'L0_ffn_gc_b2',
        'L0_ffn_gc_w3', 'L0_ffn_gc_b3', 'L0_ffn_adaptive_range']


def shape_constants():
    f = np.float32
    inv_freq = (f(1.0) / f(10000.0) ** (np.arange(0, HD, 2, dtype=f) / f(HD))).astype(f)
    ang = (np.arange(SEQ, dtype=f)[:, None] * inv_freq[None, :]).astype(f)
    feature = np.arange(P)[:, None]
    return {
        "ident": np.eye(P, dtype=f), "cos": np.cos(ang).astype(f), "sin": np.sin(ang).astype(f),
        "causal": np.triu(np.ones((P, P), f)),
        "head": (feature // HD == np.arange(HPK)[None, :]).astype(f),
        "diag": (feature // HD == np.arange(DIM)[None, :] // HD % HPK).astype(f),
        "sign": np.where(feature < 64, 1.0, -1.0).astype(f),
    }


def lay_out(inputs):
    a = {n: np.ascontiguousarray(np.asarray(inputs[n])) for n in _INS}
    w = a["L0_attn_a_Wo"].reshape(GROUP, KV_HEADS, HD, DIM)
    a["L0_attn_a_Wo"] = np.ascontiguousarray(w.transpose(1, 0, 2, 3).reshape(DIM, DIM))
    return a


def kernel(**inputs):
    import numpy as _np
    import concourse.bacc as _bacc
    from concourse import mybir as _mybir
    from concourse.bass_utils import run_bass_kernel_spmd as _run

    nc = _bacc.Bacc("TRN2", target_bir_lowering=False, num_devices=1)
    arrays, args = {}, []
    named = {**lay_out(inputs), **shape_constants()}
    for name, a in named.items():
        arrays[f"in_{name}_dram"] = a
        args.append(nc.dram_tensor(f"in_{name}_dram", a.shape, _mybir.dt.from_np(a.dtype), kind="ExternalInput").ap())
    args.append(nc.dram_tensor("out_0_dram", (BATCH, SEQ, DIM), F32, kind="ExternalOutput").ap())
    hybrid_block(nc, *args)
    r = _run(nc, [arrays], core_ids=[0])
    return r.results[0]["out_0_dram"]
```

```python
from contextlib import ExitStack

import numpy as np

import concourse.bass as bass
from concourse import mybir

F32 = mybir.dt.float32
BF16 = mybir.dt.bfloat16
ACT = mybir.ActivationFunctionType
ALU = mybir.AluOpType
AX_X = mybir.AxisListType.X

P = 128
BATCH, SEQ, DIM = 2, 2048, 256
TOKENS = BATCH * SEQ
KT = DIM // P
CH = 512
NCH = TOKENS // CH
HEADS, KV_HEADS, HD = 16, 4, 16
GROUP = HEADS // KV_HEADS
KVD = KV_HEADS * HD
EPS = 1e-5

CPG = SEQ // CH
NKV = BATCH * KV_HEADS
STEPS = NKV * CPG
KTILES = SEQ // P
UNITS = KTILES * GROUP
MAXU = GROUP * (CH // P) * 2
Q_STACK = ((0, 3), (0, 2), (0, 1))
K_STACK = ((0, 3), (1, 2), (2, 1))
ROWS = 6 * HD
ROWS_M = ROWS + 2
LOADED = 16 * (len(Q_STACK) + len(K_STACK))

CYCLES = 3
FN = CYCLES * NCH
AHEAD = 16
MAXMM = 2 * MAXU
TURN = 2
LAG = 3

TILES = TOKENS // P
TPB = SEQ // P
HPK = P // HD


def hybrid_block(nc, x, wq, bq, wk, bk, wv, bv, wo, bo, lq, lk, lv, lo, g1, g2, ln_w, ln_b,
                 c1, d1, c2, d2, c3, d3, c4, d4, e1, f1, e2, f2, e3, f3, ar,
                 ident_in, cos_in, sin_in, causal_in, head_in, diag_in, sign_in, out):
    with ExitStack() as ctx:
        def sb(name, shape, dt=F32):
            return ctx.enter_context(nc.sbuf_tensor(name, shape, dt))

        def sem(name):
            return ctx.enter_context(nc.semaphore(name))

        q_scr = nc.dram_tensor("q_scr", [STEPS, 3, HD, GROUP, CH], BF16, kind="Internal").ap()
        k_scr = nc.dram_tensor("k_scr", [NKV, 3, HD, SEQ], BF16, kind="Internal").ap()
        o_scr = nc.dram_tensor("o_scr", [STEPS, GROUP, 32, CH], F32, kind="Internal").ap()
        inv_scr = nc.dram_tensor("inv_scr", [STEPS * GROUP, CH], F32, kind="Internal").ap()

        ps = ctx.enter_context(nc.psum_tensor("ps", [P, 8, CH], F32))

        XT = sb("XT", [P, KT, TOKENS])
        YT = sb("YT", [P, KT, TOKENS])
        ident = sb("ident", [P, P])
        ones = sb("ones", [P, P])
        eps = sb("eps", [P, 1])

        wq_s = sb("wq_s", [P, KT, DIM])
        wkk_s = sb("wkk_s", [P, KT, 2 * KVD])
        wv_s = sb("wv_s", [P, KT, KVD])
        wo_s = sb("wo_s", [P, KT, DIM])
        bv_s = sb("bv_s", [P, KVD])
        c1_s = sb("c1_s", [P, KT, DIM])
        c2_s = sb("c2_s", [P, KT, P])
        c3_s = sb("c3_s", [P, 64])
        c4_s = sb("c4_s", [64, P])
        e1_s = sb("e1_s", [P, KT, P])
        e2_s = sb("e2_s", [P, 64])
        e3_s = sb("e3_s", [64, P])
        last_c = sb("last_c", [64, 2])
        lqk_s = sb("lqk_s", [P, KT, 2 * DIM])
        lv_s = sb("lv_s", [P, KT, DIM])
        lo_s = sb("lo_s", [P, KT, DIM])
        g1_s = sb("g1_s", [P, KT, HD])
        g2_s = sb("g2_s", [HD, DIM])
        cos_s = sb("cos_s", [P, TPB, HD // 2])
        sin_s = sb("sin_s", [P, TPB, HD // 2])
        causal = sb("causal", [P, P])
        head = sb("head", [P, HPK])
        diag = sb("diag", [P, HEADS, HD])
        bias = sb("bias", [P, 20])
        BQ, BK, BO, D1, D2, D3, D4, F1, F2, F3, AR, LW, LB, SG = 0, 2, 3, 5, 7, 8, 9, 10, 11, 12, 13, 14, 16, 18
        half_b = sb("half_b", [P, 2])
        coup = sb("coup", [P, 4])

        def col(v):
            return v.rearrange("(p a) -> p a", a=1)

        def tiled(w):
            return w.rearrange("(k p) n -> p k n", p=P)

        weights = [
            (ident[:], ident_in), (wq_s[:], tiled(wq)),
            (wkk_s[:, :, 0:KVD], tiled(wk)), (wkk_s[:, :, KVD:2 * KVD], tiled(wk)), (wv_s[:], tiled(wv)),
            (bias[0:KVD, BK:BK + 1], col(bk)), (bias[KVD:P, BK:BK + 1], col(bk)),
            (bias[:, D2:D2 + 1], col(d2)), (bias[0:64, D3:D3 + 1], col(d3)),
            (bias[:, D4:D4 + 1], col(d4).broadcast_to((P, 1))),
            (bias[:, F1:F1 + 1], col(f1)), (bias[0:64, F2:F2 + 1], col(f2)),
            (bias[:, F3:F3 + 1], col(f3).broadcast_to((P, 1))),
            (bias[:, AR:AR + 1], col(ar).broadcast_to((P, 1))),
            (bias[:, SG:SG + 1], sign_in),
            (bv_s[:], bv.rearrange("(a n) -> a n", a=1).broadcast_to((P, KVD))),
            (wo_s[:], tiled(wo)), (c1_s[:], tiled(c1)), (c2_s[:], tiled(c2)), (c3_s[:], c3),
            (last_c[:, 0:1], c4), (e1_s[:], tiled(e1)), (e2_s[:], e2),
            (last_c[:, 1:2], e3),
            (lqk_s[:, :, 0:DIM], tiled(lq)), (lqk_s[:, :, DIM:2 * DIM], tiled(lk)), (lv_s[:], tiled(lv)),
            (lo_s[:], tiled(lo)), (g1_s[:], tiled(g1)), (g2_s[:], g2),
            (cos_s[:], cos_in.rearrange("(t p) e -> p t e", p=P)),
            (sin_s[:], sin_in.rearrange("(t p) e -> p t e", p=P)),
            (causal[:], causal_in), (head[:], head_in),
            (diag[:], diag_in.rearrange("p (h e) -> p h e", h=HEADS)),
        ]
        for at_, v in ((BQ, bq), (BO, bo), (D1, d1), (LW, ln_w), (LB, ln_b)):
            for kt in range(KT):
                weights.append((bias[:, at_ + kt:at_ + kt + 1], col(v[kt * P:(kt + 1) * P])))

        x_row = sb("x_row", [P, 2, 4, DIM])
        sq = sb("sq", [P, 2, KT, CH])
        std = sb("std", [P, 2, CH])
        rec = sb("rec", [P, 2, CH])
        vals = sb("vals", [P, NKV, KTILES, 32])
        o_sb = sb("o_sb", [P, 2, CH])
        mx = sb("mx", [P, MAXU])
        mxq = sb("mxq", [P, MAXU // 2])
        negm = sb("negm", [HD, 2, P], BF16)
        gm = sb("gm", [P, KT, BATCH])
        gh1 = sb("gh1", [P, BATCH])
        gh2 = sb("gh2", [64, BATCH])
        gth = sb("gth", [P, BATCH])
        cb = sb("cb", [P, BATCH])
        WORK = 13 * 1024
        work = sb("work", [P, WORK])
        at = [0]

        def take(*shape, dt=F32):
            n = int(np.prod(shape))
            words = n if dt == F32 else n // 2
            ap = work[:, at[0]:at[0] + words]
            at[0] += words
            assert at[0] <= WORK, at[0]
            if dt != F32:
                ap = ap.bitcast(dt)
            names = "abcd"[:len(shape)]
            return ap.rearrange(f"p ({' '.join(names)}) -> p {' '.join(names)}", **dict(zip(names, shape)))

        qkf = take(2, 3, CH)
        res = take(2, 3, CH)
        part = take(2, 3, 3, CH, dt=BF16)
        at[0] = 0
        ka, kb = take(2, SEQ, dt=BF16), take(2, SEQ, dt=BF16)
        qa, qb = take(2, GROUP, CH, dt=BF16), take(2, GROUP, CH, dt=BF16)
        vst = take(2, KTILES, 32)
        prob = take(8, CH)
        at[0] = 0
        a_in, a_inv, den = take(2, KT, CH), take(2, KT, CH), take(CH)
        at[0] = 0
        h1, h2, h3 = take(2, KT, CH), take(2, CH), take(2, CH)
        th, cs, tw = take(2, CH), take(2, CH), take(2, KT, CH)
        at[0] = 0
        y_st8 = take(2, KT, P)
        qk_a, qk_r = take(2, 2 * DIM), take(2, 2 * DIM)
        rt = take(4, 2 * HEADS, HD // 2)
        v_r, gate = take(2, DIM), take(2, DIM)
        k_t, q_t = take(2, KT, P), take(2, KT, P)
        q_x = take(KT, HPK, P)
        e_m = take(HEADS, P)
        s_x = take(HEADS, 32)
        o_t = take(CH)
        o_r, o_n = take(2, DIM), take(2, DIM)
        on_t = take(2, KT, P)
        hg_tile = sb("hg_tile", [HD, 2, P])
        h_g = vals[0:HD].rearrange("p a b c -> p (a b c)")
        stats = sb("stats", [P, 6])
        mv = sb("mv", [P, 2, 2])
        var_e = sb("var_e", [P, 2])
        rstd = sb("rstd", [P, 2])
        mhalf = sb("mhalf", [P, 1])

        names = """w_ld consts c_dve x_tr x_eva x_evd ln_mean ln_cent ln_sq ln_var ln_std ln_rec ln_out
            p_mm p_act p_res p_mid p_low p_val v_ones kb_ones a_mm a_max a_fin a_tr
            nm_hi nm_lo m_ld qk_mm exp_ok pv_mm o_ev v_st den_ld den_inv inv_st o_norm o_mm
            o_res f_sum f_g f_ga f_cb f_h1 f_a1 f_h2 f_a2 f_h3 f_a3 f_z f_th f_cs f_tw f_up f_out
            l_hm l_hg l_ys l_qk l_vg l_silu l_v l_gate l_rt l_rope l_t l_kt l_qt l_qx l_e l_em
            l_o l_s l_sx l_oe l_ot l_r l_bn l_mv l_ve l_rs l_n l_y l_ye l_w l_x
            y_tr y_eva y_evd """.split()
        S = {n: sem(n) for n in names}
        (w_ld, consts, c_dve, x_tr, x_eva, x_evd, ln_mean, ln_cent, ln_sq, ln_var, ln_std, ln_rec, ln_out,
         p_mm, p_act, p_res, p_mid, p_low, p_val, v_ones, kb_ones, a_mm, a_max, a_fin, a_tr,
         nm_hi, nm_lo, m_ld, qk_mm, exp_ok, pv_mm, o_ev, v_st, den_ld, den_inv, inv_st, o_norm, o_mm,
         o_res, f_sum, f_g, f_ga, f_cb, f_h1, f_a1, f_h2, f_a2, f_h3, f_a3, f_z, f_th, f_cs, f_tw, f_up, f_out,
         l_hm, l_hg, l_ys, l_qk, l_vg, l_silu, l_v, l_gate, l_rt, l_rope, l_t, l_kt, l_qt, l_qx, l_e, l_em,
         l_o, l_s, l_sx, l_oe, l_ot, l_r, l_bn, l_mv, l_ve, l_rs, l_n, l_y, l_ye, l_w, l_x,
         y_tr, y_eva, y_evd, ) = [S[n] for n in names]

        x_ld, p_st, qa_ld, qb_ld, o_st, o_ld, y_st = (
            [sem(f"{n}{p}") for p in range(2)] for n in ("x_ld", "p_st", "qa_ld", "qb_ld", "o_st", "o_ld", "y_st"))

        def ch(c):
            return slice(c * CH, (c + 1) * CH)

        def is_tile(m):
            return not isinstance(m, int) or 0 <= m < TILES

        def through_tiles(eng, visit):
            for n in range(4):
                visit(n, n % 2, n + 2)
            with eng.Fori(0, (TPB - 6) // 2) as i:
                visit(2 * i + 4, 0, 2 * i + 6)
                visit(2 * i + 5, 1, 2 * i + 7)
            for n in range(TPB - 2, TPB + 2):
                visit(n, n % 2, n + 2 - TPB)
            with eng.Fori(0, (TPB - 4) // 2) as i:
                visit(2 * i + TPB + 2, 0, 2 * i + 4)
                visit(2 * i + TPB + 3, 1, 2 * i + 5)
            for n in range(TILES - 2, TILES + 2):
                visit(n, n % 2, 0)

        def wait(eng, s, value):
            if not isinstance(value, int) or value > 0:
                eng.wait_ge(s, value)

        block = ctx.enter_context(nc.Block())

        @block.sync
        def _(sp):
            xr = x.rearrange("b (c t p) f -> (b c) p t f", t=4, p=P)
            yr = out.rearrange("b (c t p) f -> (b c) p t f", t=4, p=P)
            for c in range(NCH):
                wait(sp, x_tr, c - 1)
                sp.dma_start(x_row[:, c % 2], xr[c]).then_inc(x_ld[c % 2], 16)
                if c == 1:
                    for dst, src in weights:
                        sp.dma_start(dst, src).then_inc(w_ld, 16)

            for c in range(NCH):
                b, c4 = c // CPG, c % CPG
                for pt, done in ((0, p_act), (1, p_mid), (2, p_low)):
                    sp.wait_ge(done, c + 1)
                    for g in range(KV_HEADS):
                        s = (b * KV_HEADS + g) * CPG + c4
                        row = g % 2 * 64
                        sp.dma_start(q_scr[s, pt].rearrange("d j n -> j d n"),
                                     part[row:row + 64, c % 2, pt, g // 2, :]).then_inc(p_st[c % 2], 16)
                    sp.dma_start(k_scr[b * KV_HEADS:(b + 1) * KV_HEADS, pt, :, ch(c4)],
                                 part[0:64, c % 2, pt, 2, :]).then_inc(p_st[c % 2], 16)
            for p in range(2):
                sp.wait_ge(p_st[p], 16 * 15 * NCH // 2)

            def load(q_dst, k_dst, p, s, done):
                done = done[p]
                row = 0
                for first, n in Q_STACK:
                    sp.dma_start(q_dst[row:row + n * HD, p],
                                 q_scr[s, 0:n].rearrange("r d j n -> (r d) j n")).then_inc(done, 16)
                    row += n * HD
                row = 0
                for first, n in K_STACK:
                    sp.dma_start(k_dst[row:row + n * HD, p],
                                 k_scr[s // CPG, first:first + 1].broadcast_to((n, HD, SEQ))).then_inc(done, 16)
                    row += n * HD

            def leave(s, p, more):
                if more:
                    sp.wait_ge(nm_lo, s + 2)
                    for r in range(2):
                        sp.dma_start(qb[ROWS + r:ROWS + r + 1, 1 - p].rearrange("p j n -> p (j n)"),
                                     negm[:, r, :]).then_inc(m_ld, 16)
                sp.wait_ge(o_ev, s + 1)
                sp.dma_start(o_scr[s].rearrange("j r n -> (j r) n"), o_sb[:, p, :]).then_inc(o_st[p], 16)

            def refill(s, p):
                load(qb, kb, p, s + 2, qb_ld)

            def refill_max(s, p):
                sp.wait_ge(a_tr, s + 1)
                load(qa, ka, p, s + 2, qa_ld)

            for s in (0, 1):
                load(qa, ka, s, s, qa_ld)
            sp.wait_ge(kb_ones, 2)
            for s in (0, 1):
                load(qb, kb, s, s, qb_ld)
            sp.wait_ge(nm_lo, 1)
            for r in range(2):
                sp.dma_start(qb[ROWS + r:ROWS + r + 1, 0].rearrange("p j n -> p (j n)"), negm[:, r, :]).then_inc(m_ld, 16)
            refill_max(0, 0)
            with sp.Fori(0, STEPS // 2 - 2) as i:
                for p in range(2):
                    leave(2 * i + p, p, True)
                    refill(2 * i + p, p)
                    refill_max(2 * i + p + 1, 1 - p)
            leave(STEPS - 4, 0, True)
            refill(STEPS - 4, 0)
            refill_max(STEPS - 3, 1)
            leave(STEPS - 3, 1, True)
            refill(STEPS - 3, 1)
            leave(STEPS - 2, 0, True)
            leave(STEPS - 1, 1, False)
            for p in range(2):
                sp.wait_ge(o_st[p], 16 * STEPS // 2)

            sp.dma_start(den, o_scr[:, :, HD, :].rearrange("s j n -> (s j) n")).then_inc(den_ld, 16)
            sp.wait_ge(den_inv, 1)
            sp.dma_start(inv_scr, den).then_inc(inv_st, 16)
            sp.wait_ge(inv_st, 16)
            for c in range(NCH):
                b, c4 = c // CPG, c % CPG
                wait(sp, o_mm, c - 1)
                for g in range(KV_HEADS):
                    s = (b * KV_HEADS + g) * CPG + c4
                    row = g % 2 * 64
                    sp.dma_start(a_in[row:row + 64, c % 2, g // 2, :], o_scr[s, :, 0:HD, :]).then_inc(o_ld[c % 2], 16)
                    sp.dma_start(a_inv[row:row + 64, c % 2, g // 2, :],
                                 inv_scr[s * GROUP:(s + 1) * GROUP, :].rearrange("j (a n) -> j a n", a=1)
                                 .broadcast_to((GROUP, HD, CH))).then_inc(o_ld[c % 2], 16)

            for c in range(NCH):
                sp.wait_ge(y_eva, c + 1)
                sp.wait_ge(y_evd, c + 1)
                sp.dma_start(yr[c], x_row[:, c % 2]).then_inc(y_st[c % 2], 16)
            for p in range(2):
                sp.wait_ge(y_st[p], 16 * NCH // 2)

        @block.tensor
        def _(pe):
            mm = pe.matmul

            def layer_norm(k, ready):
                for c in range(NCH + 1):
                    if c < NCH:
                        ready(c)
                        wait(pe, ln_cent, k * NCH + c - 1)
                        for kt in range(KT):
                            m = mm(ps[:, 4 + c % 2, :], ones[:], XT[:, kt, ch(c)], start=kt == 0, stop=kt == KT - 1)
                        m.then_inc(ln_mean, 1)
                    if c >= 1:
                        v = c - 1
                        pe.wait_ge(ln_sq, k * NCH + v + 1)
                        wait(pe, ln_std, k * NCH + v - 1)
                        for kt in range(KT):
                            m = mm(ps[:, 6 + v % 2, :], ones[:], sq[:, v % 2, kt, :], start=kt == 0, stop=kt == KT - 1)
                        m.then_inc(ln_var, 1)

            pe.wait_ge(w_ld, 16 * len(weights))
            for c in range(NCH):
                pe.wait_ge(x_ld[c % 2], 16 * (c // 2 + 1))
                wait(pe, x_eva, c - 1)
                wait(pe, x_evd, c - 1)
                for kt in range(KT):
                    for t in range(4):
                        m = pe.transpose(ps[:, 2 * (c % 2) + kt, t * P:(t + 1) * P],
                                         x_row[:, c % 2, t, kt * P:(kt + 1) * P], ident[:])
                m.then_inc(x_tr, 1)
            pe.wait_ge(consts, 5)

            def x_ready(c):
                pe.wait_ge(x_eva, c + 1)
                pe.wait_ge(x_evd, c + 1)
            layer_norm(0, x_ready)

            pe.wait_ge(ln_std, NCH)
            pe.wait_ge(ln_cent, NCH)
            for c in range(NCH):
                o = 4 * (c % 2)
                pe.wait_ge(ln_out, c + 1)
                wait(pe, p_act, c - 1)
                wait(pe, p_val, c - 1)
                for n in range(3):
                    for kt in range(KT):
                        w = wq_s[:, kt, n * P:(n + 1) * P] if n < KT else wkk_s[:, kt, :]
                        mm(ps[:, o + n, :], w, YT[:, kt, ch(c)], start=kt == 0, stop=kt == KT - 1)
                for t in range(4):
                    for kt in range(KT):
                        tok = c * CH + t * P
                        m = mm(ps[:, o + 3, t * KVD:(t + 1) * KVD], YT[:, kt, tok:tok + P], wv_s[:, kt, :],
                               start=kt == 0, stop=kt == KT - 1)
                m.then_inc(p_mm, 1)

            pe.wait_ge(p_act, NCH)
            pe.wait_ge(p_val, NCH)

            def max_mm(i, p, n):
                s, u, half = 2 * i + p, n // 2, n % 2
                j, qt, hk = u // 8, u // 2 % 4, u % 2
                if n == 0:
                    pe.wait_ge(qa_ld[p], LOADED * (i + 1))
                if n == 2:
                    wait(pe, nm_lo, s)
                if half == 0:
                    wait(pe, a_max, MAXU * s + u - 1)
                m = mm(ps[:, 2 * (u % 2) + half, :], qa[0:ROWS, p, j, qt * P:(qt + 1) * P],
                       ka[0:ROWS, p, (2 * hk + half) * CH:(2 * hk + half + 1) * CH], start=True, stop=True)
                if half == 1:
                    m.then_inc(a_mm, 1)

            def max_transpose(s):
                pe.wait_ge(a_fin, s + 1)
                pe.transpose(ps[0:MAXU // 2, 2, 0:P], mxq[:], ident[:]).then_inc(a_tr, 1)

            def step(i, p, ahead):
                s = 2 * i + p

                def sums(t):
                    pe.wait_ge(exp_ok, UNITS * s + GROUP * (t + 1))
                    if t == 0:
                        pe.wait_ge(v_st, s + 1)
                        wait(pe, o_ev, s)
                    for j in range(GROUP):
                        m = mm(ps[32 * j:32 * j + 32, 7, :], vst[:, p, t, :], prob[:, (GROUP * t + j) % 8, :],
                               start=t == 0, stop=t == KTILES - 1)
                    m.then_inc(pv_mm, 1)

                def maxima(k):
                    n = k + AHEAD
                    if n < MAXMM and ahead >= 1:
                        max_mm(i + p, 1 - p, n)
                    if n >= MAXMM and ahead >= 2:
                        max_mm(i + 1, p, n - MAXMM)

                pe.wait_ge(qb_ld[p], LOADED * (i + 1))
                pe.wait_ge(m_ld, 32 * (s + 1))
                for t in range(KTILES):
                    for j in range(GROUP):
                        u = GROUP * t + j
                        wait(pe, exp_ok, UNITS * s + u - 2)
                        mm(ps[:, 4 + u % 3, :], kb[0:ROWS_M, p, t * P:(t + 1) * P], qb[0:ROWS_M, p, j, :],
                           start=True, stop=True).then_inc(qk_mm, 1)
                        if u == MAXMM - AHEAD + TURN and ahead >= 1:
                            max_transpose(s + 1)
                        maxima(u)
                    if t >= 1:
                        sums(t - 1)
                sums(KTILES - 1)

            for n in range(MAXMM):
                max_mm(0, 0, n)
            max_transpose(0)
            for n in range(AHEAD):
                max_mm(0, 1, n)
            pe.wait_ge(kb_ones, 2)
            step(0, 0, 2)
            step(0, 1, 2)
            with pe.Fori(1, STEPS // 2 - 1) as i:
                step(i, 0, 2)
                step(i, 1, 2)
            step(STEPS // 2 - 1, 0, 1)
            step(STEPS // 2 - 1, 1, 0)

            pe.wait_ge(nm_lo, STEPS)
            for c in range(NCH):
                pe.wait_ge(o_norm, c + 1)
                wait(pe, o_res, c - 1)
                for mt in range(KT):
                    for kt in range(KT):
                        m = mm(ps[:, 2 * (c % 2) + mt, :], wo_s[:, kt, mt * P:(mt + 1) * P], a_in[:, c % 2, kt, :],
                               start=kt == 0, stop=kt == KT - 1)
                m.then_inc(o_mm, 1)
            pe.wait_ge(exp_ok, UNITS * STEPS)
            pe.wait_ge(o_ev, STEPS)
            layer_norm(1, lambda c: pe.wait_ge(o_res, c + 1))

            def feed_forward(k):
                base = k * FN
                pe.wait_ge(f_sum, k + 1)
                for kt in range(KT):
                    m = mm(ps[:, 0, 0:BATCH], e1_s[:, kt, :], gm[:, kt, :], start=kt == 0, stop=kt == KT - 1)
                m.then_inc(f_g, 1)
                pe.wait_ge(f_ga, 3 * k + 1)
                mm(ps[0:64, 1, 0:BATCH], e2_s[:], gh1[:], start=True, stop=True).then_inc(f_g, 1)
                pe.wait_ge(f_ga, 3 * k + 2)
                mm(ps[:, 2, 0:BATCH], e3_s[:], gh2[0:64, :], start=True, stop=True).then_inc(f_g, 1)
                pe.wait_ge(f_ga, 3 * k + 3)

                def layers(n, c, has):
                    if has(0):
                        if has(-NCH):
                            pe.wait_ge(f_up, base + n - NCH + 1)
                        if has(-1):
                            pe.wait_ge(f_a1, base + n)
                        for mt in range(KT):
                            for kt in range(KT):
                                m = mm(ps[:, mt, :], c1_s[:, kt, mt * P:(mt + 1) * P], YT[:, kt, ch(c)],
                                       start=kt == 0, stop=kt == KT - 1)
                        m.then_inc(f_h1, 1)
                    if has(-1):
                        pe.wait_ge(f_a1, base + n)
                        if has(-2):
                            pe.wait_ge(f_a2, base + n - 1)
                        for kt in range(KT):
                            m = mm(ps[:, 2, :], c2_s[:, kt, :], h1[:, (c - 1) % 2, kt, :], start=kt == 0, stop=kt == KT - 1)
                        m.then_inc(f_h2, 1)
                    if has(-2):
                        pe.wait_ge(f_a2, base + n - 1)
                        if has(-3):
                            pe.wait_ge(f_a3, base + n - 2)
                        mm(ps[0:64, 3, :], c3_s[:], h2[:, (c - 2) % 2, :], start=True, stop=True).then_inc(f_h3, 1)
                    if has(-3):
                        pe.wait_ge(f_a3, base + n - 2)
                        if has(-4):
                            pe.wait_ge(f_th, base + n - 3)
                        mm(ps[:, 4, :], c4_s[0:64, :], h3[0:64, (c - 3) % 2, :], start=True, stop=True).then_inc(f_z, 1)

                for n in range(NCH):
                    layers(n, n, lambda d: n + d >= 0)
                with pe.Fori(1, CYCLES) as cy:
                    for c in range(NCH):
                        layers(cy * NCH + c, c, lambda d: True)
                for n in range(FN, FN + LAG):
                    layers(n, n % NCH, lambda d: n + d < FN)

            pe.wait_ge(ln_std, 2 * NCH)
            pe.wait_ge(ln_cent, 2 * NCH)
            feed_forward(0)
            pe.wait_ge(f_th, FN)
            layer_norm(2, lambda c: pe.wait_ge(f_out, c + 1))

            pe.wait_ge(ln_std, 3 * NCH)
            pe.wait_ge(ln_cent, 3 * NCH)
            for c in range(NCH):
                pe.wait_ge(ln_out, 2 * NCH + c + 1)
                wait(pe, l_hg, c - 1)
                for kt in range(KT):
                    m = mm(ps[0:HD, c % 2, :], g1_s[:, kt, :], YT[:, kt, ch(c)], start=kt == 0, stop=kt == KT - 1)
                m.then_inc(l_hm, 1)
            pe.wait_ge(l_hg, NCH)

            def project_qk(n, p):
                pe.wait_ge(l_ys, n + 1)
                wait(pe, l_silu, n)
                for kt in range(KT):
                    m = mm(ps[:, 0, :], y_st8[:, p, kt, :], lqk_s[:, kt, :], start=kt == 0, stop=kt == KT - 1)
                m.then_inc(l_qk, 1)

            def project_vg(n, p):
                wait(pe, l_v, n)
                wait(pe, l_gate, n)
                for kt in range(KT):
                    mm(ps[:, 1, 0:DIM], y_st8[:, p, kt, :], lv_s[:, kt, :], start=kt == 0, stop=kt == KT - 1)
                mm(ps[:, 1, DIM:2 * DIM], hg_tile[:, p, :], g2_s[:], start=True, stop=True).then_inc(l_vg, 1)

            def turn(n, p):
                pe.wait_ge(l_rope, n + 1)
                wait(pe, l_kt, n)
                wait(pe, l_qt, n)
                wait(pe, l_qx, n)
                wait(pe, l_ye, n - 2)
                for i in range(2 * KT):
                    m = pe.transpose(ps[:, 2, i * P:(i + 1) * P], qk_r[:, p, i * P:(i + 1) * P], ident[:])
                m.then_inc(l_t, 1)

            def energy(n, p, quarter):
                kt, half = quarter // 2, quarter % 2
                if quarter == 0:
                    pe.wait_ge(l_kt, n + 1)
                    pe.wait_ge(l_qx, n + 1)
                wait(pe, l_em, 4 * n + quarter - 1)
                mm(ps[:, 3 + half, :], k_t[:, p, kt, :], q_x[:, kt, 4 * half:4 * half + 4, :],
                   start=True, stop=True).then_inc(l_e, 1)

            def attend(n, p, first):
                pe.wait_ge(l_qt, n + 1)
                pe.wait_ge(l_sx, n + 1)
                pe.wait_ge(l_v, n + 1)
                wait(pe, l_oe, n)
                for g in range(4):
                    mm(ps[:, 6, g * P:(g + 1) * P], s_x[:, 4 * g:4 * g + 4, :], q_t[:, p, g // 2, :],
                       start=g == 0, stop=False, skip_group_check=True)
                pe.wait_ge(l_em, 4 * (n + 1))
                for g in range(4):
                    for j in range(4):
                        h = 4 * g + j
                        m = mm(ps[32 * j:32 * j + HD, 6, g * P:(g + 1) * P], v_r[:, p, h * HD:(h + 1) * HD], e_m[:, h, :],
                               start=False, stop=g == 3, skip_group_check=True)
                m.then_inc(l_o, 1)
                for kt in range(KT):
                    m = mm(ps[:, 5, kt * P:(kt + 1) * P], qk_r[:, p, DIM + kt * P:DIM + (kt + 1) * P],
                           v_r[:, p, kt * P:(kt + 1) * P], start=first and kt == 0, stop=kt == KT - 1, skip_group_check=True)
                m.then_inc(l_s, 1)

            def rows(n):
                pe.wait_ge(l_oe, n + 1)
                wait(pe, l_x, n - 1)
                for g in range(4):
                    m = pe.transpose(ps[:, 7, g * P:(g + 1) * P], o_t[:, g * P:(g + 1) * P], ident[:])
                m.then_inc(l_ot, 1)

            def norm_turn(n, p):
                pe.wait_ge(l_n, n + 1)
                turns = min(n + 3, TILES) if isinstance(n, int) else n + 3
                pe.wait_ge(l_kt, turns)
                pe.wait_ge(l_qt, turns)
                pe.wait_ge(l_qx, turns)
                for kt in range(KT):
                    m = pe.transpose(ps[:, 2, kt * P:(kt + 1) * P], o_n[:, p, kt * P:(kt + 1) * P], ident[:])
                m.then_inc(l_y, 1)

            def out_proj(n, p):
                pe.wait_ge(l_ye, n + 1)
                pe.wait_ge(l_r, min(n + 2, TILES) if isinstance(n, int) else n + 2)
                wait(pe, l_x, n)
                for mt in range(KT):
                    for kt in range(KT):
                        m = mm(ps[:, 7, mt * P:(mt + 1) * P], lo_s[:, kt, mt * P:(mt + 1) * P], on_t[:, p, kt, :],
                               start=kt == 0, stop=kt == KT - 1)
                m.then_inc(l_w, 1)

            def pipeline(n, p, place):
                if is_tile(n):
                    energy(n, p, 0)
                    energy(n, p, 1)
                if is_tile(n - 1):
                    rows(n - 1)
                if is_tile(n):
                    energy(n, p, 2)
                    energy(n, p, 3)
                if is_tile(n + 2):
                    project_qk(n + 2, p)
                if is_tile(n + 1):
                    turn(n + 1, 1 - p)
                    project_vg(n + 1, 1 - p)
                if is_tile(n):
                    attend(n, p, isinstance(n, int) and n % TPB == 0)
                if is_tile(n - 2):
                    out_proj(n - 2, p)
                if is_tile(n - 1):
                    norm_turn(n - 1, 1 - p)

            project_qk(0, 0)
            project_qk(1, 1)
            turn(0, 0)
            project_vg(0, 0)
            through_tiles(pe, pipeline)

            pe.wait_ge(l_em, 4 * TILES)
            pe.wait_ge(l_oe, TILES)
            pe.wait_ge(l_x, TILES)
            layer_norm(3, lambda c: pe.wait_ge(l_x, 4 * (c + 1)))
            pe.wait_ge(ln_std, 4 * NCH)
            pe.wait_ge(ln_cent, 4 * NCH)
            feed_forward(1)

            pe.wait_ge(f_th, 2 * FN)
            for c in range(NCH):
                pe.wait_ge(f_out, NCH + c + 1)
                wait(pe, y_eva, c - 1)
                wait(pe, y_evd, c - 1)
                for t in range(4):
                    for kt in range(KT):
                        tok = c * CH + t * P
                        m = pe.transpose(ps[:, 2 * (c % 2) + t // 2, (t % 2) * DIM + kt * P:(t % 2) * DIM + (kt + 1) * P],
                                         XT[:, kt, tok:tok + P], ident[:])
                m.then_inc(y_tr, 1)

        @block.scalar
        def _(act):
            fn = act.activation
            act.wait_ge(w_ld, 16 * len(weights))
            for c in range(NCH):
                act.wait_ge(x_tr, c + 1)
                act.copy(XT[:, 0, ch(c)], ps[:, 2 * (c % 2), :]).then_inc(x_eva, 1)

            def layer_norm(k):
                for c in range(NCH + 1):
                    if c < NCH:
                        act.wait_ge(ln_cent, k * NCH + c + 1)
                        wait(act, ln_var, k * NCH + c - 1)
                        fn(sq[:, c % 2], YT[:, :, ch(c)], ACT.Square).then_inc(ln_sq, 1)
                    if c >= 1:
                        v = c - 1
                        act.wait_ge(ln_var, k * NCH + v + 1)
                        wait(act, ln_rec, k * NCH + v - 1)
                        fn(std[:, v % 2, :], ps[:, 6 + v % 2, :], ACT.Sqrt, bias=eps[:]).then_inc(ln_std, 1)

            act.wait_ge(consts, 5)
            layer_norm(0)

            for c in range(NCH):
                o, p = 4 * (c % 2), c % 2
                act.wait_ge(p_mm, c + 1)
                wait(act, p_low, c - 1)
                wait(act, p_st[p], 16 * 15 * (c // 2))
                for n in range(3):
                    b = bias[:, BQ + n:BQ + n + 1]
                    fn(qkf[:, p, n, :], ps[:, o + n, :], ACT.Identity, bias=b)
                    m = fn(part[:, p, 0, n, :], ps[:, o + n, :], ACT.Identity, bias=b)
                m.then_inc(p_act, 1)

            def step(i, p):
                s = 2 * i + p
                for t in range(KTILES):
                    for j in range(GROUP):
                        u = GROUP * t + j
                        act.wait_ge(qk_mm, UNITS * s + u + 1)
                        if j == 0:
                            wait(act, pv_mm, KTILES * s + t - 1)
                        fn(prob[:, u % 8, :], ps[:, 4 + u % 3, :], ACT.Exp, scale=HD ** -0.5).then_inc(exp_ok, 1)
                act.wait_ge(pv_mm, KTILES * (s + 1))
                wait(act, o_st[p], 16 * i)
                act.copy(o_sb[:, p, :], ps[:, 7, :]).then_inc(o_ev, 1)

            step(0, 0)
            step(0, 1)
            with act.Fori(1, STEPS // 2) as i:
                step(i, 0)
                step(i, 1)

            layer_norm(1)

            def feed_forward(k):
                base = k * FN
                act.wait_ge(f_g, 3 * k + 1)
                fn(gh1[:], ps[:, 0, 0:BATCH], ACT.Gelu, bias=bias[:, F1:F1 + 1], scale=1.0 / SEQ).then_inc(f_ga, 1)
                act.wait_ge(f_g, 3 * k + 2)
                fn(gh2[0:64, :], ps[0:64, 1, 0:BATCH], ACT.Gelu, bias=bias[0:64, F2:F2 + 1]).then_inc(f_ga, 1)
                act.wait_ge(f_g, 3 * k + 3)
                fn(gth[:], ps[:, 2, 0:BATCH], ACT.Tanh, bias=half_b[:, 1:2], scale=0.5).then_inc(f_ga, 1)

                def layers(n, c, has):
                    if has(0):
                        act.wait_ge(f_h1, base + n + 1)
                        if has(-2):
                            act.wait_ge(f_h2, base + n - 1)
                        for mt in range(KT):
                            m = fn(h1[:, c % 2, mt, :], ps[:, mt, :], ACT.Gelu, bias=bias[:, D1 + mt:D1 + mt + 1])
                        m.then_inc(f_a1, 1)
                    if has(-1):
                        act.wait_ge(f_h2, base + n)
                        if has(-3):
                            act.wait_ge(f_h3, base + n - 2)
                        fn(h2[:, (c - 1) % 2, :], ps[:, 2, :], ACT.Gelu, bias=bias[:, D2:D2 + 1]).then_inc(f_a2, 1)
                    if has(-2):
                        act.wait_ge(f_h3, base + n - 1)
                        if has(-4):
                            act.wait_ge(f_z, base + n - 3)
                        fn(h3[0:64, (c - 2) % 2, :], ps[0:64, 3, :], ACT.Gelu, bias=bias[0:64, D3:D3 + 1]).then_inc(f_a3, 1)
                    if has(-3):
                        act.wait_ge(f_z, base + n - 2)
                        if has(-5):
                            act.wait_ge(f_cs, base + n - 4)
                        fn(th[:, (c - 3) % 2, :], ps[:, 4, :], ACT.Tanh, bias=half_b[:, 0:1], scale=0.5).then_inc(f_th, 1)

                for n in range(NCH):
                    layers(n, n, lambda d: n + d >= 0)
                with act.Fori(1, CYCLES) as cy:
                    for c in range(NCH):
                        layers(cy * NCH + c, c, lambda d: True)
                for n in range(FN, FN + LAG):
                    layers(n, n % NCH, lambda d: n + d < FN)

            feed_forward(0)
            layer_norm(2)

            for c in range(NCH):
                act.wait_ge(l_hm, c + 1)
                act.copy(h_g[:, ch(c)], ps[0:HD, c % 2, :]).then_inc(l_hg, 1)

            def queries_keys(n, p):
                act.wait_ge(l_qk, n + 1)
                wait(act, l_rope, n - 1)
                fn(qk_a[:, p, :], ps[:, 0, :], ACT.Silu).then_inc(l_silu, 1)

            def values_gate(n, p):
                act.wait_ge(l_vg, n + 1)
                wait(act, l_s, n - 1)
                fn(v_r[:, p, :], ps[:, 1, 0:DIM], ACT.Copy, scale=0.5).then_inc(l_v, 1)
                wait(act, l_r, n - 1)
                fn(gate[:, p, :], ps[:, 1, DIM:2 * DIM], ACT.Tanh, scale=0.5).then_inc(l_gate, 1)

            def turned(n, p):
                act.wait_ge(l_t, n + 1)
                act.wait_ge(l_qx, n + 1)
                wait(act, l_e, 4 * (n - 1))
                act.copy(k_t[:, p].rearrange("p a b -> p (a b)"), ps[:, 2, KT * P:2 * KT * P]).then_inc(l_kt, 1)
                wait(act, l_o, n - 1)
                act.copy(q_t[:, p].rearrange("p a b -> p (a b)"), ps[:, 2, 0:KT * P]).then_inc(l_qt, 1)

            def affine(n, p):
                act.wait_ge(l_y, n + 1)
                wait(act, l_w, n - 1)
                for kt in range(KT):
                    m = fn(on_t[:, p, kt, :], ps[:, 2, kt * P:(kt + 1) * P], ACT.Identity,
                           bias=bias[:, LB + kt:LB + kt + 1], scale=bias[:, LW + kt:LW + kt + 1])
                m.then_inc(l_ye, 1)

            def pipeline(n, p, place):
                if is_tile(n + 2):
                    queries_keys(n + 2, p)
                if is_tile(n + 1):
                    turned(n + 1, 1 - p)
                    values_gate(n + 1, 1 - p)
                if is_tile(n):
                    act.wait_ge(l_o, n + 1)
                    wait(act, l_ot, n)
                    act.copy(o_t, ps[:, 6, :]).then_inc(l_oe, 1)
                if is_tile(n - 1):
                    affine(n - 1, 1 - p)

            queries_keys(0, 0)
            queries_keys(1, 1)
            turned(0, 0)
            values_gate(0, 0)
            through_tiles(act, pipeline)

            layer_norm(3)
            feed_forward(1)
            for c in range(NCH):
                act.wait_ge(y_tr, c + 1)
                wait(act, y_st[c % 2], 16 * (c // 2))
                act.copy(x_row[:, c % 2, 0:2].rearrange("p a b -> p (a b)"), ps[:, 2 * (c % 2), :]).then_inc(y_eva, 1)

        @block.vector
        def _(dve):
            dve.memset(ones[:], 1.0 / DIM).then_inc(consts, 1)
            dve.memset(eps[:], EPS).then_inc(consts, 1)
            dve.memset(mhalf[:], -0.5).then_inc(consts, 1)
            dve.memset(vals[:, :, :, HD:32], 1.0).then_inc(v_ones, 1)
            dve.wait_ge(w_ld, 16 * len(weights))
            dve.tensor_copy(c4_s[:], last_c[:, 0:1].broadcast_to((64, P))).then_inc(consts, 1)
            dve.tensor_copy(e3_s[:], last_c[:, 1:2].broadcast_to((64, P))).then_inc(consts, 1)
            dve.tensor_scalar(half_b[:, 0:1], bias[:, D4:D4 + 1], 0.5, None, ALU.mult)
            dve.tensor_scalar(half_b[:, 1:2], bias[:, F3:F3 + 1], 0.5, None, ALU.mult)
            dve.tensor_tensor(coup[:, 0:1], bias[:, AR:AR + 1], bias[:, SG:SG + 1], ALU.mult).then_inc(c_dve, 1)
            dve.wait_ge(c_dve, 1)
            dve.tensor_scalar(coup[:, 1:2], coup[:, 0:1], 0.3, None, ALU.mult)
            dve.tensor_scalar(coup[:, 2:3], bias[:, SG:SG + 1], 0.1, None, ALU.mult)
            dve.tensor_scalar(coup[:, 3:4], coup[:, 0:1], 0.7, None, ALU.mult).then_inc(c_dve, 1)
            for c in range(NCH):
                dve.wait_ge(x_tr, c + 1)
                dve.tensor_copy(XT[:, 1, ch(c)], ps[:, 2 * (c % 2) + 1, :]).then_inc(x_evd, 1)

            def layer_norm(k):
                for c in range(NCH + 1):
                    if c < NCH:
                        dve.wait_ge(ln_mean, k * NCH + c + 1)
                        dve.tensor_tensor(YT[:, :, ch(c)], XT[:, :, ch(c)],
                                          ps[:, 4 + c % 2:5 + c % 2, :].broadcast_to((P, KT, CH)),
                                          ALU.subtract).then_inc(ln_cent, 1)
                    if c >= 1:
                        v = c - 1
                        dve.wait_ge(ln_std, k * NCH + v + 1)
                        dve.reciprocal(rec[:, v % 2, :], std[:, v % 2, :]).then_inc(ln_rec, 1)
                        dve.wait_ge(ln_rec, k * NCH + v + 1)
                        dve.tensor_tensor(YT[:, :, ch(v)], YT[:, :, ch(v)],
                                          rec[:, v % 2:v % 2 + 1, :].broadcast_to((P, KT, CH)),
                                          ALU.mult).then_inc(ln_out, 1)

            dve.wait_ge(x_eva, NCH)
            dve.wait_ge(x_evd, NCH)
            layer_norm(0)

            dve.wait_ge(v_ones, 1)
            for c in range(NCH):
                p, b = c % 2, c // CPG
                dve.wait_ge(p_act, c + 1)
                wait(dve, p_st[p], 16 * 15 * (c // 2))
                dve.tensor_tensor(res[:, p], qkf[:, p], part[:, p, 0], ALU.subtract).then_inc(p_res, 1)
                dve.tensor_tensor(vals[:, b * KV_HEADS:(b + 1) * KV_HEADS, 4 * (c % CPG):4 * (c % CPG) + 4, 0:HD]
                                  .rearrange("p g t d -> p t g d"),
                                  ps[:, 4 * (c % 2) + 3, 0:4 * KVD].rearrange("p (t g d) -> p t g d", t=4, g=KV_HEADS),
                                  bv_s[:].rearrange("p (a g d) -> p a g d", a=1, g=KV_HEADS).broadcast_to((P, 4, KV_HEADS, HD)),
                                  ALU.add).then_inc(p_val, 1)
                dve.wait_ge(p_res, c + 1)
                dve.tensor_copy(part[:, p, 1], res[:, p]).then_inc(p_mid, 1)
                dve.wait_ge(p_mid, c + 1)
                dve.tensor_tensor(part[:, p, 2], res[:, p], part[:, p, 1], ALU.subtract).then_inc(p_low, 1)

            for p in range(2):
                dve.wait_ge(p_st[p], 16 * 15 * NCH // 2)
            for p in range(2):
                dve.memset(kb[ROWS:ROWS_M, p, :], 1.0).then_inc(kb_ones, 1)

            def maxima(s):
                for u in range(MAXU):
                    dve.wait_ge(a_mm, MAXU * s + u + 1)
                    b = 2 * (u % 2)
                    dve.tensor_reduce(mx[:, u:u + 1], ps[:, b:b + 2, :], mybir.AxisListType.XY, ALU.max).then_inc(a_max, 1)
                dve.wait_ge(a_max, MAXU * (s + 1))
                halves = mx[:].rearrange("p (a b) -> p a b", b=2)
                dve.tensor_tensor(mxq[:], halves[:, :, 0], halves[:, :, 1], ALU.max).then_inc(a_fin, 1)
                dve.wait_ge(a_tr, s + 1)
                wait(dve, m_ld, 32 * s)
                turned = ps[0:MAXU // 2, 2, 0:P]
                dve.tensor_scalar(negm[:, 0, :], turned, -1.0, None, ALU.mult).then_inc(nm_hi, 1)
                dve.wait_ge(nm_hi, s + 1)
                dve.scalar_tensor_tensor(out=negm[:, 1, :], in0=turned, scalar=-1.0, in1=negm[:, 0, :],
                                         op0=ALU.mult, op1=ALU.subtract).then_inc(nm_lo, 1)

            maxima(0)
            with dve.Fori(1, STEPS) as s:
                maxima(s)

            dve.wait_ge(den_ld, 16)
            dve.reciprocal(den, den).then_inc(den_inv, 1)
            for c in range(NCH):
                dve.wait_ge(o_ld[c % 2], 128 * (c // 2 + 1))
                dve.tensor_tensor(a_in[:, c % 2], a_in[:, c % 2], a_inv[:, c % 2], ALU.mult).then_inc(o_norm, 1)
                if c >= 1:
                    v = c - 1
                    dve.wait_ge(o_mm, v + 1)
                    for kt in range(KT):
                        m = dve.scalar_tensor_tensor(out=XT[:, kt, ch(v)], in0=ps[:, 2 * (v % 2) + kt, :],
                                                     scalar=bias[:, BO + kt:BO + kt + 1], in1=XT[:, kt, ch(v)],
                                                     op0=ALU.add, op1=ALU.add)
                    m.then_inc(o_res, 1)
            dve.wait_ge(o_mm, NCH)
            for kt in range(KT):
                m = dve.scalar_tensor_tensor(out=XT[:, kt, ch(NCH - 1)], in0=ps[:, 2 * ((NCH - 1) % 2) + kt, :],
                                             scalar=bias[:, BO + kt:BO + kt + 1], in1=XT[:, kt, ch(NCH - 1)],
                                             op0=ALU.add, op1=ALU.add)
            m.then_inc(o_res, 1)
            dve.wait_ge(o_res, NCH)
            layer_norm(1)

            def feed_forward(k):
                base = k * FN
                dve.wait_ge(ln_out, (2 * k + 2) * NCH)
                dve.tensor_reduce(gm[:], YT[:].rearrange("p k (b n) -> p k b n", b=BATCH), AX_X, ALU.add).then_inc(f_sum, 1)
                dve.wait_ge(f_ga, 3 * k + 3)
                dve.tensor_scalar(cb[:], gth[:], coup[:, 3:4], coup[:, 2:3], ALU.mult, ALU.add).then_inc(f_cb, 1)
                dve.wait_ge(f_cb, k + 1)

                def update(n, c):
                    p, b = c % 2, c // CPG
                    dve.wait_ge(f_th, base + n + 1)
                    dve.tensor_scalar(cs[:, p, :], th[:, p, :], coup[:, 1:2], cb[:, b:b + 1], ALU.mult, ALU.add).then_inc(f_cs, 1)
                    dve.wait_ge(f_cs, base + n + 1)
                    dve.tensor_tensor(tw[:, p, 0, :], cs[:, p, :], YT[:, 1, ch(c)], ALU.mult)
                    dve.tensor_tensor(tw[:, p, 1, :], cs[:, p, :], YT[:, 0, ch(c)], ALU.mult).then_inc(f_tw, 1)
                    dve.wait_ge(f_tw, base + n + 1)
                    dve.tensor_tensor(YT[:, 0, ch(c)], YT[:, 0, ch(c)], tw[:, p, 0, :], ALU.add)
                    dve.tensor_tensor(YT[:, 1, ch(c)], YT[:, 1, ch(c)], tw[:, p, 1, :], ALU.subtract).then_inc(f_up, 1)

                with dve.Fori(0, CYCLES) as cy:
                    for c in range(NCH):
                        update(cy * NCH + c, c)
                for c in range(NCH):
                    dve.wait_ge(f_up, base + FN - NCH + c + 1)
                    dve.tensor_tensor(XT[:, :, ch(c)], XT[:, :, ch(c)], YT[:, :, ch(c)], ALU.add).then_inc(f_out, 1)

            feed_forward(0)
            dve.wait_ge(f_out, NCH)
            layer_norm(2)

            def halves(ap):
                v = ap.rearrange("p (h a e) -> p h a e", a=2, e=HD // 2)
                return v[:, :, 0, :], v[:, :, 1, :]

            def rope(n, p, t):
                dve.wait_ge(l_silu, n + 1)
                wait(dve, l_s, n - 1)
                wait(dve, l_t, n - 1)
                wait(dve, l_rope, n)
                a, b = halves(qk_a[:, p, :])
                ra, rb = halves(qk_r[:, p, :])
                co = cos_s[:, bass.ds(t, 1), :].broadcast_to((P, 2 * HEADS, HD // 2))
                si = sin_s[:, bass.ds(t, 1), :].broadcast_to((P, 2 * HEADS, HD // 2))
                for i, (u, v) in enumerate(((a, co), (b, si), (b, co), (a, si))):
                    m = dve.tensor_tensor(rt[:, i], u, v, ALU.mult)
                m.then_inc(l_rt, 1)
                dve.wait_ge(l_rt, n + 1)
                dve.tensor_tensor(ra, rt[:, 0], rt[:, 1], ALU.subtract)
                dve.tensor_tensor(rb, rt[:, 2], rt[:, 3], ALU.add).then_inc(l_rope, 1)

            def spread(n, p):
                dve.wait_ge(l_t, n + 1)
                wait(dve, l_e, 4 * n)
                for kt in range(KT):
                    m = dve.tensor_tensor(q_x[:, kt], ps[:, 2, kt * P:(kt + 1) * P].rearrange("p (a n) -> p a n", a=1)
                                          .broadcast_to((P, HPK, P)),
                                          head[:].rearrange("p (h a) -> p h a", a=1).broadcast_to((P, HPK, P)), ALU.mult)
                m.then_inc(l_qx, 1)

            def mask(n, quarter):
                dve.wait_ge(l_e, 4 * n + quarter + 1)
                if quarter == 0:
                    wait(dve, l_o, n)
                dve.tensor_tensor(e_m[:, 4 * quarter:4 * quarter + 4, :],
                                  ps[:, 3 + quarter % 2, :].rearrange("p (h n) -> p h n", h=4),
                                  causal[:].rearrange("p (a n) -> p a n", a=1).broadcast_to((P, 4, P)),
                                  ALU.mult).then_inc(l_em, 1)

            def state(n, reset):
                dve.wait_ge(l_s, n + 1)
                dve.wait_ge(l_o, n + 1)
                if reset:
                    dve.memset(s_x[:, :, 0:HD], 0.0).then_inc(l_sx, 1)
                else:
                    dve.tensor_tensor(s_x[:, :, 0:HD], ps[:, 5, 0:DIM].rearrange("p (h d) -> p h d", h=HEADS),
                                      diag[:], ALU.mult).then_inc(l_sx, 1)

            def gated(n, p):
                dve.wait_ge(l_gate, n + 1)
                dve.wait_ge(l_ot, n + 1)
                dve.scalar_tensor_tensor(out=o_r[:, p, :].rearrange("p (h d) -> p h d", h=HEADS),
                                         in0=gate[:, p, :].rearrange("p (h d) -> p h d", h=HEADS), scalar=1.0,
                                         in1=ps[:, 7, :].rearrange("p (h r) -> p h r", r=32)[:, :, 0:HD],
                                         op0=ALU.add, op1=ALU.mult).then_inc(l_r, 1)
                dve.wait_ge(l_r, n + 1)
                dve.bn_stats(stats[:], o_r[:, p, :]).then_inc(l_bn, 1)

            def variance(n, p):
                dve.bn_aggr(mv[:, p, :], stats[:]).then_inc(l_mv, 1)
                dve.wait_ge(l_mv, n + 1)
                dve.tensor_scalar(var_e[:, p:p + 1], mv[:, p, 1:2], EPS, None, ALU.add).then_inc(l_ve, 1)

            def normalise(n, p):
                wait(dve, l_y, n - 1)
                dve.wait_ge(l_rs, n + 1)
                dve.tensor_scalar(o_n[:, p, :], o_r[:, p, :], mv[:, p, 0:1], rstd[:, p:p + 1],
                                  ALU.subtract, ALU.mult).then_inc(l_n, 1)

            def residual(n):
                dve.wait_ge(l_w, n + 1)
                dve.tensor_tensor(XT[:, :, bass.ds(n * P, P)], XT[:, :, bass.ds(n * P, P)],
                                  ps[:, 7, 0:DIM].rearrange("p (k n) -> p k n", k=KT), ALU.add).then_inc(l_x, 1)

            def pipeline(n, p, place):
                if is_tile(n):
                    for quarter in range(4):
                        mask(n, quarter)
                if is_tile(n - 1):
                    gated(n - 1, 1 - p)
                    dve.wait_ge(l_bn, n)
                if is_tile(n + 1):
                    spread(n + 1, 1 - p)
                if is_tile(n - 1):
                    variance(n - 1, 1 - p)
                if is_tile(n) and is_tile(n + 1):
                    state(n, isinstance(n, int) and n % TPB == TPB - 1)
                if is_tile(n - 1):
                    normalise(n - 1, 1 - p)
                if is_tile(n - 2):
                    residual(n - 2)
                if is_tile(n + 2):
                    rope(n + 2, p, place)

            rope(0, 0, 0)
            rope(1, 1, 1)
            spread(0, 0)
            dve.memset(s_x, 0.0).then_inc(l_sx, 1)
            through_tiles(dve, pipeline)

            dve.wait_ge(l_x, TILES)
            layer_norm(3)
            feed_forward(1)
            for c in range(NCH):
                dve.wait_ge(y_tr, c + 1)
                wait(dve, y_st[c % 2], 16 * (c // 2))
                dve.tensor_copy(x_row[:, c % 2, 2:4].rearrange("p a b -> p (a b)"), ps[:, 2 * (c % 2) + 1, :]).then_inc(y_evd, 1)

        @block.gpsimd
        def _(pool):
            pool.wait_ge(p_val, NCH)
            for p in range(2):
                pool.wait_ge(p_st[p], 16 * 15 * NCH // 2)

            def values(s, p):
                wait(pool, pv_mm, KTILES * (s - 1))
                pool.tensor_copy(vst[:, p].rearrange("p t d -> p (t d)"),
                                 vals[:, s // CPG].rearrange("p t d -> p (t d)")).then_inc(v_st, 1)

            values(0, 0)
            values(1, 1)
            with pool.Fori(1, STEPS // 2) as i:
                values(2 * i, 0)
                values(2 * i + 1, 1)

            pool.wait_ge(ln_out, 3 * NCH)
            pool.wait_ge(l_hg, NCH)

            def columns(n, p):
                wait(pool, l_vg, n - 1)
                pool.tensor_copy(hg_tile[:, p, :], h_g[:, bass.ds(n * P, P)])
                pool.tensor_copy(y_st8[:, p], YT[:, :, bass.ds(n * P, P)]).then_inc(l_ys, 1)

            def root(n, p):
                pool.wait_ge(l_ve, n + 1)
                wait(pool, l_n, n - 1)
                pool.tensor_tensor(rstd[:, p:p + 1], var_e[:, p:p + 1], mhalf[:], ALU.pow).then_inc(l_rs, 1)

            for n in range(3):
                columns(n, n % 2)
            for n in range(2):
                columns(n + 3, 1 - n % 2)
                root(n, n % 2)
            with pool.Fori(1, TILES // 2 - 2) as i:
                columns(2 * i + 3, 1)
                root(2 * i, 0)
                columns(2 * i + 4, 0)
                root(2 * i + 1, 1)
            for n in range(TILES - 4, TILES):
                if is_tile(n + 3):
                    columns(n + 3, 1 - n % 2)
                root(n, n % 2)


_INS = ['L0_attn_a_x', 'L0_attn_a_Wq', 'L0_attn_a_bq', 'L0_attn_a_Wk', 'L0_attn_a_bk', 'L0_attn_a_Wv',
        'L0_attn_a_bv', 'L0_attn_a_Wo', 'L0_attn_a_bo', 'L0_attn_b_Wq', 'L0_attn_b_Wk', 'L0_attn_b_Wv',
        'L0_attn_b_Wo', 'L0_attn_b_Wg1', 'L0_attn_b_Wg2', 'L0_attn_b_ln_w', 'L0_attn_b_ln_b',
        'L0_ffn_cn_w1', 'L0_ffn_cn_b1', 'L0_ffn_cn_w2', 'L0_ffn_cn_b2', 'L0_ffn_cn_w3', 'L0_ffn_cn_b3',
        'L0_ffn_cn_w4', 'L0_ffn_cn_b4', 'L0_ffn_gc_w1', 'L0_ffn_gc_b1', 'L0_ffn_gc_w2', 'L0_ffn_gc_b2',
        'L0_ffn_gc_w3', 'L0_ffn_gc_b3', 'L0_ffn_adaptive_range']


def shape_constants():
    f = np.float32
    inv_freq = (f(1.0) / f(10000.0) ** (np.arange(0, HD, 2, dtype=f) / f(HD))).astype(f)
    ang = (np.arange(SEQ, dtype=f)[:, None] * inv_freq[None, :]).astype(f)
    feature = np.arange(P)[:, None]
    return {
        "ident": np.eye(P, dtype=f), "cos": np.cos(ang).astype(f), "sin": np.sin(ang).astype(f),
        "causal": np.triu(np.ones((P, P), f)),
        "head": (feature // HD == np.arange(HPK)[None, :]).astype(f),
        "diag": (feature // HD == np.arange(DIM)[None, :] // HD % HPK).astype(f),
        "sign": np.where(feature < 64, 1.0, -1.0).astype(f),
    }


def lay_out(inputs):
    a = {n: np.ascontiguousarray(np.asarray(inputs[n])) for n in _INS}
    w = a["L0_attn_a_Wo"].reshape(GROUP, KV_HEADS, HD, DIM)
    a["L0_attn_a_Wo"] = np.ascontiguousarray(w.transpose(1, 0, 2, 3).reshape(DIM, DIM))
    return a


def kernel(**inputs):
    import numpy as _np
    import concourse.bacc as _bacc
    from concourse import mybir as _mybir
    from concourse.bass_utils import run_bass_kernel_spmd as _run

    nc = _bacc.Bacc("TRN2", target_bir_lowering=False, num_devices=1)
    arrays, args = {}, []
    named = {**lay_out(inputs), **shape_constants()}
    for name, a in named.items():
        arrays[f"in_{name}_dram"] = a
        args.append(nc.dram_tensor(f"in_{name}_dram", a.shape, _mybir.dt.from_np(a.dtype), kind="ExternalInput").ap())
    args.append(nc.dram_tensor("out_0_dram", (BATCH, SEQ, DIM), F32, kind="ExternalOutput").ap())
    hybrid_block(nc, *args)
    r = _run(nc, [arrays], core_ids=[0])
    return r.results[0]["out_0_dram"]
```

```python
from contextlib import ExitStack

import numpy as np

import concourse.bass as bass
from concourse import mybir

F32 = mybir.dt.float32
BF16 = mybir.dt.bfloat16
ACT = mybir.ActivationFunctionType
ALU = mybir.AluOpType
AX_X = mybir.AxisListType.X

P = 128
BATCH, SEQ, DIM = 2, 2048, 256
TOKENS = BATCH * SEQ
KT = DIM // P
CH = 512
NCH = TOKENS // CH
HEADS, KV_HEADS, HD = 16, 4, 16
GROUP = HEADS // KV_HEADS
KVD = KV_HEADS * HD
EPS = 1e-5

CPG = SEQ // CH
NKV = BATCH * KV_HEADS
STEPS = NKV * CPG
KTILES = SEQ // P
UNITS = KTILES * GROUP
MAXU = GROUP * (CH // P) * 2
EARLY = (STEPS - KV_HEADS) * GROUP
Q_STACK = ((0, 3), (0, 2), (0, 1))
K_STACK = ((0, 3), (1, 2), (2, 1))
ROWS = 6 * HD
ROWS_M = ROWS + 2
STORED = 3 * (KT + 1)
LOADED = 16 * (len(Q_STACK) + len(K_STACK))

BEHIND = 2
GANG = 4
CYCLES = 3
FN = CYCLES * NCH
AHEAD = 16
MAXMM = 2 * MAXU
TURN = 2
GLOBAL_AT = NCH - 4
Y_LAG = 5
LAG = 3

TILES = TOKENS // P
TPB = SEQ // P
HPK = P // HD


def hybrid_block(nc, x, wq, bq, wk, bk, wv, bv, wo, bo, lq, lk, lv, lo, g1, g2, ln_w, ln_b,
                 c1, d1, c2, d2, c3, d3, c4, d4, e1, f1, e2, f2, e3, f3, ar,
                 ident_in, cos_in, sin_in, causal_in, head_in, diag_in, sign_in, out):
    with ExitStack() as ctx:
        def sb(name, shape, dt=F32):
            return ctx.enter_context(nc.sbuf_tensor(name, shape, dt))

        def sem(name):
            return ctx.enter_context(nc.semaphore(name))

        q_scr = nc.dram_tensor("q_scr", [STEPS, GROUP, 3, HD, CH], BF16, kind="Internal").ap()
        k_scr = nc.dram_tensor("k_scr", [NKV, 3, HD, SEQ], BF16, kind="Internal").ap()
        o_scr = nc.dram_tensor("o_scr", [STEPS, GROUP, 32, CH], F32, kind="Internal").ap()
        inv_scr = nc.dram_tensor("inv_scr", [STEPS * GROUP, CH], F32, kind="Internal").ap()

        ps = ctx.enter_context(nc.psum_tensor("ps", [P, 8, CH], F32))

        XT = sb("XT", [P, KT, TOKENS])
        YT = sb("YT", [P, KT, TOKENS])
        ident = sb("ident", [P, P])
        ones = sb("ones", [P, P])
        eps = sb("eps", [P, 1])
        pick = sb("pick", [P, GANG, P])

        wq_s = sb("wq_s", [P, KT, DIM])
        wkk_s = sb("wkk_s", [P, KT, 2 * KVD])
        wv_s = sb("wv_s", [P, KT, KVD])
        wo_s = sb("wo_s", [P, KT, DIM])
        bv_s = sb("bv_s", [P, KVD])
        c1_s = sb("c1_s", [P, KT, DIM])
        c2_s = sb("c2_s", [P, KT, P])
        c3_s = sb("c3_s", [P, 64])
        c4_s = sb("c4_s", [64, P])
        e1_s = sb("e1_s", [P, KT, P])
        e2_s = sb("e2_s", [P, 64])
        e3_s = sb("e3_s", [64, P])
        last_c = sb("last_c", [64, 2])
        lqk_s = sb("lqk_s", [P, KT, 2 * DIM])
        lv_s = sb("lv_s", [P, KT, DIM])
        lo_s = sb("lo_s", [P, KT, DIM])
        g1_s = sb("g1_s", [P, KT, HD])
        g2_s = sb("g2_s", [HD, DIM])
        cos_s = sb("cos_s", [P, TPB, HD // 2])
        sin_s = sb("sin_s", [P, TPB, HD // 2])
        causal = sb("causal", [P, P])
        head = sb("head", [P, HPK])
        diag = sb("diag", [P, HEADS, HD])
        bias = sb("bias", [P, 20])
        BQ, BK, BO, D1, D2, D3, D4, F1, F2, F3, AR, LW, LB, SG = 0, 2, 3, 5, 7, 8, 9, 10, 11, 12, 13, 14, 16, 18
        half_b = sb("half_b", [P, 2])
        coup = sb("coup", [P, 4])

        def col(v):
            return v.rearrange("(p a) -> p a", a=1)

        def tiled(w):
            return w.rearrange("(k p) n -> p k n", p=P)

        weights = [
            (wq_s[:], tiled(wq)),
            (wkk_s[:, :, 0:KVD], tiled(wk)), (wkk_s[:, :, KVD:2 * KVD], tiled(wk)), (wv_s[:], tiled(wv)),
            (bias[0:KVD, BK:BK + 1], col(bk)), (bias[KVD:P, BK:BK + 1], col(bk)),
            (bias[:, D2:D2 + 1], col(d2)), (bias[0:64, D3:D3 + 1], col(d3)),
            (bias[:, D4:D4 + 1], col(d4).broadcast_to((P, 1))),
            (bias[:, F1:F1 + 1], col(f1)), (bias[0:64, F2:F2 + 1], col(f2)),
            (bias[:, F3:F3 + 1], col(f3).broadcast_to((P, 1))),
            (bias[:, AR:AR + 1], col(ar).broadcast_to((P, 1))),
            (bias[:, SG:SG + 1], sign_in),
            (bv_s[:], bv.rearrange("(a n) -> a n", a=1).broadcast_to((P, KVD))),
            (wo_s[:], tiled(wo)), (c1_s[:], tiled(c1)), (c2_s[:], tiled(c2)), (c3_s[:], c3),
            (last_c[:, 0:1], c4), (e1_s[:], tiled(e1)), (e2_s[:], e2),
            (last_c[:, 1:2], e3),
            (lqk_s[:, :, 0:DIM], tiled(lq)), (lqk_s[:, :, DIM:2 * DIM], tiled(lk)), (lv_s[:], tiled(lv)),
            (lo_s[:], tiled(lo)), (g1_s[:], tiled(g1)), (g2_s[:], g2),
            (cos_s[:], cos_in.rearrange("(t p) e -> p t e", p=P)),
            (sin_s[:], sin_in.rearrange("(t p) e -> p t e", p=P)),
            (causal[:], causal_in), (head[:], head_in),
            (diag[:], diag_in.rearrange("p (h e) -> p h e", h=HEADS)),
        ]
        for at_, v in ((BQ, bq), (BO, bo), (D1, d1), (LW, ln_w), (LB, ln_b)):
            for kt in range(KT):
                weights.append((bias[:, at_ + kt:at_ + kt + 1], col(v[kt * P:(kt + 1) * P])))

        x_row = sb("x_row", [P, 2, 4, DIM])
        sq = sb("sq", [P, 2, KT, CH])
        std = sb("std", [P, 2, CH])
        rec = sb("rec", [P, 2, CH])
        vals = sb("vals", [P, NKV, KTILES, 32])
        den, den_last = rec[:, 0, :], rec[:, 1, :]
        o_sb = sb("o_sb", [P, 2, CH])
        mx = sb("mx", [P, MAXU])
        mxq = sb("mxq", [P, MAXU // 2])
        negm = sb("negm", [HD, 2, P], BF16)
        gmc = sb("gmc", [P, KT, NCH])
        gm = sb("gm", [P, KT, BATCH])
        gh1 = sb("gh1", [P, BATCH])
        gh2 = sb("gh2", [64, BATCH])
        gth = sb("gth", [P, BATCH])
        cb = sb("cb", [P, BATCH])
        WORK = 13 * 1024
        work = sb("work", [P, WORK])
        at = [0]

        def take(*shape, dt=F32):
            n = int(np.prod(shape))
            words = n if dt == F32 else n // 2
            ap = work[:, at[0]:at[0] + words]
            at[0] += words
            assert at[0] <= WORK, at[0]
            if dt != F32:
                ap = ap.bitcast(dt)
            names = "abcd"[:len(shape)]
            return ap.rearrange(f"p ({' '.join(names)}) -> p {' '.join(names)}", **dict(zip(names, shape)))

        qkf = take(2, 3, CH)
        part = take(2, 3, 3, CH, dt=BF16)
        projections_end = at[0]
        at[0] = 0
        kb, qb = take(2, SEQ, dt=BF16), take(2, GROUP, CH, dt=BF16)
        vst = take(2, KTILES, 32)
        prob = take(8, CH)
        assert at[0] >= projections_end
        ka, qa = take(2, SEQ, dt=BF16), take(2, GROUP, CH, dt=BF16)
        at[0] = WORK - 2 * SEQ
        a_in, a_inv = take(2, KT, CH), take(2, KT, CH)
        at[0] = 0
        h1, h2, h3 = take(2, KT, CH), take(2, CH), take(2, CH)
        th, cs, tw = take(NCH, CH), take(2, CH), take(2, KT, CH)
        at[0] = 0
        y_st8 = take(2, KT, P)
        qk_a, qk_r = take(2, 2 * DIM), take(2, 2 * DIM)
        rt = take(4, 2 * HEADS, HD // 2)
        v_r, gate = take(2, DIM), take(2, DIM)
        k_t, q_t = take(2, KT, P), take(2, KT, P)
        q_x = take(KT, HPK, P)
        e_m = take(HEADS, P)
        s_x = take(HEADS, 32)
        o_t = take(CH)
        o_r, o_n = take(2, DIM), take(2, DIM)
        on_t = take(2, KT, P)
        hg_tile = sb("hg_tile", [HD, 2, P])
        h_g = vals[0:HD].rearrange("p a b c -> p (a b c)")
        at[0] = GANG * KT * CH
        sq_gang = take(GANG, KT, CH)
        stats = sb("stats", [P, 6])
        mv = sb("mv", [P, 2, 2])
        var_e = sb("var_e", [P, 2])
        rstd = sb("rstd", [P, 2])
        mhalf = sb("mhalf", [P, 1])

        names = """id_ld w_ld consts cols c_dve x_tr x_eva x_evd ln_mean ln_cent ln_sq ln_var ln_std ln_rec ln_out g_var g_std g_rec g_bc
            p_mm p_act p_res p_mid p_low p_val v_ones kb_ones a_mm a_max a_fin a_tr
            nm_hi nm_lo m_ld qk_mm exp_ok pv_mm o_ev v_st den_ld den_inv inv_st o_norm o_mm
            o_res f_csum f_sum f_g f_ga f_cb f_h1 f_a1 f_h2 f_a2 f_h3 f_a3 f_z f_th f_cs f_tw f_up f_out
            l_hm l_hg l_ys l_qk l_vg l_silu l_v l_gate l_rt l_rope l_t l_kt l_qt l_qx l_e l_em
            l_o l_s l_sx l_oe l_ot l_r l_bn l_mv l_ve l_rs l_n l_y l_ye l_w l_x
            y_tr y_eva y_evd """.split()
        S = {n: sem(n) for n in names}
        (id_ld, w_ld, consts, cols, c_dve, x_tr, x_eva, x_evd, ln_mean, ln_cent, ln_sq, ln_var, ln_std, ln_rec, ln_out, g_var, g_std, g_rec, g_bc,
         p_mm, p_act, p_res, p_mid, p_low, p_val, v_ones, kb_ones, a_mm, a_max, a_fin, a_tr,
         nm_hi, nm_lo, m_ld, qk_mm, exp_ok, pv_mm, o_ev, v_st, den_ld, den_inv, inv_st, o_norm, o_mm,
         o_res, f_csum, f_sum, f_g, f_ga, f_cb, f_h1, f_a1, f_h2, f_a2, f_h3, f_a3, f_z, f_th, f_cs, f_tw, f_up, f_out,
         l_hm, l_hg, l_ys, l_qk, l_vg, l_silu, l_v, l_gate, l_rt, l_rope, l_t, l_kt, l_qt, l_qx, l_e, l_em,
         l_o, l_s, l_sx, l_oe, l_ot, l_r, l_bn, l_mv, l_ve, l_rs, l_n, l_y, l_ye, l_w, l_x,
         y_tr, y_eva, y_evd, ) = [S[n] for n in names]

        x_ld, p_st, qa_ld, qb_ld, o_st, o_ld, y_st = (
            [sem(f"{n}{p}") for p in range(2)] for n in ("x_ld", "p_st", "qa_ld", "qb_ld", "o_st", "o_ld", "y_st"))

        def ch(c):
            return slice(c * CH, (c + 1) * CH)

        def kv_of(s):
            return s // (CPG * KV_HEADS) * KV_HEADS + s % KV_HEADS

        def is_tile(m):
            return not isinstance(m, int) or 0 <= m < TILES

        def through_tiles(eng, visit):
            for n in range(4):
                visit(n, n % 2, n + 2)
            with eng.Fori(0, (TPB - 6) // 2) as i:
                visit(2 * i + 4, 0, 2 * i + 6)
                visit(2 * i + 5, 1, 2 * i + 7)
            for n in range(TPB - 2, TPB + 2):
                visit(n, n % 2, n + 2 - TPB)
            with eng.Fori(0, (TPB - 4) // 2) as i:
                visit(2 * i + TPB + 2, 0, 2 * i + 4)
                visit(2 * i + TPB + 3, 1, 2 * i + 5)
            for n in range(TILES - 2, TILES + 2):
                visit(n, n % 2, 0)

        def wait(eng, s, value):
            if not isinstance(value, int) or value > 0:
                eng.wait_ge(s, value)

        block = ctx.enter_context(nc.Block())

        @block.sync
        def _(sp):
            xr = x.rearrange("b (c t p) f -> (b c) p t f", t=4, p=P)
            yr = out.rearrange("b (c t p) f -> (b c) p t f", t=4, p=P)
            sp.dma_start(ident[:], ident_in).then_inc(id_ld, 16)
            share = -(-len(weights) // (NCH - 1))
            for c in range(NCH):
                wait(sp, x_tr, c - 1)
                sp.dma_start(x_row[:, c % 2], xr[c]).then_inc(x_ld[c % 2], 16)
                if c >= 1:
                    for dst, src in weights[(c - 1) * share:c * share]:
                        sp.dma_start(dst, src).then_inc(w_ld, 16)

            def load(q_dst, k_dst, p, s, done):
                done = done[p]
                row = 0
                for first, n in Q_STACK:
                    sp.dma_start(q_dst[row:row + n * HD, p],
                                 q_scr[s, :, 0:n].rearrange("j r d n -> (r d) j n")).then_inc(done, 16)
                    row += n * HD
                row = 0
                for first, n in K_STACK:
                    sp.dma_start(k_dst[row:row + n * HD, p],
                                 k_scr[kv_of(s), first:first + 1].broadcast_to((n, HD, SEQ))).then_inc(done, 16)
                    row += n * HD

            for c in range(NCH):
                b, c4 = c // CPG, c % CPG
                for pt, done in ((0, p_act), (1, p_mid), (2, p_low)):
                    sp.wait_ge(done, c + 1)
                    for kt in range(KT):
                        s = c * KV_HEADS + 2 * kt
                        sp.dma_start(q_scr[s:s + 2, :, pt].rearrange("g j d n -> (g j) d n"),
                                     part[:, c % 2, pt, kt, :]).then_inc(p_st[c % 2], 16)
                    sp.dma_start(k_scr[b * KV_HEADS:(b + 1) * KV_HEADS, pt, :, ch(c4)],
                                 part[0:64, c % 2, pt, 2, :]).then_inc(p_st[c % 2], 16)
                if c == CPG - 1:
                    for p in range(2):
                        sp.wait_ge(p_st[p], 16 * STORED * (c + 1) // 2)
                    for s in (0, 1):
                        load(qa, ka, s, s, qa_ld)
            for p in range(2):
                sp.wait_ge(p_st[p], 16 * STORED * NCH // 2)

            def next_maxima(s, p):
                sp.wait_ge(nm_lo, s + 2)
                for r in range(2):
                    sp.dma_start(qb[ROWS + r:ROWS + r + 1, 1 - p].rearrange("p j n -> p (j n)"),
                                 negm[:, r, :]).then_inc(m_ld, 16)

            def leave(s, p, more):
                if more:
                    next_maxima(s, p)
                sp.wait_ge(o_ev, s + 1)
                sp.dma_start(o_scr[s].rearrange("j r n -> (j r) n"), o_sb[:, p, :]).then_inc(o_st[p], 16)

            def refill(s, p):
                load(qb, kb, p, s + 2, qb_ld)

            def refill_max(s, p):
                sp.wait_ge(a_tr, s + 1)
                load(qa, ka, p, s + 2, qa_ld)

            for s in (0, 1):
                load(qb, kb, s, s, qb_ld)
            sp.wait_ge(nm_lo, 1)
            for r in range(2):
                sp.dma_start(qb[ROWS + r:ROWS + r + 1, 0].rearrange("p j n -> p (j n)"), negm[:, r, :]).then_inc(m_ld, 16)
            refill_max(0, 0)
            with sp.Fori(0, STEPS // 2 - 2) as i:
                for p in range(2):
                    leave(2 * i + p, p, True)
                    refill(2 * i + p, p)
                    refill_max(2 * i + p + 1, 1 - p)
            leave(STEPS - 4, 0, True)
            refill(STEPS - 4, 0)
            refill_max(STEPS - 3, 1)
            leave(STEPS - 3, 1, True)
            refill(STEPS - 3, 1)

            den_rows = o_scr[:, :, HD, :].rearrange("s j n -> (s j) n")

            def load_sums(c):
                for kt in range(KT):
                    s = c * KV_HEADS + 2 * kt
                    sp.dma_start(a_in[:, c % 2, kt, :],
                                 o_scr[s:s + 2, :, 0:HD, :].rearrange("g j d n -> (g j) d n")).then_inc(o_ld[c % 2], 16)

            def load_inverses(c):
                for kt in range(KT):
                    r = (c * KV_HEADS + 2 * kt) * GROUP
                    sp.dma_start(a_inv[:, c % 2, kt, :],
                                 inv_scr[r:r + 2 * GROUP, :].rearrange("j (a n) -> j a n", a=1)
                                 .broadcast_to((2 * GROUP, HD, CH))).then_inc(o_ld[c % 2], 16)

            for p in range(2):
                sp.wait_ge(o_st[p], 16 * (STEPS // 2 - 1))
            sp.dma_start(den[0:EARLY], den_rows[0:EARLY]).then_inc(den_ld, 16)
            next_maxima(STEPS - 2, 0)
            for c in (0, 1):
                load_sums(c)
            sp.wait_ge(den_inv, 1)
            sp.dma_start(inv_scr[0:EARLY], den[0:EARLY]).then_inc(inv_st, 16)
            sp.wait_ge(inv_st, 16)
            for c in (0, 1):
                load_inverses(c)
            leave(STEPS - 2, 0, False)
            for c in range(2, NCH - 1):
                sp.wait_ge(o_mm, c - 1)
                load_sums(c)
                load_inverses(c)
            leave(STEPS - 1, 1, False)
            for p in range(2):
                sp.wait_ge(o_st[p], 16 * STEPS // 2)
            sp.dma_start(den_last[0:P - EARLY], den_rows[EARLY:P]).then_inc(den_ld, 16)
            sp.wait_ge(o_mm, NCH - 2)
            load_sums(NCH - 1)
            sp.wait_ge(den_inv, 2)
            sp.dma_start(inv_scr[EARLY:P], den_last[0:P - EARLY]).then_inc(inv_st, 16)
            sp.wait_ge(inv_st, 32)
            load_inverses(NCH - 1)

            for c in range(NCH):
                sp.wait_ge(y_eva, c + 1)
                sp.wait_ge(y_evd, c + 1)
                sp.dma_start(yr[c], x_row[:, c % 2]).then_inc(y_st[c % 2], 16)
            for p in range(2):
                sp.wait_ge(y_st[p], 16 * NCH // 2)

        @block.tensor
        def _(pe):
            mm = pe.matmul

            def mean(k, c):
                wait(pe, ln_cent, k * NCH + c - 1)
                for kt in range(KT):
                    m = mm(ps[:, 5 + c % 2, :], ones[:], XT[:, kt, ch(c)], start=kt == 0, stop=kt == KT - 1)
                m.then_inc(ln_mean, 1)

            def variance(k, v):
                pe.wait_ge(ln_sq, k * NCH + v + 1)
                wait(pe, ln_std, k * NCH + v)
                for kt in range(KT):
                    m = mm(ps[:, 7, :], ones[:], sq[:, v % 2, kt, :], start=kt == 0, stop=kt == KT - 1)
                m.then_inc(ln_var, 1)

            def gang_variance(k, g):
                pe.wait_ge(ln_sq, k * NCH + GANG * (g + 1))
                wait(pe, g_std, 2 * (k - 1) + g)
                for kt in range(KT):
                    for j in range(GANG):
                        m = mm(ps[32 * j:32 * j + 32, 7, :], ones[:, 0:32], sq_gang[:, j, kt, :],
                               start=kt == 0, stop=kt == KT - 1)
                m.then_inc(g_var, 1)

            def spread_root(k, c):
                g, j = c // GANG, c % GANG
                pe.wait_ge(g_rec, 2 * (k - 1) + g + 1)
                if c >= 2:
                    pe.wait_ge(ln_out, k * NCH + c - 1)
                mm(ps[:, 3 + c % 2, :], pick[:, j, :], rec[:, g, :], start=True, stop=True).then_inc(g_bc, 1)

            def layer_norm(k, ready, then=None, early=None):
                def means(*chunks):
                    for c in chunks:
                        if k == 2 and c < NCH + LAG - Y_LAG:
                            continue
                        ready(c)
                        mean(k, c)

                def roots(*chunks):
                    for c in chunks:
                        spread_root(k, c)
                        if then and c >= 2:
                            then(c - 2)
                means(0, 1, 2, 3, 4)
                gang_variance(k, 0)
                means(5, 6, 7)
                roots(0, 1, 2, 3)
                gang_variance(k, 1)
                if early:
                    early()
                roots(4, 5, 6, 7)
                if then:
                    then(6)
                    then(7)

            pe.wait_ge(id_ld, 16)
            for c in range(NCH):
                pe.wait_ge(x_ld[c % 2], 16 * (c // 2 + 1))
                wait(pe, x_eva, c - 1)
                wait(pe, x_evd, c - 1)
                for kt in range(KT):
                    for t in range(4):
                        m = pe.transpose(ps[:, 2 * (c % 2) + kt, t * P:(t + 1) * P],
                                         x_row[:, c % 2, t, kt * P:(kt + 1) * P], ident[:])
                m.then_inc(x_tr, 1)
            pe.wait_ge(consts, 2)

            def project_chunk(c):
                pe.wait_ge(ln_out, c + 1)
                wait(pe, p_act, c)
                wait(pe, p_val, c)
                for n in range(3):
                    for kt in range(KT):
                        w = wq_s[:, kt, n * P:(n + 1) * P] if n < KT else wkk_s[:, kt, :]
                        mm(ps[:, n, :], w, YT[:, kt, ch(c)], start=kt == 0, stop=kt == KT - 1)
                for t in range(4):
                    for kt in range(KT):
                        tok = c * CH + t * P
                        m = mm(ps[:, 3, t * KVD:(t + 1) * KVD], YT[:, kt, tok:tok + P], wv_s[:, kt, :],
                               start=kt == 0, stop=kt == KT - 1)
                m.then_inc(p_mm, 1)

            pe.wait_ge(x_eva, NCH)
            pe.wait_ge(x_evd, NCH)
            pe.wait_ge(w_ld, 16 * len(weights))
            for c in range(NCH + BEHIND):
                if c < NCH:
                    mean(0, c)
                if 1 <= c <= NCH:
                    variance(0, c - 1)
                if c >= BEHIND:
                    project_chunk(c - BEHIND)

            pe.wait_ge(p_act, NCH)
            pe.wait_ge(p_val, NCH)

            def max_mm(i, p, n):
                s, u, half = 2 * i + p, n // 2, n % 2
                j, qt, hk = u // 8, u // 2 % 4, u % 2
                if n == 0:
                    pe.wait_ge(qa_ld[p], LOADED * (i + 1))
                if n == 2:
                    wait(pe, nm_lo, s)
                if half == 0:
                    wait(pe, a_max, MAXU * s + u - 1)
                m = mm(ps[:, 2 * (u % 2) + half, :], qa[0:ROWS, p, j, qt * P:(qt + 1) * P],
                       ka[0:ROWS, p, (2 * hk + half) * CH:(2 * hk + half + 1) * CH], start=True, stop=True)
                if half == 1:
                    m.then_inc(a_mm, 1)

            def max_transpose(s):
                pe.wait_ge(a_fin, s + 1)
                pe.transpose(ps[0:MAXU // 2, 2, 0:P], mxq[:], ident[:]).then_inc(a_tr, 1)

            def out_projection(c):
                if c == 0:
                    pe.wait_ge(nm_lo, STEPS)
                pe.wait_ge(o_norm, c + 1)
                wait(pe, o_res, c - 1)
                for mt in range(KT):
                    for kt in range(KT):
                        m = mm(ps[:, 2 * (c % 2) + mt, :], wo_s[:, kt, mt * P:(mt + 1) * P], a_in[:, c % 2, kt, :],
                               start=kt == 0, stop=kt == KT - 1)
                m.then_inc(o_mm, 1)

            def step(i, p, ahead):
                s = 2 * i + p

                def sums(t):
                    pe.wait_ge(exp_ok, UNITS * s + GROUP * (t + 1))
                    if t == 0:
                        pe.wait_ge(v_st, s + 1)
                        wait(pe, o_ev, s)
                    for j in range(GROUP):
                        m = mm(ps[32 * j:32 * j + 32, 7, :], vst[:, p, t, :], prob[:, (GROUP * t + j) % 8, :],
                               start=t == 0, stop=t == KTILES - 1)
                    m.then_inc(pv_mm, 1)

                def maxima(k):
                    n = k + AHEAD
                    if n < MAXMM and ahead >= 1:
                        max_mm(i + p, 1 - p, n)
                    if n >= MAXMM and ahead >= 2:
                        max_mm(i + 1, p, n - MAXMM)

                pe.wait_ge(qb_ld[p], LOADED * (i + 1))
                pe.wait_ge(m_ld, 32 * (s + 1))
                for t in range(KTILES):
                    for j in range(GROUP):
                        u = GROUP * t + j
                        wait(pe, exp_ok, UNITS * s + u - 2)
                        mm(ps[:, 4 + u % 3, :], kb[0:ROWS_M, p, t * P:(t + 1) * P], qb[0:ROWS_M, p, j, :],
                           start=True, stop=True).then_inc(qk_mm, 1)
                        if u == MAXMM - AHEAD + TURN and ahead >= 1:
                            max_transpose(s + 1)
                        maxima(u)
                        if ahead == 0 and u % 8 == 7 and u // 8 >= 1:
                            out_projection(u // 8 - 1)
                    if t >= 1:
                        sums(t - 1)
                sums(KTILES - 1)

            for n in range(MAXMM):
                max_mm(0, 0, n)
            max_transpose(0)
            for n in range(AHEAD):
                max_mm(0, 1, n)
            pe.wait_ge(kb_ones, 1)
            step(0, 0, 2)
            step(0, 1, 2)
            with pe.Fori(1, STEPS // 2 - 1) as i:
                step(i, 0, 2)
                step(i, 1, 2)
            step(STEPS // 2 - 1, 0, 1)
            step(STEPS // 2 - 1, 1, 0)

            pe.wait_ge(exp_ok, UNITS * STEPS)
            pe.wait_ge(cols, 3)
            pe.wait_ge(o_ev, STEPS)

            def feed_forward(k, ready):
                base = k * FN

                def global_net(layer):
                    if layer == 0:
                        pe.wait_ge(f_sum, k + 1)
                        for kt in range(KT):
                            m = mm(ps[:, 5, 0:BATCH], e1_s[:, kt, :], gm[:, kt, :], start=kt == 0, stop=kt == KT - 1)
                    else:
                        pe.wait_ge(f_ga, 3 * k + layer)
                    if layer == 1:
                        m = mm(ps[0:64, 6, 0:BATCH], e2_s[:], gh1[:], start=True, stop=True)
                    if layer == 2:
                        m = mm(ps[:, 5, 0:BATCH], e3_s[:], gh2[0:64, :], start=True, stop=True)
                    m.then_inc(f_g, 1)

                def layers(n, c, has):
                    if has(0):
                        if has(-NCH):
                            pe.wait_ge(f_up, base + n - NCH + 1)
                        else:
                            pe.wait_ge(ln_out, (2 * k + 1) * NCH + n + 1)
                        if has(-1):
                            pe.wait_ge(f_a1, base + n)
                        for mt in range(KT):
                            for kt in range(KT):
                                m = mm(ps[:, mt, :], c1_s[:, kt, mt * P:(mt + 1) * P], YT[:, kt, ch(c)],
                                       start=kt == 0, stop=kt == KT - 1)
                        m.then_inc(f_h1, 1)
                    if has(-1):
                        pe.wait_ge(f_a1, base + n)
                        if has(-2):
                            pe.wait_ge(f_a2, base + n - 1)
                        for kt in range(KT):
                            m = mm(ps[:, 2, :], c2_s[:, kt, :], h1[:, (c - 1) % 2, kt, :], start=kt == 0, stop=kt == KT - 1)
                        m.then_inc(f_h2, 1)
                    if has(-2):
                        pe.wait_ge(f_a2, base + n - 1)
                        if has(-3):
                            pe.wait_ge(f_a3, base + n - 2)
                        else:
                            pe.wait_ge(ln_out, (2 * k + 2) * NCH)
                        mm(ps[0:64, 3, :], c3_s[:], h2[:, (c - 2) % 2, :], start=True, stop=True).then_inc(f_h3, 1)
                    if has(-3):
                        pe.wait_ge(f_a3, base + n - 2)
                        if has(-4):
                            pe.wait_ge(f_th, base + n - 3)
                        mm(ps[:, 4, :], c4_s[0:64, :], h3[0:64, (c - 3) % 2, :], start=True, stop=True).then_inc(f_z, 1)

                def first(n):
                    layers(n, n, lambda d: n + d >= 0)

                layer_norm(2 * k + 1, ready, early=lambda: first(0))
                for n in range(1, NCH):
                    first(n)
                    if n == GLOBAL_AT:
                        pe.wait_ge(ln_cent, (2 * k + 2) * NCH)
                    if GLOBAL_AT <= n < GLOBAL_AT + 3:
                        global_net(n - GLOBAL_AT)
                with pe.Fori(1, CYCLES - 1) as cy:
                    for c in range(NCH):
                        layers(cy * NCH + c, c, lambda d: True)
                for n in range(FN - NCH, FN + LAG):
                    layers(n, n % NCH, lambda d: n + d < FN)
                    if k == 1 and n >= FN - NCH + Y_LAG:
                        rows_again(n - (FN - NCH + Y_LAG))
                    if k == 0 and n >= FN - NCH + Y_LAG:
                        pe.wait_ge(f_out, n - (FN - NCH + Y_LAG) + 1)
                        mean(2, n - (FN - NCH + Y_LAG))

            def rows_again(c):
                pe.wait_ge(f_out, NCH + c + 1)
                for half in range(2):
                    if half == 0:
                        wait(pe, y_evd, c - 1)
                    else:
                        wait(pe, y_eva, c)
                    for t in (2 * half, 2 * half + 1):
                        for kt in range(KT):
                            tok = c * CH + t * P
                            m = pe.transpose(ps[:, 5 + (2 * c + half) % 3, (t % 2) * DIM + kt * P:(t % 2) * DIM + (kt + 1) * P],
                                             XT[:, kt, tok:tok + P], ident[:])
                    m.then_inc(y_tr, 1)

            def x1_ready(c):
                if c == NCH - 1:
                    out_projection(c)
                pe.wait_ge(o_res, c + 1)
            feed_forward(0, x1_ready)
            pe.wait_ge(f_th, FN)
            pe.wait_ge(f_ga, 3)

            def gate_inner(c):
                pe.wait_ge(ln_out, 2 * NCH + c + 1)
                wait(pe, l_hg, c - 1)
                for kt in range(KT):
                    m = mm(ps[0:HD, c % 2, :], g1_s[:, kt, :], YT[:, kt, ch(c)], start=kt == 0, stop=kt == KT - 1)
                m.then_inc(l_hm, 1)

            layer_norm(2, lambda c: pe.wait_ge(f_out, c + 1), gate_inner)

            pe.wait_ge(ln_cent, 3 * NCH)
            pe.wait_ge(g_std, 4)
            pe.wait_ge(l_hg, NCH)

            def project_qk(n, p):
                pe.wait_ge(l_ys, n + 1)
                wait(pe, l_silu, n)
                for kt in range(KT):
                    m = mm(ps[:, 0, :], y_st8[:, p, kt, :], lqk_s[:, kt, :], start=kt == 0, stop=kt == KT - 1)
                m.then_inc(l_qk, 1)

            def project_vg(n, p):
                wait(pe, l_v, n)
                wait(pe, l_gate, n)
                for kt in range(KT):
                    mm(ps[:, 1, 0:DIM], y_st8[:, p, kt, :], lv_s[:, kt, :], start=kt == 0, stop=kt == KT - 1)
                mm(ps[:, 1, DIM:2 * DIM], hg_tile[:, p, :], g2_s[:], start=True, stop=True).then_inc(l_vg, 1)

            def turn(n, p):
                pe.wait_ge(l_rope, n + 1)
                wait(pe, l_kt, n)
                wait(pe, l_qt, n)
                wait(pe, l_qx, n)
                wait(pe, l_ye, n - 2)
                for i in range(2 * KT):
                    m = pe.transpose(ps[:, 2, i * P:(i + 1) * P], qk_r[:, p, i * P:(i + 1) * P], ident[:])
                m.then_inc(l_t, 1)

            def energy(n, p, quarter):
                kt, half = quarter // 2, quarter % 2
                if quarter == 0:
                    pe.wait_ge(l_kt, n + 1)
                    pe.wait_ge(l_qx, n + 1)
                wait(pe, l_em, 4 * n + quarter - 1)
                mm(ps[:, 3 + half, :], k_t[:, p, kt, :], q_x[:, kt, 4 * half:4 * half + 4, :],
                   start=True, stop=True).then_inc(l_e, 1)

            def attend(n, p, first):
                pe.wait_ge(l_qt, n + 1)
                pe.wait_ge(l_sx, n + 1)
                pe.wait_ge(l_v, n + 1)
                wait(pe, l_oe, n)
                for g in range(4):
                    mm(ps[:, 6, g * P:(g + 1) * P], s_x[:, 4 * g:4 * g + 4, :], q_t[:, p, g // 2, :],
                       start=g == 0, stop=False, skip_group_check=True)
                pe.wait_ge(l_em, 4 * (n + 1))
                for g in range(4):
                    for j in range(4):
                        h = 4 * g + j
                        m = mm(ps[32 * j:32 * j + HD, 6, g * P:(g + 1) * P], v_r[:, p, h * HD:(h + 1) * HD], e_m[:, h, :],
                               start=False, stop=g == 3, skip_group_check=True)
                m.then_inc(l_o, 1)
                for kt in range(KT):
                    m = mm(ps[:, 5, kt * P:(kt + 1) * P], qk_r[:, p, DIM + kt * P:DIM + (kt + 1) * P],
                           v_r[:, p, kt * P:(kt + 1) * P], start=first and kt == 0, stop=kt == KT - 1, skip_group_check=True)
                m.then_inc(l_s, 1)

            def rows(n):
                pe.wait_ge(l_oe, n + 1)
                wait(pe, l_x, n - 1)
                for g in range(4):
                    m = pe.transpose(ps[:, 7, g * P:(g + 1) * P], o_t[:, g * P:(g + 1) * P], ident[:])
                m.then_inc(l_ot, 1)

            def norm_turn(n, p):
                pe.wait_ge(l_n, n + 1)
                turns = min(n + 3, TILES) if isinstance(n, int) else n + 3
                pe.wait_ge(l_kt, turns)
                pe.wait_ge(l_qt, turns)
                pe.wait_ge(l_qx, turns)
                for kt in range(KT):
                    m = pe.transpose(ps[:, 2, kt * P:(kt + 1) * P], o_n[:, p, kt * P:(kt + 1) * P], ident[:])
                m.then_inc(l_y, 1)

            def out_proj(n, p):
                pe.wait_ge(l_ye, n + 1)
                pe.wait_ge(l_r, min(n + 2, TILES) if isinstance(n, int) else n + 2)
                wait(pe, l_x, n)
                for mt in range(KT):
                    for kt in range(KT):
                        m = mm(ps[:, 7, mt * P:(mt + 1) * P], lo_s[:, kt, mt * P:(mt + 1) * P], on_t[:, p, kt, :],
                               start=kt == 0, stop=kt == KT - 1)
                m.then_inc(l_w, 1)

            def pipeline(n, p, place):
                if is_tile(n):
                    energy(n, p, 0)
                    energy(n, p, 1)
                if is_tile(n - 1):
                    rows(n - 1)
                if is_tile(n + 2):
                    project_qk(n + 2, p)
                if is_tile(n):
                    energy(n, p, 2)
                    energy(n, p, 3)
                if is_tile(n + 1):
                    turn(n + 1, 1 - p)
                    project_vg(n + 1, 1 - p)
                if is_tile(n):
                    attend(n, p, isinstance(n, int) and n % TPB == 0)
                if is_tile(n - 2):
                    out_proj(n - 2, p)
                if is_tile(n - 1):
                    norm_turn(n - 1, 1 - p)

            project_qk(0, 0)
            project_qk(1, 1)
            turn(0, 0)
            project_vg(0, 0)
            through_tiles(pe, pipeline)

            pe.wait_ge(l_em, 4 * TILES)
            pe.wait_ge(l_oe, TILES)
            pe.wait_ge(l_x, TILES)
            feed_forward(1, lambda c: pe.wait_ge(l_x, 4 * (c + 1)))

            for c in range(NCH + LAG - Y_LAG, NCH):
                rows_again(c)

        @block.scalar
        def _(act):
            fn = act.activation
            for c in range(NCH):
                act.wait_ge(x_tr, c + 1)
                act.copy(XT[:, 0, ch(c)], ps[:, 2 * (c % 2), :]).then_inc(x_eva, 1)

            def squares(k, c, dst):
                act.wait_ge(ln_cent, k * NCH + c + 1)
                fn(dst, YT[:, :, ch(c)], ACT.Square).then_inc(ln_sq, 1)

            def root(v):
                act.wait_ge(ln_var, v + 1)
                wait(act, ln_rec, v - 1)
                fn(std[:, v % 2, :], ps[:, 7, :], ACT.Sqrt, bias=eps[:]).then_inc(ln_std, 1)

            def layer_norm(k):
                for g in range(NCH // GANG):
                    for j in range(GANG):
                        squares(k, GANG * g + j, sq_gang[:, j])
                    act.wait_ge(g_var, 2 * (k - 1) + g + 1)
                    fn(std[:, g, :], ps[:, 7, :], ACT.Sqrt, bias=eps[:]).then_inc(g_std, 1)

            def high(c):
                p = c % 2
                act.wait_ge(p_mm, c + 1)
                wait(act, p_low, c - 1)
                wait(act, p_st[p], 16 * STORED * (c // 2))
                for n in range(3):
                    b = bias[:, BQ + n:BQ + n + 1]
                    fn(qkf[:, p, n, :], ps[:, n, :], ACT.Identity, bias=b)
                    m = fn(part[:, p, 0, n, :], ps[:, n, :], ACT.Identity, bias=b)
                m.then_inc(p_act, 1)

            def middle(c):
                act.wait_ge(p_res, c + 1)
                act.copy(part[:, c % 2, 1], qkf[:, c % 2]).then_inc(p_mid, 1)

            act.wait_ge(consts, 2)
            act.wait_ge(w_ld, 16 * len(weights))
            for c in range(NCH + BEHIND + 1):
                if c < NCH:
                    wait(act, ln_var, c - 1)
                    squares(0, c, sq[:, c % 2])
                if 1 <= c <= NCH:
                    root(c - 1)
                if BEHIND <= c < NCH + BEHIND:
                    high(c - BEHIND)
                if c >= BEHIND + 1:
                    middle(c - BEHIND - 1)

            def step(i, p):
                s = 2 * i + p
                for t in range(KTILES):
                    for j in range(GROUP):
                        u = GROUP * t + j
                        act.wait_ge(qk_mm, UNITS * s + u + 1)
                        if j == 0:
                            wait(act, pv_mm, KTILES * s + t - 1)
                        fn(prob[:, u % 8, :], ps[:, 4 + u % 3, :], ACT.Exp, scale=HD ** -0.5).then_inc(exp_ok, 1)
                act.wait_ge(pv_mm, KTILES * (s + 1))
                wait(act, o_st[p], 16 * i)
                act.copy(o_sb[:, p, :], ps[:, 7, :]).then_inc(o_ev, 1)

            step(0, 0)
            step(0, 1)
            with act.Fori(1, STEPS // 2) as i:
                step(i, 0)
                step(i, 1)

            layer_norm(1)

            def feed_forward(k):
                base = k * FN

                def global_net(layer):
                    act.wait_ge(f_g, 3 * k + layer + 1)
                    if layer == 0:
                        fn(gh1[:], ps[:, 5, 0:BATCH], ACT.Gelu, bias=bias[:, F1:F1 + 1], scale=1.0 / SEQ).then_inc(f_ga, 1)
                    if layer == 1:
                        fn(gh2[0:64, :], ps[0:64, 6, 0:BATCH], ACT.Gelu, bias=bias[0:64, F2:F2 + 1]).then_inc(f_ga, 1)
                    if layer == 2:
                        fn(gth[:], ps[:, 5, 0:BATCH], ACT.Tanh, bias=half_b[:, 1:2], scale=0.5).then_inc(f_ga, 1)

                def layers(n, c, has):
                    if has(0):
                        act.wait_ge(f_h1, base + n + 1)
                        if has(-2):
                            act.wait_ge(f_h2, base + n - 1)
                        for mt in range(KT):
                            m = fn(h1[:, c % 2, mt, :], ps[:, mt, :], ACT.Gelu, bias=bias[:, D1 + mt:D1 + mt + 1])
                        m.then_inc(f_a1, 1)
                    if has(-1):
                        act.wait_ge(f_h2, base + n)
                        if has(-3):
                            act.wait_ge(f_h3, base + n - 2)
                        fn(h2[:, (c - 1) % 2, :], ps[:, 2, :], ACT.Gelu, bias=bias[:, D2:D2 + 1]).then_inc(f_a2, 1)
                    if has(-2):
                        act.wait_ge(f_h3, base + n - 1)
                        if has(-4):
                            act.wait_ge(f_z, base + n - 3)
                        fn(h3[0:64, (c - 2) % 2, :], ps[0:64, 3, :], ACT.Gelu, bias=bias[0:64, D3:D3 + 1]).then_inc(f_a3, 1)
                    if has(-3):
                        act.wait_ge(f_z, base + n - 2)
                        fn(th[:, (c - 3) % NCH, :], ps[:, 4, :], ACT.Tanh, bias=half_b[:, 0:1], scale=0.5).then_inc(f_th, 1)

                for n in range(NCH):
                    layers(n, n, lambda d: n + d >= 0)
                    if GLOBAL_AT <= n < GLOBAL_AT + 3:
                        global_net(n - GLOBAL_AT)
                with act.Fori(1, CYCLES - 1) as cy:
                    for c in range(NCH):
                        layers(cy * NCH + c, c, lambda d: True)
                for n in range(FN - NCH, FN + LAG):
                    layers(n, n % NCH, lambda d: n + d < FN)
                    if k == 1 and n >= FN - NCH + Y_LAG:
                        out_rows(n - (FN - NCH + Y_LAG))

            def out_rows(c):
                act.wait_ge(y_tr, 2 * c + 1)
                wait(act, y_st[c % 2], 16 * (c // 2))
                act.copy(x_row[:, c % 2, 0:2].rearrange("p a b -> p (a b)"), ps[:, 5 + 2 * c % 3, :]).then_inc(y_eva, 1)

            feed_forward(0)
            act.wait_ge(f_cs, FN)
            layer_norm(2)

            for c in range(NCH):
                act.wait_ge(l_hm, c + 1)
                act.copy(h_g[:, ch(c)], ps[0:HD, c % 2, :]).then_inc(l_hg, 1)

            def queries_keys(n, p):
                act.wait_ge(l_qk, n + 1)
                wait(act, l_rope, n - 1)
                fn(qk_a[:, p, :], ps[:, 0, :], ACT.Silu).then_inc(l_silu, 1)

            def values_gate(n, p):
                act.wait_ge(l_vg, n + 1)
                wait(act, l_s, n - 1)
                fn(v_r[:, p, :], ps[:, 1, 0:DIM], ACT.Copy, scale=0.5).then_inc(l_v, 1)
                wait(act, l_r, n - 1)
                fn(gate[:, p, :], ps[:, 1, DIM:2 * DIM], ACT.Tanh, scale=0.5).then_inc(l_gate, 1)

            def turned(n, p):
                act.wait_ge(l_t, n + 1)
                act.wait_ge(l_qx, n + 1)
                wait(act, l_e, 4 * (n - 1))
                act.copy(k_t[:, p].rearrange("p a b -> p (a b)"), ps[:, 2, KT * P:2 * KT * P]).then_inc(l_kt, 1)
                wait(act, l_o, n - 1)
                act.copy(q_t[:, p].rearrange("p a b -> p (a b)"), ps[:, 2, 0:KT * P]).then_inc(l_qt, 1)

            def affine(n, p):
                act.wait_ge(l_y, n + 1)
                wait(act, l_w, n - 1)
                for kt in range(KT):
                    m = fn(on_t[:, p, kt, :], ps[:, 2, kt * P:(kt + 1) * P], ACT.Identity,
                           bias=bias[:, LB + kt:LB + kt + 1], scale=bias[:, LW + kt:LW + kt + 1])
                m.then_inc(l_ye, 1)

            def pipeline(n, p, place):
                if is_tile(n + 2):
                    queries_keys(n + 2, p)
                if is_tile(n + 1):
                    turned(n + 1, 1 - p)
                    values_gate(n + 1, 1 - p)
                if is_tile(n):
                    act.wait_ge(l_o, n + 1)
                    wait(act, l_ot, n)
                    act.copy(o_t, ps[:, 6, :]).then_inc(l_oe, 1)
                if is_tile(n - 1):
                    affine(n - 1, 1 - p)

            queries_keys(0, 0)
            queries_keys(1, 1)
            turned(0, 0)
            values_gate(0, 0)
            through_tiles(act, pipeline)

            layer_norm(3)
            feed_forward(1)
            for c in range(NCH + LAG - Y_LAG, NCH):
                out_rows(c)

        @block.vector
        def _(dve):
            dve.memset(ones[:], 1.0 / DIM).then_inc(consts, 1)
            dve.memset(eps[:], EPS).then_inc(consts, 1)
            dve.memset(mhalf[:], -0.5).then_inc(consts, 1)
            dve.memset(vals[:, :, :, HD:32], 1.0).then_inc(v_ones, 1)
            for c in range(NCH):
                dve.wait_ge(x_tr, c + 1)
                dve.tensor_copy(XT[:, 1, ch(c)], ps[:, 2 * (c % 2) + 1, :]).then_inc(x_evd, 1)

            def centre(k, c):
                dve.wait_ge(ln_mean, k * NCH + c + 1)
                dve.tensor_tensor(YT[:, :, ch(c)], XT[:, :, ch(c)],
                                  ps[:, 5 + c % 2:6 + c % 2, :].broadcast_to((P, KT, CH)),
                                  ALU.subtract).then_inc(ln_cent, 1)

            def scale(v):
                dve.wait_ge(ln_std, v + 1)
                wait(dve, ln_out, v - 1)
                dve.reciprocal(rec[:, v % 2, :], std[:, v % 2, :]).then_inc(ln_rec, 1)
                dve.wait_ge(ln_sq, v + 1)
                dve.wait_ge(ln_rec, v + 1)
                dve.tensor_tensor(YT[:, :, ch(v)], YT[:, :, ch(v)],
                                  rec[:, v % 2:v % 2 + 1, :].broadcast_to((P, KT, CH)),
                                  ALU.mult).then_inc(ln_out, 1)

            def scale_spread(k, v):
                dve.wait_ge(g_bc, (k - 1) * NCH + v + 1)
                dve.tensor_tensor(YT[:, :, ch(v)], YT[:, :, ch(v)],
                                  ps[:, 3 + v % 2:4 + v % 2, :].broadcast_to((P, KT, CH)),
                                  ALU.mult).then_inc(ln_out, 1)

            def chunk_sum(k, v):
                dve.wait_ge(ln_out, k * NCH + v + 1)
                dve.tensor_reduce(gmc[:, :, v:v + 1], YT[:, :, ch(v)], AX_X, ALU.add).then_inc(f_csum, 1)

            def layer_norm(k, sums, before={}, centred=0):
                def centres(*chunks):
                    for c in chunks:
                        if c in before:
                            before[c]()
                        if c >= centred:
                            centre(k, c)

                def inverses(g):
                    dve.wait_ge(g_std, 2 * (k - 1) + g + 1)
                    dve.reciprocal(rec[:, g, :], std[:, g, :]).then_inc(g_rec, 1)

                def scales(*chunks):
                    for c in chunks:
                        scale_spread(k, c)
                centres(0, 1, 2, 3, 4, 5)
                if not before:
                    inverses(0)
                centres(6, 7)
                if before:
                    inverses(0)
                scales(0, 1, 2, 3)
                if sums:
                    for v in range(2):
                        chunk_sum(k, v)
                inverses(1)
                for c in range(4, NCH):
                    scales(c)
                    if sums:
                        chunk_sum(k, c - 2)
                if sums:
                    chunk_sum(k, NCH - 2)
                    chunk_sum(k, NCH - 1)

            def residue(c):
                p, b = c % 2, c // CPG
                dve.wait_ge(p_mm, c + 1)
                dve.tensor_tensor(vals[:, b * KV_HEADS:(b + 1) * KV_HEADS, 4 * (c % CPG):4 * (c % CPG) + 4, 0:HD]
                                  .rearrange("p g t d -> p t g d"),
                                  ps[:, 3, 0:4 * KVD].rearrange("p (t g d) -> p t g d", t=4, g=KV_HEADS),
                                  bv_s[:].rearrange("p (a g d) -> p a g d", a=1, g=KV_HEADS).broadcast_to((P, 4, KV_HEADS, HD)),
                                  ALU.add).then_inc(p_val, 1)
                dve.wait_ge(p_act, c + 1)
                dve.tensor_tensor(qkf[:, p], qkf[:, p], part[:, p, 0], ALU.subtract).then_inc(p_res, 1)

            def low(c):
                p = c % 2
                dve.wait_ge(p_mid, c + 1)
                dve.tensor_tensor(part[:, p, 2], qkf[:, p], part[:, p, 1], ALU.subtract).then_inc(p_low, 1)

            dve.wait_ge(x_eva, NCH)
            dve.wait_ge(x_evd, NCH)
            dve.wait_ge(v_ones, 1)
            dve.wait_ge(w_ld, 16 * len(weights))
            for c in range(NCH + BEHIND + 1):
                if c < NCH:
                    centre(0, c)
                if 1 <= c <= NCH:
                    scale(c - 1)
                if BEHIND <= c < NCH + BEHIND:
                    residue(c - BEHIND)
                if c >= BEHIND + 1:
                    low(c - BEHIND - 1)

            dve.tensor_copy(c4_s[:], last_c[:, 0:1].broadcast_to((64, P))).then_inc(cols, 1)
            dve.tensor_copy(e3_s[:], last_c[:, 1:2].broadcast_to((64, P))).then_inc(cols, 1)
            dve.tensor_copy(pick[:], ident[:].rearrange("p (j a n) -> p j a n", j=GANG, a=1)[:, :, :, 0]
                            .broadcast_to((P, GANG, P))).then_inc(cols, 1)
            dve.tensor_scalar(half_b[:, 0:1], bias[:, D4:D4 + 1], 0.5, None, ALU.mult)
            dve.tensor_scalar(half_b[:, 1:2], bias[:, F3:F3 + 1], 0.5, None, ALU.mult)
            dve.tensor_tensor(coup[:, 0:1], bias[:, AR:AR + 1], bias[:, SG:SG + 1], ALU.mult).then_inc(c_dve, 1)
            dve.wait_ge(c_dve, 1)
            dve.tensor_scalar(coup[:, 1:2], coup[:, 0:1], 0.3, None, ALU.mult)
            dve.tensor_scalar(coup[:, 2:3], bias[:, SG:SG + 1], 0.1, None, ALU.mult)
            dve.tensor_scalar(coup[:, 3:4], coup[:, 0:1], 0.7, None, ALU.mult).then_inc(c_dve, 1)

            def maxima(s):
                for u in range(MAXU):
                    dve.wait_ge(a_mm, MAXU * s + u + 1)
                    b = 2 * (u % 2)
                    dve.tensor_reduce(mx[:, u:u + 1], ps[:, b:b + 2, :], mybir.AxisListType.XY, ALU.max).then_inc(a_max, 1)
                dve.wait_ge(a_max, MAXU * (s + 1))
                halves = mx[:].rearrange("p (a b) -> p a b", b=2)
                dve.tensor_tensor(mxq[:], halves[:, :, 0], halves[:, :, 1], ALU.max).then_inc(a_fin, 1)
                dve.wait_ge(a_tr, s + 1)
                wait(dve, m_ld, 32 * s)
                turned = ps[0:MAXU // 2, 2, 0:P]
                dve.tensor_scalar(negm[:, 0, :], turned, -1.0, None, ALU.mult).then_inc(nm_hi, 1)
                dve.wait_ge(nm_hi, s + 1)
                dve.scalar_tensor_tensor(out=negm[:, 1, :], in0=turned, scalar=-1.0, in1=negm[:, 0, :],
                                         op0=ALU.mult, op1=ALU.subtract).then_inc(nm_lo, 1)

            maxima(0)
            with dve.Fori(1, STEPS) as s:
                maxima(s)

            dve.wait_ge(den_ld, 16)
            dve.reciprocal(den[0:EARLY], den[0:EARLY]).then_inc(den_inv, 1)

            def normalised(c):
                dve.wait_ge(o_ld[c % 2], 16 * 2 * KT * (c // 2 + 1))
                dve.tensor_tensor(a_in[:, c % 2], a_in[:, c % 2], a_inv[:, c % 2], ALU.mult).then_inc(o_norm, 1)

            def add_attention(c):
                dve.wait_ge(o_mm, c + 1)
                for kt in range(KT):
                    m = dve.scalar_tensor_tensor(out=XT[:, kt, ch(c)], in0=ps[:, 2 * (c % 2) + kt, :],
                                                 scalar=bias[:, BO + kt:BO + kt + 1], in1=XT[:, kt, ch(c)],
                                                 op0=ALU.add, op1=ALU.add)
                m.then_inc(o_res, 1)

            for c in range(NCH - 1):
                normalised(c)
                if c >= 1:
                    add_attention(c - 1)
            add_attention(NCH - 2)
            dve.wait_ge(o_res, NCH - 1)

            def last_inverses():
                dve.wait_ge(den_ld, 32)
                dve.reciprocal(den_last[0:P - EARLY], den_last[0:P - EARLY]).then_inc(den_inv, 1)

            def last_chunk():
                normalised(NCH - 1)
                add_attention(NCH - 1)
                dve.wait_ge(o_res, NCH)
            layer_norm(1, True, {4: last_inverses, NCH - 1: last_chunk})

            def feed_forward(k):
                base = k * FN
                dve.wait_ge(f_csum, (k + 1) * NCH)
                dve.tensor_reduce(gm[:], gmc[:].rearrange("p k (b c) -> p k b c", b=BATCH), AX_X, ALU.add).then_inc(f_sum, 1)
                dve.wait_ge(f_ga, 3 * k + 3)
                dve.tensor_scalar(cb[:], gth[:], coup[:, 3:4], coup[:, 2:3], ALU.mult, ALU.add).then_inc(f_cb, 1)
                dve.wait_ge(f_cb, k + 1)

                def update(n, c):
                    p, b = c % 2, c // CPG
                    dve.wait_ge(f_th, base + n + 1)
                    dve.tensor_scalar(cs[:, p, :], th[:, c, :], coup[:, 1:2], cb[:, b:b + 1], ALU.mult, ALU.add).then_inc(f_cs, 1)
                    dve.wait_ge(f_cs, base + n + 1)
                    dve.tensor_tensor(tw[:, p, 0, :], cs[:, p, :], YT[:, 1, ch(c)], ALU.mult)
                    dve.tensor_tensor(tw[:, p, 1, :], cs[:, p, :], YT[:, 0, ch(c)], ALU.mult).then_inc(f_tw, 1)
                    dve.wait_ge(f_tw, base + n + 1)
                    dve.tensor_tensor(YT[:, 0, ch(c)], YT[:, 0, ch(c)], tw[:, p, 0, :], ALU.add)
                    dve.tensor_tensor(YT[:, 1, ch(c)], YT[:, 1, ch(c)], tw[:, p, 1, :], ALU.subtract).then_inc(f_up, 1)

                with dve.Fori(0, CYCLES - 1) as cy:
                    for c in range(NCH):
                        update(cy * NCH + c, c)
                for c in range(NCH):
                    update(FN - NCH + c, c)
                    dve.wait_ge(f_up, base + FN - NCH + c + 1)
                    dve.tensor_tensor(XT[:, :, ch(c)], XT[:, :, ch(c)], YT[:, :, ch(c)], ALU.add).then_inc(f_out, 1)
                    if k == 1 and c >= 2:
                        out_rows(c - 2)
                    if k == 0 and c >= 2:
                        dve.wait_ge(f_out, c - 1)
                        centre(2, c - 2)

            def out_rows(c):
                dve.wait_ge(y_tr, 2 * c + 2)
                wait(dve, y_st[c % 2], 16 * (c // 2))
                dve.tensor_copy(x_row[:, c % 2, 2:4].rearrange("p a b -> p (a b)"), ps[:, 5 + (2 * c + 1) % 3, :]).then_inc(y_evd, 1)

            feed_forward(0)
            dve.wait_ge(f_out, NCH)
            layer_norm(2, False, centred=NCH - 2)

            def halves(ap):
                v = ap.rearrange("p (h a e) -> p h a e", a=2, e=HD // 2)
                return v[:, :, 0, :], v[:, :, 1, :]

            def rope(n, p, t):
                dve.wait_ge(l_silu, n + 1)
                wait(dve, l_s, n - 1)
                wait(dve, l_t, n - 1)
                wait(dve, l_rope, n)
                a, b = halves(qk_a[:, p, :])
                ra, rb = halves(qk_r[:, p, :])
                co = cos_s[:, bass.ds(t, 1), :].broadcast_to((P, 2 * HEADS, HD // 2))
                si = sin_s[:, bass.ds(t, 1), :].broadcast_to((P, 2 * HEADS, HD // 2))
                for i, (u, v) in enumerate(((a, co), (b, si), (b, co), (a, si))):
                    m = dve.tensor_tensor(rt[:, i], u, v, ALU.mult)
                m.then_inc(l_rt, 1)
                dve.wait_ge(l_rt, n + 1)
                dve.tensor_tensor(ra, rt[:, 0], rt[:, 1], ALU.subtract)
                dve.tensor_tensor(rb, rt[:, 2], rt[:, 3], ALU.add).then_inc(l_rope, 1)

            def spread(n, p):
                dve.wait_ge(l_t, n + 1)
                wait(dve, l_e, 4 * n)
                for kt in range(KT):
                    m = dve.tensor_tensor(q_x[:, kt], ps[:, 2, kt * P:(kt + 1) * P].rearrange("p (a n) -> p a n", a=1)
                                          .broadcast_to((P, HPK, P)),
                                          head[:].rearrange("p (h a) -> p h a", a=1).broadcast_to((P, HPK, P)), ALU.mult)
                m.then_inc(l_qx, 1)

            def mask(n, quarter):
                dve.wait_ge(l_e, 4 * n + quarter + 1)
                if quarter == 0:
                    wait(dve, l_o, n)
                dve.tensor_tensor(e_m[:, 4 * quarter:4 * quarter + 4, :],
                                  ps[:, 3 + quarter % 2, :].rearrange("p (h n) -> p h n", h=4),
                                  causal[:].rearrange("p (a n) -> p a n", a=1).broadcast_to((P, 4, P)),
                                  ALU.mult).then_inc(l_em, 1)

            def state(n, reset):
                dve.wait_ge(l_s, n + 1)
                dve.wait_ge(l_o, n + 1)
                if reset:
                    dve.memset(s_x[:, :, 0:HD], 0.0).then_inc(l_sx, 1)
                else:
                    dve.tensor_tensor(s_x[:, :, 0:HD], ps[:, 5, 0:DIM].rearrange("p (h d) -> p h d", h=HEADS),
                                      diag[:], ALU.mult).then_inc(l_sx, 1)

            def gated(n, p):
                dve.wait_ge(l_gate, n + 1)
                dve.wait_ge(l_ot, n + 1)
                dve.scalar_tensor_tensor(out=o_r[:, p, :].rearrange("p (h d) -> p h d", h=HEADS),
                                         in0=gate[:, p, :].rearrange("p (h d) -> p h d", h=HEADS), scalar=1.0,
                                         in1=ps[:, 7, :].rearrange("p (h r) -> p h r", r=32)[:, :, 0:HD],
                                         op0=ALU.add, op1=ALU.mult).then_inc(l_r, 1)
                dve.wait_ge(l_r, n + 1)
                dve.bn_stats(stats[:], o_r[:, p, :]).then_inc(l_bn, 1)

            def variance(n, p):
                dve.bn_aggr(mv[:, p, :], stats[:]).then_inc(l_mv, 1)
                dve.wait_ge(l_mv, n + 1)
                dve.tensor_scalar(var_e[:, p:p + 1], mv[:, p, 1:2], EPS, None, ALU.add).then_inc(l_ve, 1)

            def normalise(n, p):
                wait(dve, l_y, n - 1)
                dve.wait_ge(l_rs, n + 1)
                dve.tensor_scalar(o_n[:, p, :], o_r[:, p, :], mv[:, p, 0:1], rstd[:, p:p + 1],
                                  ALU.subtract, ALU.mult).then_inc(l_n, 1)

            def residual(n):
                dve.wait_ge(l_w, n + 1)
                dve.tensor_tensor(XT[:, :, bass.ds(n * P, P)], XT[:, :, bass.ds(n * P, P)],
                                  ps[:, 7, 0:DIM].rearrange("p (k n) -> p k n", k=KT), ALU.add).then_inc(l_x, 1)

            def pipeline(n, p, place):
                if is_tile(n):
                    for quarter in range(4):
                        mask(n, quarter)
                if is_tile(n - 1):
                    gated(n - 1, 1 - p)
                    dve.wait_ge(l_bn, n)
                if is_tile(n + 1):
                    spread(n + 1, 1 - p)
                if is_tile(n - 1):
                    variance(n - 1, 1 - p)
                if is_tile(n) and is_tile(n + 1):
                    state(n, isinstance(n, int) and n % TPB == TPB - 1)
                if is_tile(n - 1):
                    normalise(n - 1, 1 - p)
                if is_tile(n - 2):
                    residual(n - 2)
                if is_tile(n + 2):
                    rope(n + 2, p, place)

            rope(0, 0, 0)
            rope(1, 1, 1)
            spread(0, 0)
            dve.memset(s_x, 0.0).then_inc(l_sx, 1)
            through_tiles(dve, pipeline)

            dve.wait_ge(l_x, TILES)
            layer_norm(3, True)
            feed_forward(1)
            out_rows(NCH - 2)
            out_rows(NCH - 1)

        @block.gpsimd
        def _(pool):
            pool.wait_ge(p_val, NCH)
            for p in range(2):
                pool.wait_ge(p_st[p], 16 * STORED * NCH // 2)

            pool.memset(kb[ROWS:ROWS_M], 1.0).then_inc(kb_ones, 1)
            pool.wait_ge(kb_ones, 1)

            def values(s, p):
                wait(pool, pv_mm, KTILES * (s - 1))
                pool.tensor_copy(vst[:, p].rearrange("p t d -> p (t d)"),
                                 vals[:, kv_of(s)].rearrange("p t d -> p (t d)")).then_inc(v_st, 1)

            values(0, 0)
            values(1, 1)
            with pool.Fori(1, STEPS // 2) as i:
                values(2 * i, 0)
                values(2 * i + 1, 1)

            pool.wait_ge(ln_out, 3 * NCH)
            pool.wait_ge(l_hg, NCH)

            def columns(n, p):
                wait(pool, l_vg, n - 1)
                pool.tensor_copy(hg_tile[:, p, :], h_g[:, bass.ds(n * P, P)])
                pool.tensor_copy(y_st8[:, p], YT[:, :, bass.ds(n * P, P)]).then_inc(l_ys, 1)

            def root(n, p):
                pool.wait_ge(l_ve, n + 1)
                wait(pool, l_n, n - 1)
                pool.tensor_tensor(rstd[:, p:p + 1], var_e[:, p:p + 1], mhalf[:], ALU.pow).then_inc(l_rs, 1)

            for n in range(3):
                columns(n, n % 2)
            for n in range(2):
                columns(n + 3, 1 - n % 2)
                root(n, n % 2)
            with pool.Fori(1, TILES // 2 - 2) as i:
                columns(2 * i + 3, 1)
                root(2 * i, 0)
                columns(2 * i + 4, 0)
                root(2 * i + 1, 1)
            for n in range(TILES - 4, TILES):
                if is_tile(n + 3):
                    columns(n + 3, 1 - n % 2)
                root(n, n % 2)


_INS = ['L0_attn_a_x', 'L0_attn_a_Wq', 'L0_attn_a_bq', 'L0_attn_a_Wk', 'L0_attn_a_bk', 'L0_attn_a_Wv',
        'L0_attn_a_bv', 'L0_attn_a_Wo', 'L0_attn_a_bo', 'L0_attn_b_Wq', 'L0_attn_b_Wk', 'L0_attn_b_Wv',
        'L0_attn_b_Wo', 'L0_attn_b_Wg1', 'L0_attn_b_Wg2', 'L0_attn_b_ln_w', 'L0_attn_b_ln_b',
        'L0_ffn_cn_w1', 'L0_ffn_cn_b1', 'L0_ffn_cn_w2', 'L0_ffn_cn_b2', 'L0_ffn_cn_w3', 'L0_ffn_cn_b3',
        'L0_ffn_cn_w4', 'L0_ffn_cn_b4', 'L0_ffn_gc_w1', 'L0_ffn_gc_b1', 'L0_ffn_gc_w2', 'L0_ffn_gc_b2',
        'L0_ffn_gc_w3', 'L0_ffn_gc_b3', 'L0_ffn_adaptive_range']


def shape_constants():
    f = np.float32
    inv_freq = (f(1.0) / f(10000.0) ** (np.arange(0, HD, 2, dtype=f) / f(HD))).astype(f)
    ang = (np.arange(SEQ, dtype=f)[:, None] * inv_freq[None, :]).astype(f)
    feature = np.arange(P)[:, None]
    return {
        "ident": np.eye(P, dtype=f), "cos": np.cos(ang).astype(f), "sin": np.sin(ang).astype(f),
        "causal": np.triu(np.ones((P, P), f)),
        "head": (feature // HD == np.arange(HPK)[None, :]).astype(f),
        "diag": (feature // HD == np.arange(DIM)[None, :] // HD % HPK).astype(f),
        "sign": np.where(feature < 64, 1.0, -1.0).astype(f),
    }


def lay_out(inputs):
    a = {n: np.ascontiguousarray(np.asarray(inputs[n])) for n in _INS}
    w = a["L0_attn_a_Wo"].reshape(GROUP, KV_HEADS, HD, DIM)
    a["L0_attn_a_Wo"] = np.ascontiguousarray(w.transpose(1, 0, 2, 3).reshape(DIM, DIM))
    return a


def kernel(**inputs):
    import numpy as _np
    import concourse.bacc as _bacc
    from concourse import mybir as _mybir
    from concourse.bass_utils import run_bass_kernel_spmd as _run

    nc = _bacc.Bacc("TRN2", target_bir_lowering=False, num_devices=1)
    arrays, args = {}, []
    named = {**lay_out(inputs), **shape_constants()}
    for name, a in named.items():
        arrays[f"in_{name}_dram"] = a
        args.append(nc.dram_tensor(f"in_{name}_dram", a.shape, _mybir.dt.from_np(a.dtype), kind="ExternalInput").ap())
    args.append(nc.dram_tensor("out_0_dram", (BATCH, SEQ, DIM), F32, kind="ExternalOutput").ap())
    hybrid_block(nc, *args)
    r = _run(nc, [arrays], core_ids=[0])
    return r.results[0]["out_0_dram"]
```
